# Optimizing a Trainium2 kernel written in Bass

```python
import numpy as np
import jax
import jax.numpy as jnp

def _softmax(x, axis=-1):
    return jax.nn.softmax(x, axis=axis)

def _gelu(x):
    return jax.nn.gelu(x, approximate=True)

def _silu(x):
    return jax.nn.silu(x)

def _sigmoid(x):
    return jax.nn.sigmoid(x)

def _layernorm(x, axis=-1, eps=1e-05):
    m = jnp.mean(x, axis=axis, keepdims=True)
    v = jnp.var(x, axis=axis, keepdims=True)
    return (x - m) / jnp.sqrt(v + eps)

def _scatter_add(tgt, idx, src, axis=0):
    return tgt.at[idx].add(src)

def _segment_sum(src, seg, n):
    return jax.ops.segment_sum(src, seg, n)
kernel_name = 'mk_gnn_preln_d4_gnn_r32_6f5656'

def setup_inputs(seed: int=0):
    np.random.seed(seed)
    _w = jnp.asarray

    def _rec_inputs():
        import jax
        import jax.numpy as jnp
        _gk = jax.random.key(seed)
        x = -0.000202 + 1 * jax.random.normal(jax.random.fold_in(_gk, 1), (50000, 64), jnp.float32)
        src = jax.random.randint(jax.random.fold_in(_gk, 2), (50000,), 0, 50000, jnp.int32)
        dst = jax.random.randint(jax.random.fold_in(_gk, 3), (50000,), 0, 50000, jnp.int32)
        _o = jnp.argsort(dst, stable=True)
        src = src[_o]
        dst = dst[_o]
        edge_attr_16 = 0.000196303 + 1.00016 * jax.random.normal(jax.random.fold_in(_gk, 12), (50000, 16), jnp.float32)
        edge_weight = jax.random.uniform(jax.random.fold_in(_gk, 14), (50000,), jnp.float32, 0.0, 0.999999)
        edge_weight_n2 = jax.random.uniform(jax.random.fold_in(_gk, 15), (50000,), jnp.float32, 0.0, 0.999999)
        return (x, src, dst, edge_attr_16, edge_weight, edge_weight_n2)
    x, src, dst, edge_attr_16, edge_weight, edge_weight_n2 = _rec_inputs()

    def _L0_gnn_setup():
        import jax, jax.numpy as jnp
        import numpy as np
        NODE_DIM = 64
        EDGE_DIM = 16
        HIDDEN = 64
        N_NODES = 3125
        N_EDGES = 50000

        def _mlp(x, W1, b1, W2, b2):
            h = jax.nn.elu(x @ W1.T + b1)
            return h @ W2.T + b2
        key = jax.random.key(seed)
        ks = jax.random.split(key, 12)
        node_features = jax.random.normal(ks[0], (N_NODES, NODE_DIM), dtype=jnp.float32)
        edge_index = jax.random.randint(ks[1], (2, N_EDGES), 0, N_NODES, dtype=jnp.int64)
        edge_features = jax.random.normal(ks[2], (N_EDGES, EDGE_DIM), dtype=jnp.float32)
        msg_in = 2 * NODE_DIM + EDGE_DIM
        s1 = 1.0 / np.sqrt(msg_in)
        W1m = jax.random.uniform(ks[3], (HIDDEN, msg_in), minval=-s1, maxval=s1, dtype=jnp.float32)
        b1m = jax.random.uniform(ks[4], (HIDDEN,), minval=-s1, maxval=s1, dtype=jnp.float32)
        s2 = 1.0 / np.sqrt(HIDDEN)
        W2m = jax.random.uniform(ks[5], (HIDDEN, HIDDEN), minval=-s2, maxval=s2, dtype=jnp.float32)
        b2m = jax.random.uniform(ks[6], (HIDDEN,), minval=-s2, maxval=s2, dtype=jnp.float32)
        upd_in = NODE_DIM + HIDDEN
        s3 = 1.0 / np.sqrt(upd_in)
        W1u = jax.random.uniform(ks[7], (HIDDEN, upd_in), minval=-s3, maxval=s3, dtype=jnp.float32)
        b1u = jax.random.uniform(ks[8], (HIDDEN,), minval=-s3, maxval=s3, dtype=jnp.float32)
        s4 = 1.0 / np.sqrt(HIDDEN)
        W2u = jax.random.uniform(ks[9], (NODE_DIM, HIDDEN), minval=-s4, maxval=s4, dtype=jnp.float32)
        b2u = jax.random.uniform(ks[10], (NODE_DIM,), minval=-s4, maxval=s4, dtype=jnp.float32)
        return {'node_features': node_features, 'edge_features': edge_features, 'W1m': W1m, 'b1m': b1m, 'W2m': W2m, 'b2m': b2m, 'W1u': W1u, 'b1u': b1u, 'W2u': W2u, 'b2u': b2u, 'edge_index': edge_index}
    _L0_gnn_all = _L0_gnn_setup()
    _L0_gnn_in = {k: v for k, v in _L0_gnn_all.items() if k in ('W1m', 'b1m', 'W2m', 'b2m', 'W1u', 'b1u', 'W2u', 'b2u')}
    del _L0_gnn_all

    def _L1_gnn_setup():
        import jax, jax.numpy as jnp
        import numpy as np
        N_NODES = 3125
        N_EDGES = 50000
        D_IN = 64
        D_HID = 64

        def _graph_conv(x, src, dst, n_nodes, W, b, norm_src, norm_dst):
            h = x * norm_src[:, None]
            msg = jax.ops.segment_sum(h[src], dst, num_segments=n_nodes)
            h = msg * norm_dst[:, None]
            return jax.nn.relu(h @ W + b)
        key = jax.random.key(seed)
        ks = jax.random.split(key, 6)
        node_features = jax.random.normal(ks[0], (N_NODES, D_IN), dtype=jnp.float32)
        edge_src = jax.random.randint(ks[1], (N_EDGES,), 0, N_NODES, dtype=jnp.int32)
        edge_dst = jax.random.randint(ks[2], (N_EDGES,), 0, N_NODES, dtype=jnp.int32)
        W1 = jax.random.normal(ks[3], (D_IN, D_HID), dtype=jnp.float32) / np.sqrt(D_IN)
        b1 = jnp.zeros((D_HID,), dtype=jnp.float32)
        W2 = jax.random.normal(ks[4], (D_HID, D_HID), dtype=jnp.float32) / np.sqrt(D_HID)
        b2 = jnp.zeros((D_HID,), dtype=jnp.float32)
        return {'node_features': node_features, 'edge_src': edge_src, 'edge_dst': edge_dst, 'W1': W1, 'b1': b1, 'W2': W2, 'b2': b2}
    _L1_gnn_all = _L1_gnn_setup()
    _L1_gnn_in = {k: v for k, v in _L1_gnn_all.items() if k in ('W1', 'b1', 'W2', 'b2')}
    del _L1_gnn_all

    def _L2_gnn_setup():
        import jax, jax.numpy as jnp
        import numpy as np
        N = 3125
        E = 50000
        D = 64

        def _graph_conv(x, src, dst, ew, W_rel, b_rel, W_root):
            msg = x[src] * ew[:, None]
            agg = jax.ops.segment_sum(msg, dst, num_segments=x.shape[0])
            return agg @ W_rel.T + b_rel + x @ W_root.T
        key = jax.random.key(seed)
        ks = jax.random.split(key, 10)
        x = jax.random.normal(ks[0], (N, D), dtype=jnp.float32)
        edge_index = jax.random.randint(ks[1], (2, E), 0, N, dtype=jnp.int64)
        edge_weight = jax.random.uniform(ks[2], (E,), dtype=jnp.float32)
        s = 1.0 / np.sqrt(D)
        W_rel1 = jax.random.uniform(ks[3], (D, D), jnp.float32, -s, s)
        b_rel1 = jax.random.uniform(ks[4], (D,), jnp.float32, -s, s)
        W_root1 = jax.random.uniform(ks[5], (D, D), jnp.float32, -s, s)
        W_rel2 = jax.random.uniform(ks[6], (D, D), jnp.float32, -s, s)
        b_rel2 = jax.random.uniform(ks[7], (D,), jnp.float32, -s, s)
        W_root2 = jax.random.uniform(ks[8], (D, D), jnp.float32, -s, s)
        return {'x': x, 'edge_index': edge_index, 'edge_weight': edge_weight, 'W_rel1': W_rel1, 'b_rel1': b_rel1, 'W_root1': W_root1, 'W_rel2': W_rel2, 'b_rel2': b_rel2, 'W_root2': W_root2}
    _L2_gnn_all = _L2_gnn_setup()
    _L2_gnn_in = {k: v for k, v in _L2_gnn_all.items() if k in ('W_rel1', 'b_rel1', 'W_root1', 'W_rel2', 'b_rel2', 'W_root2')}
    del _L2_gnn_all

    def _L3_gnn_setup():
        import jax, jax.numpy as jnp
        import numpy as np
        N, E, D_IN, D_OUT = (2048, 32768, 64, 64)
        EPS = 1e-08
        key = jax.random.key(seed)
        ks = jax.random.split(key, 8)
        h = jax.random.normal(ks[0], (N, D_IN), dtype=jnp.float32)
        edge_index = jax.random.randint(ks[1], (2, E), 0, N, dtype=jnp.int64 if jax.config.jax_enable_x64 else jnp.int32)
        adj_v = jax.random.uniform(ks[2], (E,), dtype=jnp.float32)
        deg_v = jax.random.uniform(ks[3], (E,), dtype=jnp.float32)
        W = jax.random.normal(ks[4], (D_IN, D_OUT), dtype=jnp.float32) / np.sqrt(D_IN)
        b = jax.random.normal(ks[5], (D_OUT,), dtype=jnp.float32) * 0.01
        deg_coeff = jnp.array([0.5, 0.0], dtype=jnp.float32)
        coeff_param = jnp.zeros((3,), dtype=jnp.float32)
        scale_param = 2.0 * jnp.ones((1,), dtype=jnp.float32)
        return {'h': h, 'edge_index': edge_index, 'adj_v': adj_v, 'deg_v': deg_v, 'W': W, 'b': b, 'deg_coeff': deg_coeff, 'coeff_param': coeff_param, 'scale_param': scale_param}
    _L3_gnn_all = _L3_gnn_setup()
    _L3_gnn_in = {k: v for k, v in _L3_gnn_all.items() if k in ('W', 'b', 'deg_coeff', 'coeff_param', 'scale_param')}
    del _L3_gnn_all
    return {'x': x, 'src': src, 'dst': dst, 'edge_attr_16': edge_attr_16, 'edge_weight': edge_weight, 'edge_weight_n2': edge_weight_n2, 'L0_gnn_W1m': _L0_gnn_in['W1m'], 'L0_gnn_b1m': _L0_gnn_in['b1m'], 'L0_gnn_W2m': _L0_gnn_in['W2m'], 'L0_gnn_b2m': _L0_gnn_in['b2m'], 'L0_gnn_W1u': _L0_gnn_in['W1u'], 'L0_gnn_b1u': _L0_gnn_in['b1u'], 'L0_gnn_W2u': _L0_gnn_in['W2u'], 'L0_gnn_b2u': _L0_gnn_in['b2u'], 'L1_gnn_W1': _L1_gnn_in['W1'], 'L1_gnn_b1': _L1_gnn_in['b1'], 'L1_gnn_W2': _L1_gnn_in['W2'], 'L1_gnn_b2': _L1_gnn_in['b2'], 'L2_gnn_W_rel1': _L2_gnn_in['W_rel1'], 'L2_gnn_b_rel1': _L2_gnn_in['b_rel1'], 'L2_gnn_W_root1': _L2_gnn_in['W_root1'], 'L2_gnn_W_rel2': _L2_gnn_in['W_rel2'], 'L2_gnn_b_rel2': _L2_gnn_in['b_rel2'], 'L2_gnn_W_root2': _L2_gnn_in['W_root2'], 'L3_gnn_W': _L3_gnn_in['W'], 'L3_gnn_b': _L3_gnn_in['b'], 'L3_gnn_deg_coeff': _L3_gnn_in['deg_coeff'], 'L3_gnn_coeff_param': _L3_gnn_in['coeff_param'], 'L3_gnn_scale_param': _L3_gnn_in['scale_param']}

def reference(x, src, dst, edge_attr_16, edge_weight, edge_weight_n2, L0_gnn_W1m, L0_gnn_b1m, L0_gnn_W2m, L0_gnn_b2m, L0_gnn_W1u, L0_gnn_b1u, L0_gnn_W2u, L0_gnn_b2u, L1_gnn_W1, L1_gnn_b1, L1_gnn_W2, L1_gnn_b2, L2_gnn_W_rel1, L2_gnn_b_rel1, L2_gnn_W_root1, L2_gnn_W_rel2, L2_gnn_b_rel2, L2_gnn_W_root2, L3_gnn_W, L3_gnn_b, L3_gnn_deg_coeff, L3_gnn_coeff_param, L3_gnn_scale_param):
    import jax
    import jax.numpy as jnp

    def _L0_gnn_ref(node_features, edge_features, W1m, b1m, W2m, b2m, W1u, b1u, W2u, b2u, edge_index):
        import jax, jax.numpy as jnp
        import numpy as np
        NODE_DIM = 64
        EDGE_DIM = 16
        HIDDEN = 64
        N_NODES = 3125
        N_EDGES = 50000

        def _mlp(x, W1, b1, W2, b2):
            h = jax.nn.elu(x @ W1.T + b1)
            return h @ W2.T + b2
        senders = edge_index[0]
        receivers = edge_index[1]
        h_senders = node_features[senders]
        h_receivers = node_features[receivers]
        msg_input = jnp.concatenate([h_senders, h_receivers, edge_features], axis=-1)
        messages = _mlp(msg_input, W1m, b1m, W2m, b2m)
        num_nodes = node_features.shape[0]
        aggregated = jax.ops.segment_sum(messages, receivers, num_segments=num_nodes)
        update_input = jnp.concatenate([node_features, aggregated], axis=-1)
        return _mlp(update_input, W1u, b1u, W2u, b2u)

    def _L1_gnn_ref(node_features, edge_src, edge_dst, W1, b1, W2, b2):
        import jax, jax.numpy as jnp
        import numpy as np
        N_NODES = 3125
        N_EDGES = 50000
        D_IN = 64
        D_HID = 64

        def _graph_conv(x, src, dst, n_nodes, W, b, norm_src, norm_dst):
            h = x * norm_src[:, None]
            msg = jax.ops.segment_sum(h[src], dst, num_segments=n_nodes)
            h = msg * norm_dst[:, None]
            return jax.nn.relu(h @ W + b)
        n_nodes = node_features.shape[0]
        ones = jnp.ones(edge_src.shape[0], dtype=node_features.dtype)
        deg_out = jax.ops.segment_sum(ones, edge_src, num_segments=n_nodes)
        deg_in = jax.ops.segment_sum(ones, edge_dst, num_segments=n_nodes)
        norm_src = jax.lax.rsqrt(jnp.clip(deg_out, 1.0))
        norm_dst = jax.lax.rsqrt(jnp.clip(deg_in, 1.0))
        h = _graph_conv(node_features, edge_src, edge_dst, n_nodes, W1, b1, norm_src, norm_dst)
        h = _graph_conv(h, edge_src, edge_dst, n_nodes, W2, b2, norm_src, norm_dst)
        return h

    def _L2_gnn_ref(x, edge_index, edge_weight, W_rel1, b_rel1, W_root1, W_rel2, b_rel2, W_root2):
        import jax, jax.numpy as jnp
        import numpy as np
        N = 3125
        E = 50000
        D = 64

        def _graph_conv(x, src, dst, ew, W_rel, b_rel, W_root):
            msg = x[src] * ew[:, None]
            agg = jax.ops.segment_sum(msg, dst, num_segments=x.shape[0])
            return agg @ W_rel.T + b_rel + x @ W_root.T
        src, dst = (edge_index[0], edge_index[1])
        h = _graph_conv(x, src, dst, edge_weight, W_rel1, b_rel1, W_root1)
        h = jax.nn.relu(h)
        h = _graph_conv(h, src, dst, edge_weight, W_rel2, b_rel2, W_root2)
        return h

    def _L3_gnn_ref(h, edge_index, adj_v, deg_v, W, b, deg_coeff, coeff_param, scale_param):
        import jax, jax.numpy as jnp
        import numpy as np
        N, E, D_IN, D_OUT = (2048, 32768, 64, 64)
        EPS = 1e-08
        n_nodes = h.shape[0]
        Wh = h @ W + b
        row, col = (edge_index[0], edge_index[1])
        sc = jax.nn.softplus(deg_coeff[0] * deg_v + deg_coeff[1])
        Wr = Wh[row]
        Wc = Wh[col]
        dot = jnp.sum(Wr * Wc, axis=-1)
        nr = jnp.sqrt(jnp.sum(Wr * Wr, axis=-1))
        nc = jnp.sqrt(jnp.sum(Wc * Wc, axis=-1))
        sim = dot / jnp.maximum(nr * nc, EPS)
        sim_pos = jax.nn.relu(sim)
        sim_neg = -jax.nn.relu(-sim)
        no_diag = (row != col).astype(Wh.dtype)
        base = adj_v * sc * no_diag
        prop_pos = jax.ops.segment_sum((base * sim_pos)[:, None] * Wc, row, num_segments=n_nodes)
        prop_neg = jax.ops.segment_sum((base * sim_neg)[:, None] * Wc, row, num_segments=n_nodes)
        coeff = jax.nn.softmax(coeff_param)
        scale = jax.nn.softplus(scale_param)
        return scale * (coeff[0] * prop_pos + coeff[1] * prop_neg + coeff[2] * Wh)
    edge_index = jnp.stack([src, dst])
    h = jnp.maximum(_layernorm(x, axis=-1), 0.0)
    x = x + _L0_gnn_ref(h, edge_attr_16, L0_gnn_W1m, L0_gnn_b1m, L0_gnn_W2m, L0_gnn_b2m, L0_gnn_W1u, L0_gnn_b1u, L0_gnn_W2u, L0_gnn_b2u, edge_index)
    h = jnp.maximum(_layernorm(x, axis=-1), 0.0)
    x = x + _L1_gnn_ref(h, src, dst, L1_gnn_W1, L1_gnn_b1, L1_gnn_W2, L1_gnn_b2)
    h = jnp.maximum(_layernorm(x, axis=-1), 0.0)
    x = x + _L2_gnn_ref(h, edge_index, edge_weight, L2_gnn_W_rel1, L2_gnn_b_rel1, L2_gnn_W_root1, L2_gnn_W_rel2, L2_gnn_b_rel2, L2_gnn_W_root2)
    h = jnp.maximum(_layernorm(x, axis=-1), 0.0)
    x = x + _L3_gnn_ref(h, edge_index, edge_weight, edge_weight_n2, L3_gnn_W, L3_gnn_b, L3_gnn_deg_coeff, L3_gnn_coeff_param, L3_gnn_scale_param)
    return x

_drawn_inputs = setup_inputs


def setup_inputs(seed=0):
    import zlib

    import numpy as np

    out = dict(_drawn_inputs(seed))
    spreads = {'L1_gnn_b1': (0.0, 0.1), 'L1_gnn_b2': (0.0, 0.1), 'L3_gnn_coeff_param': (0.0, 0.1)}
    factors = {'edge_attr_16': 2.8,
     'edge_weight_n2': 6.047,
     'L0_gnn_b1m': 6.557,
     'L3_gnn_b': 7.501,
     'L3_gnn_deg_coeff': 3.766}
    for name, (base, spread) in spreads.items():
        noise = np.random.default_rng([zlib.crc32(name.encode()), seed]).standard_normal(out[name].shape)
        drawn = base * np.exp(spread * noise) if base else spread * noise
        out[name] = jnp.asarray(drawn.astype(out[name].dtype))
    for name, factor in factors.items():
        out[name] = (out[name] * factor).astype(out[name].dtype)
    return out
```

```python
from contextlib import ExitStack

import concourse.bass as bass
from concourse import mybir
from concourse.alu_op_type import AluOpType as ALU

F32 = mybir.dt.float32
I32 = mybir.dt.int32
BF16 = mybir.dt.bfloat16
ACT = mybir.ActivationFunctionType
AX_X = mybir.AxisListType.X

P = 128
D = 64
FE = 16
T = 8
N = 50000
EDGES = 50000
ET = -(-EDGES // P)
LAST = EDGES - (ET - 1) * P
BLOCKS = -(-ET // T)
PAIRS_E = (BLOCKS - 1) // 2
TAIL = ET - (BLOCKS - 1) * T
GROUPS = 50
NT = GROUPS * T
NP = NT * P
NODE_TILES = -(-N // P)
FULL_GROUPS = N // (P * T)
PAIRS_N = GROUPS // 2
AW = D + 1
WINDOW = 3
TABLES = 4
CREDIT = 2
EPS = 1e-5
SIM_EPS = 1e-8


N_LOADS = 16 + 4 + T + 2 + 8 + 3
E5_STEPS = 15 + T


def gathered(i):
    return 16 * T * i


def scatters(j):
    return sum(1 for t in range((BLOCKS - 1) * T + TAIL) if t % T % TABLES == j)


def done(c, k):
    return c.sem, c.base + k + 1 + CREDIT


def reuse(c, k):
    return c.sem, c.base + k - 1 + CREDIT


def landed(c, i):
    return c.sem, c.base + 16 * (i + 2)


def landed_before(c, i):
    return c.sem, c.base + 16 * (i + 1)


def program(nc, a, out):
    with ExitStack() as ctx:
        def sb(name, shape, dt=F32):
            return ctx.enter_context(nc.sbuf_tensor(name, shape, dt))

        ring_sems, dma_rings = [], []

        def sem(name):
            return ctx.enter_context(nc.semaphore(name))

        def ring(name):
            s = sem(name)
            ring_sems.append(s)
            return s

        def dma_ring(name, n=2):
            s = [sem(f"{name}{u}") for u in range(n)]
            dma_rings.extend(s)
            return s

        def dram(name, rows=NP, width=D):
            return nc.dram_tensor(name, (rows, width), F32).ap()

        tab_a, tab_b, tab_q = dram("tab_a"), dram("tab_b"), dram("tab_q")
        tab_x1, tab_x2 = dram("tab_x1"), dram("tab_x2")
        tab_g1, tab_g2, tab_h2, tab_h3 = dram("tab_g1"), dram("tab_g2"), dram("tab_h2"), dram("tab_h3")
        tab_wh = dram("tab_wh", NP, AW)
        acc = [dram(f"acc{j}", NP + P) for j in range(TABLES)]

        def group(table, g, n=1):
            w = table.shape[1]
            return table[0:NP, :].rearrange("(g p j) d -> g p (j d)", p=P, j=T)[g]

        agg = sb("agg", [P, NT, AW])
        zeros = sb("zeros", [P, T * D // 2])
        zeros_b = sb("zeros_b", [P, NODE_TILES], BF16)
        ident = sb("ident", [P, P])
        ones = sb("ones", [P, P])
        iota_node = sb("iota_node", [P, WINDOW * P])
        iota_tile = sb("iota_tile", [P, NODE_TILES])
        tile_base = sb("tile_base", [P, NT])
        below = sb("below", [P, P])
        lane_dump = sb("lane_dump", [P, 1])
        minus_one = sb("minus_one", [P, 1])
        power = sb("power", [P, 1])
        half = sb("half", [P, 1])
        block_mask = sb("block_mask", [P, T])
        src_f = sb("src_f", [P, 4, P])
        dst_f = sb("dst_f", [P, 4, P])
        rel = sb("rel", [P, 4, P])
        src_row = sb("src_row", [P, 4 * P], I32)
        dst_row = sb("dst_row", [P, 4 * P], I32)
        ew = sb("ew", [P, 4 * P])
        base = sb("base", [P, 4 * P])
        first_i = sb("first_i", [P, 4], I32)
        last_i = sb("last_i", [P, 4], I32)
        span_f = sb("span_f", [P, 4, 2])
        first_row = sb("first_row", [1, 4 * P], I32)
        xhi_row = sb("xhi_row", [1, 4 * P], I32)
        beyond_i = sb("beyond_i", [1, 4 * P // T], I32)
        deg_out = sb("deg_out", [P, NT])
        deg_in = sb("deg_in", [P, NT])
        norm_in = sb("norm_in", [P, NT])
        norm_out = sb("norm_out", [P, NT])
        w1e_nat = sb("w1e_nat", [D, T, FE])
        w2m_nat = sb("w2m_nat", [D, AW])
        wt = sb("wt", [P, 7, D])
        w_upd_agg = sb("w_upd_agg", [AW, D])
        w_pair = sb("w_pair", [P, 7, 2 * D])
        w1e_t = sb("w1e_t", [P, D])
        w1e_diag = sb("w1e_diag", [P, T, D])
        bias = sb("bias", [1, 8, D])
        par = sb("par", [P, 8])
        par_w = sb("par_w", [P, 16])
        buf = [sb(f"buf{j}", [P, 2, T * D]) for j in range(8)]
        wide = sb("wide", [P, 2, T * P])
        wide_t = sb("wide_t", [P, 2, T * P])
        rows_u = sb("rows_u", [P, 2, T, AW])
        rows_v = sb("rows_v", [P, 2, T, AW])
        hot = sb("hot", [P, 2, WINDOW * P])
        hot_x = sb("hot_x", [P, P])
        hot_lo = sb("hot_lo", [P, 2, P], BF16)
        hot_hi = sb("hot_hi", [P, 2, NODE_TILES], BF16)
        idx_s = sb("idx_s", [P, 2, T], I32)
        idx_d = sb("idx_d", [P, 2, T], I32)
        idx_o = sb("idx_o", [P, 2, T], I32)
        edge_io = rows_v[:, :, :, :].rearrange("p u t d -> p u (t d)")
        edge_in, edge_t = edge_io[:, :, 0:T * FE], edge_io[:, :, T * FE:T * FE + P]
        small = sb("small", [P, 2, 12, T])
        four = lambda x: x.rearrange("p (b q) -> p b q", b=4)
        stage_i = [four(buf[2 + j // 2][:, j % 2, :].bitcast(I32)) for j in range(3)]
        stage_f = four(buf[3][:, 1, :])
        first_f, last_f = buf[7][:, 0, :], buf[7][:, 1, :]
        beyond_f = buf[6][0:1, 0, :]
        nat = buf[1][0:D, :, :].rearrange("p u (w k) -> p (u w) k", k=2 * D)
        src_lo, src_hi = wide[:, 0, 0:4 * P], wide[:, 1, 0:4 * P]
        same = hot
        junk = hot_x
        ps = [ctx.enter_context(nc.psum_tensor(f"ps{j}", [P, 512], F32)) for j in range(8)]

        WA, WB, WQ, WU2, WC1, WC2, WUM = range(7)
        PA, PB, PQ, PU2, PG1, PG2, PL3 = range(7)
        B1M, B1U, B2U, BG1, BG2, BR1, BR2, BL3 = range(8)

        s_in = sem("s_in")
        s_stage_clear = sem("s_stage_clear")
        s_idx_in = sem("s_idx_in")
        s_const = sem("s_const")
        s_pool_self = sem("s_pool_self")
        s_credit = sem("s_credit")
        s_agg0 = sem("s_agg0")
        s_pe_setup = sem("s_pe_setup")
        s_dve = sem("s_dve")
        s_act_setup = sem("s_act_setup")
        s_setup_done = sem("s_setup_done")
        s_pool_hold = sem("s_pool_hold")
        s_slow_built = sem("s_slow_built")
        s_slow_mul = sem("s_slow_mul")
        s_slow_added = sem("s_slow_added")
        s_degrees = sem("s_degrees")
        s_norms = sem("s_norms")
        s_acc_zero = sem("s_acc_zero")
        s_out = sem("s_out")
        s_rest = sem("s_rest")
        s_src_staged, s_dst_staged, s_spans = sem("s_src_staged"), sem("s_dst_staged"), sem("s_spans")
        s_exp_args, s_wt = sem("s_exp_args"), sem("s_wt")
        s_slow_self = sem("s_slow_self")
        s_z_self, s_elu_self, s_elu1_self, s_sq_self = (sem(f"s_{n}_self") for n in ("z", "elu", "elu1", "sq"))
        s_e5 = [sem(f"s_e5_self{u}") for u in range(2)]
        s_total_self = [sem(f"s_total_self{u}") for u in range(2)]
        ln_self = [[sem(f"s_ln{j}_self{u}") for u in range(2)] for j in range(4)]

        class Count:
            def __init__(self, sem_, base):
                self.sem, self.base = sem_, base

        totals = {}

        def counted(name, n, per=1):
            if name not in totals:
                totals[name] = [sem(name), 0]
                if "_got" not in name or name[:3] in ("edg", "row"):
                    (ring_sems if per == 1 else dma_rings).append(totals[name][0])
            c = Count(totals[name][0], totals[name][1])
            totals[name][1] += n * per
            return c

        def edge_stage(per_block, per_tile, dmas, **more):
            names = {n: counted(f"{n}_done", BLOCKS) for n in per_block.split()}
            names.update({n: counted(f"{n}_done", ET) for n in per_tile.split()})
            for n in dmas.split():
                one = n in ("edge_got", "row_got")
                names[n] = [counted(f"{n}{u}", (PAIRS_E + 1 - u) if one else
                                    PAIRS_E * T + (TAIL if u == 0 else 0), 16) for u in range(2)]
            return {**names, **more}

        def node_stage(steps, loads=0, stores=1, groups=GROUPS):
            names = {n: counted(f"{n}_done", groups) for n in steps.split()}
            names["load"] = [[counted(f"load{j}_{u}", PAIRS_N, 16) for u in range(2)] for j in range(loads)]
            names["store"] = [[counted(f"store{j}_{u}", PAIRS_N, 16) for u in range(2)] for j in range(stores)]
            return names

        LN = "s mean xc sq v r h "
        E, NS = [None] * 6, [None] * 7
        NS[0] = node_stage(LN + "ht htc mm o", 1, 3)
        E[0] = edge_stage("idx edge_t edge_c z_mm z act msg consumed", "hot seg added hist_hot hist",
                          "src_got dst_got edge_got", sums_done=sem("sums_done"))
        NS[1] = node_stage(LN + "ag at atc zmm z act e et etc xmm x zero", 2, 2)
        E[1] = edge_stage("idx consumed", "hot seg added", "src_got")
        NS[2] = node_stage("sc st stc mm o zero", 0, 1)
        E[2] = edge_stage("idx consumed", "hot seg added", "src_got")
        NS[3] = node_stage(LN + "sc st stc mm x zero", 1, 2)
        E[3] = edge_stage("idx consumed", "hot seg added", "src_got")
        NS[4] = node_stage("cat ct ctc mm o zero", 1, 1)
        E[4] = edge_stage("idx consumed", "hot seg added", "src_got")
        NS[5] = node_stage(LN + "cat ct ctc mm x ht htc wmm wh nrm nrm2 t0", 2, 2)
        E[5] = edge_stage("idx contrib dedup rows_used sum oidx", "same same_used", "src_got dst_got row_got",
                          table=[sem(f"scattered{j}") for j in range(TABLES)])
        NS[6] = node_stage("sum", 1, 1, FULL_GROUPS + 1)

        def slot(b, u, width=D):
            return b[:, u, 0:T * width].rearrange("p (t d) -> p t d", d=width)

        def over_features(v):
            return v.unsqueeze(2).to_broadcast([P, v.shape[1], D])

        def cols(x, b, n):
            return x[:, bass.ds(b * T, n)]

        def beyond(eng, b, step, n):
            some = eng.value_load(beyond_i[0:1, bass.ds(b, 1)], min_val=0, max_val=1)
            with eng.If(some > 0):
                for t in range(n):
                    k = b * T + t
                    lo = eng.value_load(first_row[0:1, bass.ds(k, 1)], min_val=0, max_val=NODE_TILES) + WINDOW
                    hi = eng.value_load(xhi_row[0:1, bass.ds(k, 1)], min_val=1, max_val=NODE_TILES + WINDOW + 1)
                    with eng.Fori(lo, hi) as tile:
                        step(t)(tile)

        block = ctx.enter_context(nc.Block())

        @block.sync
        def _(sp):
            sp.wait_ge(s_stage_clear, 7)
            n_load = n_rest = 0
            for j, v in enumerate((a["src"], a["dst"], a["dst"])):
                sp.dma_start(stage_i[j][:, 0:3, :],
                             v[0:3 * P * P].rearrange("(b t p) -> t b p", t=P, p=P)).then_inc(s_idx_in, 16)
                sp.dma_start(stage_i[j][0:ET - 1 - 3 * P, 3, :],
                             v[3 * P * P:(ET - 1) * P].rearrange("(t p) -> t p", p=P)).then_inc(s_idx_in, 16)
                sp.dma_start(stage_i[j][ET - 1 - 3 * P:ET - 3 * P, 3, 0:LAST],
                             v[(ET - 1) * P:EDGES].rearrange("(t p) -> t p", t=1)).then_inc(s_idx_in, 16)
            for j, v in enumerate((a["edge_weight"], a["edge_weight_n2"])):
                w = wide[:, j, 0:4 * P].rearrange("p (b q) -> p b q", b=4)
                sp.dma_start(w[:, 0:3, :],
                             v[0:3 * P * P].rearrange("(b t p) -> t b p", t=P, p=P)).then_inc(s_idx_in, 16)
                sp.dma_start(w[0:ET - 1 - 3 * P, 3, :],
                             v[3 * P * P:(ET - 1) * P].rearrange("(t p) -> t p", p=P)).then_inc(s_idx_in, 16)
                sp.dma_start(w[ET - 1 - 3 * P:ET - 3 * P, 3, 0:LAST],
                             v[(ET - 1) * P:EDGES].rearrange("(t p) -> t p", t=1)).then_inc(s_idx_in, 16)

            def load(dst, src):
                nonlocal n_load
                sp.dma_start(dst, src).then_inc(s_in, 16)
                n_load += 1

            w1m, w1u = a["L0_gnn_W1m"], a["L0_gnn_W1u"]
            for h in range(2):
                load(nat[:, WA, h * D:(h + 1) * D], w1m[:, 0:D])
                load(nat[:, WB, h * D:(h + 1) * D], w1m[:, D:2 * D])
                load(nat[:, WQ, h * D:(h + 1) * D], w1u[:, 0:D])
                load(nat[:, WU2, h * D:(h + 1) * D], a["L0_gnn_W2u"])
                load(nat[:, WUM, h * D:(h + 1) * D], w1u[:, D:2 * D])
                load(w_pair[h * D:(h + 1) * D, PG1, h * D:(h + 1) * D], a["L1_gnn_W1"])
                load(w_pair[h * D:(h + 1) * D, PG2, h * D:(h + 1) * D], a["L1_gnn_W2"])
                load(w_pair[h * D:(h + 1) * D, PL3, h * D:(h + 1) * D], a["L3_gnn_W"])
            load(nat[:, WC1, 0:D], a["L2_gnn_W_rel1"])
            load(nat[:, WC1, D:2 * D], a["L2_gnn_W_root1"])
            load(nat[:, WC2, 0:D], a["L2_gnn_W_rel2"])
            load(nat[:, WC2, D:2 * D], a["L2_gnn_W_root2"])
            for t in range(T):
                load(w1e_nat[:, t, :], w1m[:, 2 * D:2 * D + FE])
            load(w2m_nat[:, 0:D], a["L0_gnn_W2m"])
            load(w2m_nat[:, D:D + 1], a["L0_gnn_b2m"].rearrange("(p o) -> p o", o=1))
            for j, n in enumerate(("L0_gnn_b1m", "L0_gnn_b1u", "L0_gnn_b2u", "L1_gnn_b1", "L1_gnn_b2",
                                   "L2_gnn_b_rel1", "L2_gnn_b_rel2", "L3_gnn_b")):
                load(bias[0:1, j, :], a[n].rearrange("(o d) -> o d", o=1))
            for c0, n, w in ((0, "L3_gnn_deg_coeff", 2), (2, "L3_gnn_coeff_param", 3), (5, "L3_gnn_scale_param", 1)):
                load(par[:, c0:c0 + w], a[n].rearrange("(o d) -> o d", o=1).to_broadcast([P, w]))
            assert n_load == N_LOADS

            def stream(st, loads, stores, pairs=PAIRS_N):
                with sp.Fori(0, pairs) as i:
                    for u in range(2):
                        g = i * 2 + u
                        for j, (dst, table, readers) in enumerate(loads):
                            for r in readers:
                                sp.wait_ge(*reuse(r, g))
                            sp.dma_start(dst(u), group(table, g)).then_inc(st["load"][j][u].sem, 16)
                    for j, (srcb, table, w) in enumerate(stores):
                        for u in range(2):
                            g = i * 2 + u
                            sp.wait_ge(*done(w, g))
                            sp.dma_start(group(table, g), srcb(u)).then_inc(st["store"][j][u].sem, 16)

            sp.wait_ge(s_credit, 1)
            sp.wait_ge(s_const, 1)
            st = NS[0]
            x_in = a["x"]

            def stores0(g, u):
                for j, (b, table) in enumerate(((5, tab_a), (6, tab_b), (7, tab_q))):
                    if j == 0:
                        sp.wait_ge(*done(st["o"], g))
                    sp.dma_start(group(table, g), buf[b][:, u, :]).then_inc(st["store"][j][u].sem, 16)

            with sp.Fori(0, FULL_GROUPS // 2) as i:
                for u in range(2):
                    g = i * 2 + u
                    sp.wait_ge(*reuse(st["xc"], g))
                    sp.dma_start(slot(buf[0], u), x_in[bass.ds(g * (P * T), P * T), :]
                                 .rearrange("(t p) d -> p t d", p=P)).then_inc(st["load"][0][u].sem, 16)
                for u in range(2):
                    stores0(i * 2 + u, u)
            g = FULL_GROUPS
            whole = (N - g * P * T) // P
            rest = N - g * P * T - whole * P
            r0 = g * P * T
            sp.wait_ge(*reuse(st["xc"], g))
            sp.dma_start(slot(buf[0], 0)[0:rest, whole, :], x_in[r0 + whole * P:N, :]).then_inc(s_rest, 16)
            n_rest += 1
            sp.wait_ge(s_rest, 16 * n_rest)
            sp.dma_start(slot(buf[0], 0)[:, 0:whole, :], x_in[r0:r0 + whole * P, :]
                         .rearrange("(t p) d -> p t d", p=P)).then_inc(st["load"][0][0].sem, 16)
            sp.wait_ge(*reuse(st["xc"], g + 1))
            sp.sem_inc(st["load"][0][1].sem, 16)
            for u in range(2):
                stores0(g + u, u)

            e = E[0]
            with sp.Fori(0, PAIRS_E) as i:
                for u in range(2):
                    b = i * 2 + u
                    sp.wait_ge(*reuse(e["edge_t"], b))
                    sp.dma_start(edge_in[:, u, :].rearrange("p (t f) -> p t f", f=FE),
                                 a["edge_attr_16"][bass.ds(b * (P * T), P * T), :]
                                 .rearrange("(t p) f -> p t f", p=P)).then_inc(e["edge_got"][u].sem, 16)
            b = BLOCKS - 1
            r0 = b * P * T
            sp.wait_ge(*reuse(e["edge_t"], b))
            sp.dma_start(edge_in[0:LAST, 0, (TAIL - 1) * FE:TAIL * FE],
                         a["edge_attr_16"][EDGES - LAST:EDGES, :]).then_inc(s_rest, 16)
            n_rest += 1
            sp.wait_ge(s_rest, 16 * n_rest)
            sp.dma_start(edge_in[:, 0, 0:(TAIL - 1) * FE].rearrange("p (t f) -> p t f", f=FE),
                         a["edge_attr_16"][r0:r0 + (TAIL - 1) * P, :]
                         .rearrange("(t p) f -> p t f", p=P)).then_inc(e["edge_got"][0].sem, 16)

            st = NS[1]
            sp.wait_ge(*done(E[0]["z"], BLOCKS - 1))
            for u in range(2):
                sp.wait_ge(*landed_before(NS[0]["store"][2][u], PAIRS_N))
            with sp.Fori(0, FULL_GROUPS // 2) as i:
                for u in range(2):
                    g = i * 2 + u
                    sp.wait_ge(*reuse(st["x"], g))
                    sp.dma_start(slot(buf[0], u), x_in[bass.ds(g * (P * T), P * T), :]
                                 .rearrange("(t p) d -> p t d", p=P)).then_inc(st["load"][0][u].sem, 16)
                    sp.wait_ge(*reuse(st["z"], g))
                    sp.dma_start(buf[1][:, u, :], group(tab_q, g)).then_inc(st["load"][1][u].sem, 16)
                for u in range(2):
                    g = i * 2 + u
                    sp.wait_ge(*done(st["x"], g))
                    sp.dma_start(group(tab_x1, g), buf[6][:, u, :]).then_inc(st["store"][0][u].sem, 16)
                for u in range(2):
                    g = i * 2 + u
                    sp.wait_ge(*done(st["h"], g))
                    sp.dma_start(group(tab_g1, g), buf[4][:, u, :]).then_inc(st["store"][1][u].sem, 16)
            g = FULL_GROUPS
            r0 = g * P * T
            sp.wait_ge(*reuse(st["x"], g))
            sp.dma_start(slot(buf[0], 0)[0:rest, whole, :], x_in[r0 + whole * P:N, :]).then_inc(s_rest, 16)
            n_rest += 1
            sp.wait_ge(s_rest, 16 * n_rest)
            sp.dma_start(slot(buf[0], 0)[:, 0:whole, :], x_in[r0:r0 + whole * P, :]
                         .rearrange("(t p) d -> p t d", p=P)).then_inc(st["load"][0][0].sem, 16)
            sp.wait_ge(*reuse(st["x"], g + 1))
            sp.sem_inc(st["load"][0][1].sem, 16)
            for u in range(2):
                sp.wait_ge(*reuse(st["z"], g + u))
                sp.dma_start(buf[1][:, u, :], group(tab_q, g + u)).then_inc(st["load"][1][u].sem, 16)
            for u in range(2):
                sp.wait_ge(*done(st["x"], g + u))
                sp.dma_start(group(tab_x1, g + u), buf[6][:, u, :]).then_inc(st["store"][0][u].sem, 16)
            for u in range(2):
                sp.wait_ge(*done(st["h"], g + u))
                sp.dma_start(group(tab_g1, g + u), buf[4][:, u, :]).then_inc(st["store"][1][u].sem, 16)

            for j in range(TABLES):
                sp.dma_start(acc[j][NP:NP + P, :], zeros[:, 0:D]).then_inc(s_acc_zero, 16)
            for j in range(1, TABLES):
                sp.dma_start(acc[j][0:NP, :].rearrange("(p g j) d -> p g (j d)", p=P, j=T // 2),
                             zeros[:, :].unsqueeze(1).to_broadcast([P, 2 * NT // T, T * D // 2])).then_inc(s_acc_zero, 16)

            b = lambda j: (lambda u: buf[j][:, u, :])
            stream(NS[2], [], [(b(7), tab_g2, NS[2]["o"])])
            for u in range(2):
                sp.wait_ge(*landed_before(NS[1]["store"][0][u], PAIRS_N))
            stream(NS[3], [(b(0), tab_x1, (NS[3]["x"],))], [(b(6), tab_x2, NS[3]["x"]), (b(4), tab_h2, NS[3]["h"])])
            for u in range(2):
                sp.wait_ge(*landed_before(NS[3]["store"][0][u], PAIRS_N))
                sp.wait_ge(*landed_before(NS[3]["store"][1][u], PAIRS_N))
            cat_h = lambda u: wide[:, u, :].rearrange("p (t c) -> p t c", c=P)[:, :, D:P]
            stream(NS[4], [(cat_h, tab_h2, (NS[4]["ct"],))], [(b(7), tab_h3, NS[4]["o"])])
            for u in range(2):
                sp.wait_ge(*landed_before(NS[4]["store"][0][u], PAIRS_N))
            stream(NS[5], [(cat_h, tab_h3, (NS[5]["ct"],)), (b(0), tab_x2, (NS[5]["x"],))],
                   [(lambda u: rows_u[:, u, :, :].rearrange("p t d -> p (t d)"), tab_wh, NS[5]["nrm2"]),
                    (b(7), acc[0], NS[5]["t0"])])

            e = E[5]

            def src_rows(b, u, n):
                sp.wait_ge(*reuse(e["rows_used"], b))
                v = a["src"][bass.ds(b * (P * T), n * P)] if n == T else a["src"][b * P * T:b * P * T + n * P]
                sp.dma_start(wide[:, u, 0:n * P].bitcast(I32),
                             v.rearrange("(o q) -> o q", o=1).to_broadcast([P, n * P])).then_inc(e["row_got"][u].sem, 16)

            with sp.Fori(0, PAIRS_E) as i:
                for u in range(2):
                    src_rows(i * 2 + u, u, T)
            b_ = BLOCKS - 1
            sp.wait_ge(*reuse(e["rows_used"], b_))
            left = EDGES - b_ * P * T
            sp.dma_start(wide[:, 0, 0:left].bitcast(I32),
                         a["src"][b_ * P * T:EDGES].rearrange("(o q) -> o q", o=1).to_broadcast([P, left])
                         ).then_inc(e["row_got"][0].sem, 16)

            for j in range(TABLES):
                sp.wait_ge(e["table"][j], 16 * scatters(j))
            st = NS[6]

            def out_loads(g, u):
                for j in range(TABLES):
                    sp.wait_ge(*reuse(st["sum"], g))
                    sp.dma_start(buf[j][:, u, :], group(acc[j], g)).then_inc(st["load"][0][u].sem, 16)

            with sp.Fori(0, FULL_GROUPS // 2) as i:
                for u in range(2):
                    g = i * 2 + u
                    out_loads(g, u)
                for u in range(2):
                    g = i * 2 + u
                    sp.wait_ge(*done(st["sum"], g))
                    sp.dma_start(out[bass.ds(g * (P * T), P * T), :].rearrange("(t p) d -> p t d", p=P),
                                 slot(buf[7], u)).then_inc(st["store"][0][u].sem, 16)
            g = FULL_GROUPS
            r0 = g * P * T
            out_loads(g, 0)
            sp.wait_ge(*done(st["sum"], g))
            sp.dma_start(out[r0:r0 + whole * P, :].rearrange("(t p) d -> p t d", p=P),
                         slot(buf[7], 0)[:, 0:whole, :]).then_inc(s_out, 16)
            sp.dma_start(out[r0 + whole * P:N, :], slot(buf[7], 0)[0:rest, whole, :]).then_inc(s_out, 16)
            sp.wait_ge(s_out, 32)
            for u in range(2):
                sp.wait_ge(*landed_before(st["store"][0][u], FULL_GROUPS // 2))

        @block.gpsimd
        def _(pool):
            count = [0]

            def hold(*waits):
                for s, v in waits:
                    pool.wait_ge(s, v)
                pool.sem_inc(s_pool_hold, 1)

            def chain(ins):
                count[0] += 1
                ins.then_inc(s_pool_self, 1)
                pool.wait_ge(s_pool_self, count[0])

            for j, v in ((0, -1), (1, -1), (2, 1 << 20)):
                pool.memset(stage_i[j][:, 3, :], v).then_inc(s_stage_clear, 1)
            pool.memset(wide[:, :, 0:4 * P], 0.0).then_inc(s_stage_clear, 1)
            for j in (0, 1):
                pool.memset(buf[j][:, :, :], 0.0).then_inc(s_stage_clear, 1)
            pool.memset(w_pair[:, :, :], 0.0).then_inc(s_stage_clear, 1)
            for s_ in ring_sems:
                pool.sem_inc(s_, CREDIT)
            for s_ in dma_rings:
                pool.sem_inc(s_, 16)
            pool.sem_inc(s_credit, 1)
            chain(pool.memset(ident[:, :], 0.0))
            chain(pool.affine_select(out=ident[:, :], in_=ident[:, :], compare_op=ALU.not_equal, fill=1.0,
                                     base=0, pattern=[[-1, P]], channel_multiplier=1))
            chain(pool.memset(below[:, :], 1.0))
            chain(pool.affine_select(out=below[:, :], in_=below[:, :], compare_op=ALU.is_gt, fill=0.0,
                                     base=0, pattern=[[-1, P]], channel_multiplier=1))
            chain(pool.memset(block_mask[:, :], 1.0))
            chain(pool.affine_select(out=block_mask[:, :], in_=block_mask[:, :], compare_op=ALU.is_ge, fill=0.0,
                                     base=0, pattern=[[-FE, T]], channel_multiplier=1))
            chain(pool.affine_select(out=block_mask[:, :], in_=block_mask[:, :], compare_op=ALU.is_ge, fill=0.0,
                                     base=FE - 1, pattern=[[FE, T]], channel_multiplier=-1))
            small_ok = dict(allow_small_or_imprecise_dtypes=True)
            chain(pool.iota(iota_node[:, :], pattern=[[1, WINDOW * P]], base=0, channel_multiplier=0, **small_ok))
            chain(pool.iota(iota_tile[:, :], pattern=[[1, NODE_TILES]], base=0, channel_multiplier=0, **small_ok))
            chain(pool.iota(tile_base[:, :], pattern=[[P, NT]], base=0, channel_multiplier=0, **small_ok))
            chain(pool.iota(lane_dump[:, :], pattern=[[0, 1]], base=NP, channel_multiplier=1, **small_ok))
            chain(pool.memset(zeros[:, :], 0.0))
            chain(pool.memset(zeros_b[:, :], 0.0))
            chain(pool.memset(ones[:, :], 1.0))
            chain(pool.memset(minus_one[:, :], -1.0))
            chain(pool.memset(power[:, :], -0.5))
            chain(pool.memset(half[:, :], 0.5))
            for u in range(2):
                chain(pool.memset(rows_u[:, u, :, :], 1.0))
                chain(pool.memset(rows_v[:, u, :, :], 0.0))
            pool.sem_inc(s_const, 1)
            pool.memset(agg[:, :, :], 0.0).then_inc(s_agg0, 1)

            def ln_centre(st, x, i):
                for u in range(2):
                    g = i * 2 + u
                    hold(done(st["mean"], g), reuse(st["h"], g), reuse(st["v"], g))
                    pool.tensor_tensor(slot(buf[2], u), slot(x, u), over_features(small[:, u, 1, :]),
                                       ALU.subtract).then_inc(st["xc"].sem, 1)

            def ln_root(st, i, var=2):
                for u in range(2):
                    g = i * 2 + u
                    hold(done(st["v"], g))
                    pool.tensor_tensor(small[:, u, 4, :], small[:, u, var, :], power[:, :].to_broadcast([P, T]), ALU.pow).then_inc(st["r"].sem, 1)

            def clear_sums(st, used, i):
                for u in range(2):
                    g = i * 2 + u
                    hold(done(used, g))
                    pool.tensor_copy(agg[:, bass.ds(g * T, T), :],
                                     zeros[:, 0:AW].unsqueeze(1).to_broadcast([P, T, AW])).then_inc(st["zero"].sem, 1)

            def gathers(k, table, b, u, n, to, got, idx, width=D):
                for t in range(n):
                    pool.indirect_dma_start(
                        out=to[:, u, t, 0:width] if len(to.shape) == 4 else to[:, u, t * width:(t + 1) * width],
                        out_offset=None, in_=table[:, :],
                        in_offset=bass.IndirectOffsetOnAxis(ap=idx[:, u, t:t + 1], axis=0),
                        bounds_check=NP - 1, oob_is_err=False).then_inc(got[u].sem, 16)

            def over_blocks(body):
                with pool.Fori(0, PAIRS_E) as i:
                    for u in range(2):
                        body(i * 2 + u, u, T)
                body(BLOCKS - 1, 0, TAIL)

            def table_stored(st, j):
                for u in range(2):
                    pool.wait_ge(*landed_before(st["store"][j][u], PAIRS_N))

            with pool.Fori(0, PAIRS_N) as i:
                ln_centre(NS[0], buf[0], i)
                ln_root(NS[0], i)
            table_stored(NS[0], 0)
            table_stored(NS[0], 1)

            def edge0(b, u, n):
                e = E[0]
                hold(done(e["idx"], b), reuse(e["z"], b))
                gathers(0, tab_a, b, u, n, buf[0], e["src_got"], idx_s)
                gathers(0, tab_b, b, u, n, buf[1], e["dst_got"], idx_d)

            over_blocks(edge0)
            pool.wait_ge(s_degrees, 2)
            pool.tensor_tensor(norm_out[:, :], deg_out[:, :], power[:, :].to_broadcast([P, NT]),
                               ALU.pow).then_inc(s_norms, 1)
            pool.tensor_tensor(norm_in[:, :], deg_in[:, :], power[:, :].to_broadcast([P, NT]),
                               ALU.pow).then_inc(s_norms, 1)
            with pool.Fori(0, PAIRS_N) as i:
                clear_sums(NS[1], NS[1]["ag"], i)
                ln_centre(NS[1], buf[6], i)
                ln_root(NS[1], i, 3)

            def plain_gather(k, table):
                def body(b, u, n):
                    kb = b
                    hold(done(E[k]["idx"], kb), reuse(E[k]["consumed"], kb))
                    gathers(k, table, b, u, n, rows_u, E[k]["src_got"], idx_s)
                over_blocks(body)

            table_stored(NS[1], 1)
            plain_gather(1, tab_g1)
            with pool.Fori(0, PAIRS_N) as i:
                clear_sums(NS[2], NS[2]["sc"], i)
            table_stored(NS[2], 0)
            plain_gather(2, tab_g2)
            with pool.Fori(0, PAIRS_N) as i:
                clear_sums(NS[3], NS[3]["sc"], i)
                ln_centre(NS[3], buf[6], i)
                ln_root(NS[3], i)
            table_stored(NS[3], 1)
            plain_gather(3, tab_h2)
            with pool.Fori(0, PAIRS_N) as i:
                clear_sums(NS[4], NS[4]["cat"], i)
            table_stored(NS[4], 0)
            plain_gather(4, tab_h3)
            with pool.Fori(0, PAIRS_N) as i:
                ln_centre(NS[5], buf[6], i)
                ln_root(NS[5], i)
                for u in range(2):
                    g = i * 2 + u
                    hold(done(NS[5]["nrm"], g), landed_before(NS[5]["store"][0][u], i))
                    pool.tensor_tensor(rows_u[:, u, :, D:AW], small[:, u, 5, :].unsqueeze(2),
                                       half[:, :].to_broadcast([P, T]).unsqueeze(2), ALU.pow).then_inc(NS[5]["nrm2"].sem, 1)
            table_stored(NS[5], 0)
            table_stored(NS[5], 1)
            pool.wait_ge(s_acc_zero, 16 * (2 * TABLES - 1))

            e = E[5]

            def pull(b, u, n):
                hold(done(e["idx"], b), reuse(e["contrib"], b))
                gathers(5, tab_wh, b, u, n, rows_u, e["src_got"], idx_s, AW)
                gathers(5, tab_wh, b, u, n, rows_v, e["dst_got"], idx_d, AW)

            def push(b, u, n):
                hold(done(e["oidx"], b), done(e["sum"], b))
                for t in range(n):
                    j = t % TABLES
                    if not (isinstance(b, int) and b == 0 and t < TABLES):
                        hold((e["table"][j], 16 * (b * (T // TABLES) + t // TABLES)))
                    pool.indirect_dma_start(
                        out=acc[j][:, :], out_offset=bass.IndirectOffsetOnAxis(ap=idx_o[:, u, t:t + 1], axis=0),
                        in_=buf[5][:, u, t * D:(t + 1) * D], in_offset=None,
                        bounds_check=NP + P - 1, oob_is_err=True, compute_op=ALU.add).then_inc(e["table"][j], 16)

            pull(0, 0, T)
            pull(1, 1, T)
            for b in range(2):
                push(b, b, T)
                pull(b + 2, b, T)
            with pool.Fori(1, PAIRS_E - 1) as i:
                for u in range(2):
                    push(i * 2 + u, u, T)
                    pull(i * 2 + u + 2, u, T)
            push(BLOCKS - 3, 0, T)
            pull(BLOCKS - 1, 0, TAIL)
            push(BLOCKS - 2, 1, T)
            push(BLOCKS - 1, 0, TAIL)

        @block.scalar
        def _(act):
            act.wait_ge(s_credit, 1)

            def copy(o, i):
                return act.activation(o, i, ACT.Copy)

            def pair(i):
                return [(u, i * 2 + u) for u in range(2)]

            def ln_mean(st, i):
                for u, g in pair(i):
                    act.wait_ge(*done(st["s"], g))
                    act.wait_ge(*reuse(st["xc"], g))
                    act.activation(small[:, u, 1, :], small[:, u, 0, :], ACT.Copy, scale=1.0 / D).then_inc(st["mean"].sem, 1)

            def ln_square(st, i):
                for u, g in pair(i):
                    act.wait_ge(*done(st["xc"], g))
                    act.wait_ge(*reuse(st["v"], g))
                    if st is NS[5]:
                        act.wait_ge(*reuse(st["nrm"], g))
                    act.activation(buf[3][:, u, :], buf[2][:, u, :], ACT.Square).then_inc(st["sq"].sem, 1)

            def evac(st_done, st_wait, reused, ps_of, to, i):
                for u, g in pair(i):
                    act.wait_ge(*done(st_wait, g))
                    act.wait_ge(*reuse(reused, g))
                    copy(to(u), ps_of(u)).then_inc(st_done.sem, 1)

            act.wait_ge(s_exp_args, 1)
            act.activation(par_w[:, 2:5], par_w[:, 8:11], ACT.Exp).then_inc(s_act_setup, 1)
            act.activation(par_w[:, 5:6], par_w[:, 11:12], ACT.Exp).then_inc(s_act_setup, 1)
            act.activation(buf[4][:, 1, :], buf[4][:, 0, :], ACT.Exp).then_inc(s_act_setup, 1)
            act.wait_ge(s_act_setup, 3)
            act.activation(par_w[:, 6:7], par_w[:, 5:6], ACT.Ln, bias=1.0).then_inc(s_act_setup, 1)
            act.activation(buf[5][:, 0, :], buf[4][:, 1, :], ACT.Ln, bias=1.0).then_inc(s_act_setup, 1)

            st = NS[0]
            act.wait_ge(s_setup_done, 1)
            with act.Fori(0, PAIRS_N) as i:
                ln_mean(st, i)
                ln_square(st, i)
                evac(st["htc"], st["ht"], st["mm"], lambda u: ps[u][:, :], lambda u: wide_t[:, u, 0:512], i)
                for u, g in pair(i):
                    act.wait_ge(*done(st["mm"], g))
                    act.wait_ge(*landed_before(st["store"][0][u], i))
                    act.wait_ge(*landed_before(st["store"][1][u], i))
                    act.wait_ge(*landed_before(st["store"][2][u], i))
                    copy(buf[5][:, u, :], ps[2 + u][:, :])
                    copy(buf[6][:, u, :], ps[4 + u][:, :])
                    copy(buf[7][:, u, :], ps[6 + u][:, :]).then_inc(st["o"].sem, 1)

            def copy_indices(k, used, both=False):
                e = E[k]

                def body(b, i, u, n):
                    act.wait_ge(*reuse(used, b))
                    if both:
                        copy(idx_d[:, u, 0:n], cols(dst_row, b, n))
                    copy(idx_s[:, u, 0:n], cols(src_row, b, n)).then_inc(e["idx"].sem, 1)
                return body

            def over_blocks(body):
                with act.Fori(0, PAIRS_E) as i:
                    for u in range(2):
                        body(i * 2 + u, i, u, T)
                body(BLOCKS - 1, PAIRS_E, 0, TAIL)

            e = E[0]
            copy0 = copy_indices(0, e["z"], True)

            def edge0(b, i, u, n):
                if n == T:
                    copy0(b + 1, i + u, 1 - u, T)
                act.wait_ge(*done(e["edge_t"], b))
                act.wait_ge(*reuse(e["z_mm"], b))
                copy(edge_t[:, u, :], ps[5][:, 0:P]).then_inc(e["edge_c"].sem, 1)
                act.wait_ge(*done(e["z"], b))
                act.wait_ge(*reuse(e["msg"], b))
                w = n * D
                act.activation(buf[3][:, u, 0:w], buf[2][:, u, 0:w], ACT.Exp)
                act.activation(buf[4][:, u, 0:w], buf[2][:, u, 0:w], ACT.Relu).then_inc(e["act"].sem, 1)

            copy0(0, 0, 0, T)
            over_blocks(edge0)

            st = NS[1]
            act.wait_ge(E[0]["sums_done"], 1)
            with act.Fori(0, PAIRS_N) as i:
                for u, g in pair(i):
                    act.wait_ge(*reuse(st["at"], g))
                    copy(rows_v[:, u, :, :], agg[:, bass.ds(g * T, T), :]).then_inc(st["ag"].sem, 1)
                for u, g in pair(i):
                    act.wait_ge(*done(st["at"], g))
                    act.wait_ge(*reuse(st["zmm"], g))
                    copy(wide_t[0:AW, u, 0:512], ps[u][0:AW, :])
                    copy(wide_t[0:AW, u, 512:1024], ps[2 + u][0:AW, :]).then_inc(st["atc"].sem, 1)
                for u, g in pair(i):
                    act.wait_ge(*done(st["z"], g))
                    act.wait_ge(*reuse(st["e"], g))
                    act.wait_ge(*reuse(st["v"], g))
                    act.wait_ge(*landed_before(st["store"][1][u], i))
                    act.activation(buf[3][:, u, :], buf[2][:, u, :], ACT.Exp)
                    act.activation(buf[4][:, u, :], buf[2][:, u, :], ACT.Relu).then_inc(st["act"].sem, 1)
                for u, g in pair(i):
                    act.wait_ge(*done(st["et"], g))
                    act.wait_ge(*reuse(st["xmm"], g))
                    copy(wide[:, u, 0:512], ps[u][:, :]).then_inc(st["etc"].sem, 1)
                ln_mean(st, i)
                ln_square(st, i)

            over_blocks(copy_indices(1, E[1]["consumed"]))
            st = NS[2]
            with act.Fori(0, PAIRS_N) as i:
                evac(st["stc"], st["st"], st["mm"], lambda u: ps[u][:, :], lambda u: wide_t[:, u, 0:512], i)
            over_blocks(copy_indices(2, E[2]["consumed"]))
            st = NS[3]
            with act.Fori(0, PAIRS_N) as i:
                evac(st["stc"], st["st"], st["mm"], lambda u: ps[u][:, :], lambda u: wide_t[:, u, 0:512], i)
                ln_mean(st, i)
                ln_square(st, i)
            over_blocks(copy_indices(3, E[3]["consumed"]))

            def evac_cat(st, i):
                for u, g in pair(i):
                    act.wait_ge(*done(st["ct"], g))
                    act.wait_ge(*reuse(st["mm"], g))
                    copy(wide_t[:, u, 0:512], ps[u][:, :])
                    copy(wide_t[:, u, 512:1024], ps[2 + u][:, :]).then_inc(st["ctc"].sem, 1)

            st = NS[4]
            with act.Fori(0, PAIRS_N) as i:
                evac_cat(st, i)
                for u, g in pair(i):
                    act.wait_ge(*done(st["mm"], g))
                    act.wait_ge(*landed_before(st["store"][0][u], i))
                    act.activation(buf[7][:, u, :], ps[4 + u][:, :], ACT.Relu).then_inc(st["o"].sem, 1)
            over_blocks(copy_indices(4, E[4]["consumed"]))
            st = NS[5]
            with act.Fori(0, PAIRS_N) as i:
                evac_cat(st, i)
                ln_mean(st, i)
                ln_square(st, i)
                evac(st["htc"], st["ht"], st["wmm"], lambda u: ps[6 + u][:, :], lambda u: buf[5][:, u, :], i)
                for u, g in pair(i):
                    act.wait_ge(*done(st["wmm"], g))
                    act.wait_ge(*reuse(st["t0"], g))
                    act.wait_ge(*landed_before(st["store"][0][u], i))
                    copy(rows_u[:, u, :, 0:D], ps[u][:, :].rearrange("p (t d) -> p t d", d=D)).then_inc(st["wh"].sem, 1)

            e = E[5]
            copy5 = copy_indices(5, e["contrib"], True)

            def edge5(b, i, u, n):
                copy5(b, i, u, n)

            def edge5_out(b, u, n):
                act.wait_ge(*done(e["dedup"], b))
                for j in range(TABLES):
                    act.wait_ge(e["table"][j], 16 * (b * (T // TABLES) - T // TABLES))
                copy(buf[5][:, u, 0:n * D], ps[u][:, 0:n * D]).then_inc(e["sum"].sem, 1)

            edge5(0, 0, 0, T)
            edge5(1, 0, 1, T)
            for b in range(2):
                act.wait_ge(*done(e["dedup"], b))
                copy(buf[5][:, b, :], ps[b][:, :]).then_inc(e["sum"].sem, 1)
                edge5(b + 2, 1, b, T)
            with act.Fori(1, PAIRS_E - 1) as i:
                for u in range(2):
                    edge5_out(i * 2 + u, u, T)
                    edge5(i * 2 + u + 2, i + 1, u, T)
            edge5_out(BLOCKS - 3, 0, T)
            edge5(BLOCKS - 1, PAIRS_E, 0, TAIL)
            edge5_out(BLOCKS - 2, 1, T)
            edge5_out(BLOCKS - 1, 0, TAIL)

        @block.tensor
        def _(pe):
            def pair(i):
                return [(u, i * 2 + u) for u in range(2)]

            pe.wait_ge(s_const, 1)
            for j in range(4):
                pe.wait_ge((s_src_staged, s_dst_staged)[min(j, 1)], 1)
                w = stage_f if j < 2 else wide[:, j - 2, 0:512].rearrange("p (b q) -> p b q", b=4)
                for q in range(4):
                    m = pe.transpose(ps[j][:, q * P:(q + 1) * P], w[:, q, :], ident[:, :])
                m.then_inc(s_pe_setup, 1)
            for j in range(2):
                pe.wait_ge(s_spans, j + 1)
                w = wide_t[:, j, 0:512].rearrange("p (b q) -> p b q", b=4)
                for q in range(4):
                    m = pe.matmul(ps[4 + j][:, q * P:(q + 1) * P], w[:, q, :], ident[:, :], start=True, stop=True)
                m.then_inc(s_pe_setup, 1)
            pe.wait_ge(s_in, 16 * N_LOADS)
            for q in range(4):
                m = pe.transpose(ps[6][:, q * D:(q + 1) * D], nat[:, q, :], ident[0:D, 0:D])
            for q in range(4, 7):
                m = pe.transpose(ps[6][:, q * D:(q + 1) * D], nat[:, q, :], ident[0:D, 0:D])
            m.then_inc(s_pe_setup, 1)
            pe.transpose(ps[7][:, 0:D], w1e_nat[:, :, :].rearrange("p t f -> p (t f)"), ident[0:D, 0:D]
                         ).then_inc(s_pe_setup, 1)
            pe.wait_ge(s_wt, 1)
            pe.matmul(ps[7][0:AW, D:2 * D], w2m_nat[:, :], wt[0:D, WUM, :], start=True, stop=True
                      ).then_inc(s_pe_setup, 1)

            def add_bias(o, row, n=T):
                pe.matmul(o[:, 0:n * D], ones[0:1, :], bias[0:1, row:row + 1, :].to_broadcast([1, n, D]),
                          start=True, stop=False, skip_group_check=True)

            def products_paired(o, lhs, w, row=None):
                if row is not None:
                    add_bias(o, row)
                for q in range(T // 2):
                    m = pe.matmul(o[:, q * P:(q + 1) * P], lhs[:, q * P:(q + 1) * P], w,
                                  start=row is None, stop=True, skip_group_check=True)
                return m

            def products(o, lhs, k, w, row=None):
                if row is not None:
                    add_bias(o, row)
                for t in range(T):
                    m = pe.matmul(o[:, t * D:(t + 1) * D], lhs[0:k, t * P:(t + 1) * P], w,
                                  start=row is None, stop=True, skip_group_check=True)
                return m

            def transposes_paired(o, x):
                for q in range(T // 2):
                    m = pe.transpose(o[:, q * P:(q + 1) * P], x[:, q * P:(q + 1) * P], ident[:, :])
                return m

            pe.wait_ge(s_setup_done, 1)
            st = NS[0]
            with pe.Fori(0, PAIRS_N) as i:
                for u, g in pair(i):
                    pe.wait_ge(*done(st["h"], g))
                    pe.wait_ge(*reuse(st["htc"], g))
                    transposes_paired(ps[u], buf[4][:, u, :]).then_inc(st["ht"].sem, 1)
                for u, g in pair(i):
                    pe.wait_ge(*done(st["htc"], g))
                    pe.wait_ge(*reuse(st["o"], g))
                    products_paired(ps[2 + u], wide_t[:, u, 0:512], w_pair[:, PA, :])
                    products_paired(ps[4 + u], wide_t[:, u, 0:512], w_pair[:, PB, :], B1M)
                    products_paired(ps[6 + u], wide_t[:, u, 0:512], w_pair[:, PQ, :], B1U).then_inc(st["mm"].sem, 1)

            slow = pe.alloc_register("slow_pe")
            pe.reg_mov(slow, 0)

            def segment(k, msg, width, weights=False):
                e = E[k]

                def body(b, u, n, tile_hook=None):
                    for t in range(n):
                        k_ = b * T + t
                        kt = k_
                        pe.wait_ge(*done(e["hot"], kt))
                        pe.wait_ge(*reuse(e["added"], kt))
                        for w in range(WINDOW):
                            m = pe.matmul(ps[t % 2][:, w * AW:w * AW + width],
                                          hot[:, t % 2, w * P:(w + 1) * P], msg[:, u, t, 0:width],
                                          start=True, stop=True)
                        m.then_inc(e["seg"].sem, 1)
                        if tile_hook:
                            tile_hook(k_, t)
                    beyond(pe, b, lambda t: slow_step(msg, u, t, width), n)
                return body

            def slow_step(msg, u, t, width):
                def step(tile):
                    pe.reg_add(slow, slow, 1)
                    pe.wait_ge(s_slow_built, slow)
                    pe.matmul(ps[2][:, 0:width], hot_x[:, :], msg[:, u, t, 0:width], start=True, stop=True
                              ).then_inc(s_slow_mul, 1)
                return step

            def over_blocks(body):
                with pe.Fori(0, PAIRS_E) as i:
                    for u in range(2):
                        body(i * 2 + u, i, u, T)
                body(BLOCKS - 1, PAIRS_E, 0, TAIL)

            e = E[0]
            seg0 = segment(0, rows_u, AW)
            pe.wait_ge(*done(NS[0]["o"], GROUPS - 1))
            pe.matmul(ps[6][:, 0:NODE_TILES], zeros_b[:, 0:P], zeros_b[:, 0:NODE_TILES],
                      start=True, stop=False, skip_group_check=True)

            def hist(k_, t):
                pe.wait_ge(*done(e["hist_hot"], k_))
                pe.matmul(ps[6][:, 0:NODE_TILES], hot_lo[:, t % 2, :], hot_hi[:, t % 2, :],
                          start=False, stop=False, skip_group_check=True).then_inc(e["hist"].sem, 1)

            def edge0(b, i, u, n):
                pe.wait_ge(*landed(e["edge_got"][u], i))
                pe.wait_ge(*done(e["edge_c"], b - 1))
                pe.transpose(ps[5][:, 0:P], edge_in[:, u, :], ident[:, :]).then_inc(e["edge_t"].sem, 1)
                pe.wait_ge(*done(e["edge_c"], b))
                pe.wait_ge(*reuse(e["z"], b))
                pe.matmul(ps[3 + u][:, 0:n * D], edge_t[:, u, :],
                          w1e_diag[:, 0:n, :].rearrange("p t d -> p (t d)"), start=True, stop=True
                          ).then_inc(e["z_mm"].sem, 1)
                pe.wait_ge(*done(e["msg"], b))
                seg0(b, u, n, hist)

            over_blocks(edge0)
            pe.matmul(ps[6][:, 0:NODE_TILES], zeros_b[:, 0:P], zeros_b[:, 0:NODE_TILES],
                      start=False, stop=True, skip_group_check=True).then_inc(e["hist"].sem, 1)

            st = NS[1]
            with pe.Fori(0, PAIRS_N) as i:
                for u, g in pair(i):
                    pe.wait_ge(*done(st["ag"], g))
                    pe.wait_ge(*reuse(st["atc"], g))
                    pe.wait_ge(*reuse(st["etc"], g))
                    for t in range(T):
                        m = pe.transpose(ps[(t // 4) * 2 + u][0:AW, (t % 4) * P:(t % 4 + 1) * P],
                                         rows_v[:, u, t, :], ident[:, :])
                    m.then_inc(st["at"].sem, 1)
                for u, g in pair(i):
                    pe.wait_ge(*done(st["atc"], g))
                    pe.wait_ge(*reuse(st["z"], g))
                    products(ps[4 + u], wide_t[:, u, :], AW, w_upd_agg[:, :]).then_inc(st["zmm"].sem, 1)
                for u, g in pair(i):
                    pe.wait_ge(*done(st["e"], g))
                    transposes_paired(ps[u], buf[5][:, u, :]).then_inc(st["et"].sem, 1)
                for u, g in pair(i):
                    pe.wait_ge(*done(st["etc"], g))
                    pe.wait_ge(*reuse(st["x"], g))
                    products_paired(ps[6 + u], wide[:, u, 0:512], w_pair[:, PU2, :], B2U).then_inc(st["xmm"].sem, 1)

            def plain_segment(k):
                seg = segment(k, rows_u, D)

                def body(b, i, u, n):
                    pe.wait_ge(E[k]["src_got"][u].sem, E[k]["src_got"][u].base + gathered(i) + 16 * n)
                    seg(b, u, n)
                over_blocks(body)

            def graph_conv(st, row, w):
                with pe.Fori(0, PAIRS_N) as i:
                    for u, g in pair(i):
                        pe.wait_ge(*done(st["sc"], g))
                        pe.wait_ge(*reuse(st["stc"], g))
                        transposes_paired(ps[u], buf[5][:, u, :]).then_inc(st["st"].sem, 1)
                    for u, g in pair(i):
                        pe.wait_ge(*done(st["stc"], g))
                        pe.wait_ge(*reuse(st["o"] if st is NS[2] else st["x"], g))
                        products_paired(ps[4 + u], wide_t[:, u, 0:512], w_pair[:, w, :], row).then_inc(st["mm"].sem, 1)

            plain_segment(1)
            graph_conv(NS[2], BG1, PG1)
            plain_segment(2)
            graph_conv(NS[3], BG2, PG2)
            plain_segment(3)

            def conv_cat(st, i, w, row, freed):
                for u, g in pair(i):
                    pe.wait_ge(*done(st["cat"], g))
                    pe.wait_ge(*landed(st["load"][0][u], i))
                    pe.wait_ge(*reuse(st["ctc"], g))
                    if st is NS[5]:
                        pe.wait_ge(*reuse(st["wh"], g))
                    for t in range(T):
                        m = pe.transpose(ps[(t // 4) * 2 + u][:, (t % 4) * P:(t % 4 + 1) * P],
                                         wide[:, u, t * P:(t + 1) * P], ident[:, :])
                    m.then_inc(st["ct"].sem, 1)
                for u, g in pair(i):
                    pe.wait_ge(*done(st["ctc"], g))
                    pe.wait_ge(*reuse(freed, g))
                    products(ps[4 + u], wide_t[:, u, :], P, wt[:, w, :], row).then_inc(st["mm"].sem, 1)

            with pe.Fori(0, PAIRS_N) as i:
                conv_cat(NS[4], i, WC1, BR1, NS[4]["o"])
            plain_segment(4)
            st = NS[5]
            with pe.Fori(0, PAIRS_N) as i:
                conv_cat(st, i, WC2, BR2, st["x"])
                for u, g in pair(i):
                    pe.wait_ge(*done(st["h"], g))
                    pe.wait_ge(*reuse(st["htc"], g))
                    transposes_paired(ps[6 + u], buf[4][:, u, :]).then_inc(st["ht"].sem, 1)
                for u, g in pair(i):
                    pe.wait_ge(*done(st["htc"], g))
                    pe.wait_ge(*reuse(st["nrm"], g))
                    products_paired(ps[u], buf[5][:, u, :], w_pair[:, PL3, :], BL3).then_inc(st["wmm"].sem, 1)

            e = E[5]

            def edge5(b, i, u, n):
                pe.wait_ge(*reuse(e["sum"], b))
                for t in range(n):
                    pe.wait_ge(*done(e["same"], b * T + t))
                    m = pe.matmul(ps[u][:, t * D:(t + 1) * D], same[:, t % 2, 0:P], buf[4][:, u, t * D:(t + 1) * D],
                                  start=True, stop=True)
                    m.then_inc(e["same_used"].sem, 1)
                pe.wait_ge(*done(e["same_used"], b * T + n - 1))
                pe.sem_inc(e["dedup"].sem, 1)
            over_blocks(edge5)

        @block.vector
        def _(dve):
            count = [0]

            def link(ins, wait=True):
                count[0] += 1
                ins.then_inc(s_dve, 1)
                if wait:
                    dve.wait_ge(s_dve, count[0])
                return count[0]

            def pair(i):
                return [(u, i * 2 + u) for u in range(2)]

            V = nc.vector
            dve.wait_ge(s_credit, 1)
            dve.wait_ge(s_const, 1)
            dve.wait_ge(s_idx_in, 16 * 15)
            link(V.tensor_copy(stage_f[:, :, :], stage_i[0][:, :, :]))
            dve.sem_inc(s_src_staged, 1)
            dve.wait_ge(s_pe_setup, 1)
            link(V.tensor_copy(src_f[:, :, :], ps[0][:, :].rearrange("p (b q) -> p b q", b=4)))
            link(V.tensor_copy(stage_f[:, :, :], stage_i[1][:, :, :]))
            dve.sem_inc(s_dst_staged, 1)
            dve.wait_ge(s_pe_setup, 2)
            link(V.tensor_copy(dst_f[:, :, :], ps[1][:, :].rearrange("p (b q) -> p b q", b=4)))
            dve.wait_ge(s_pe_setup, 4)
            link(V.tensor_copy(ew[:, :], ps[2][:, :]))
            link(V.tensor_copy(buf[5][:, 1, :], ps[3][:, :]))
            link(V.tensor_reduce(first_i[:, :], stage_i[2][:, :, :], AX_X, ALU.min))
            link(V.tensor_reduce(last_i[:, :], stage_i[1][:, :, :], AX_X, ALU.max))
            link(V.tensor_scalar(first_i[:, :], first_i[:, :], float(N - 1), None, ALU.min))
            link(V.tensor_scalar(last_i[:, :], last_i[:, :], 0.0, None, ALU.max))
            for k_, x in enumerate((first_i, last_i)):
                link(V.tensor_scalar(x[:, :], x[:, :], 7, None, ALU.arith_shift_right))
                link(V.tensor_copy(span_f[:, :, k_], x[:, :]))
                w = wide_t[:, k_, 0:512].rearrange("p (b q) -> p b q", b=4)
                for q in range(4):
                    link(V.tensor_scalar(w[:, q, :], ones[:, :], span_f[:, q, k_:k_ + 1], None, ALU.mult))
                dve.sem_inc(s_spans, 1)
            dve.wait_ge(s_pe_setup, 6)
            link(V.tensor_copy(first_f[:, :], ps[4][:, :]))
            link(V.tensor_copy(last_f[:, :], ps[5][:, :]))
            link(V.tensor_copy(first_row[:, :], first_f[0:1, :]))
            link(V.scalar_tensor_tensor(out=rel[:, :, :].rearrange("p b q -> p (b q)"), in0=first_f[:, :],
                                        scalar=float(-P), in1=dst_f[:, :, :].rearrange("p b q -> p (b q)"),
                                        op0=ALU.mult, op1=ALU.add))
            link(V.tensor_scalar(beyond_f[:, :], first_f[0:1, :], float(WINDOW + 1), None, ALU.add))
            link(V.tensor_scalar(last_f[0:1, :], last_f[0:1, :], 1.0, None, ALU.add))
            link(V.tensor_tensor(xhi_row[:, :], beyond_f[:, :], last_f[0:1, :], ALU.max))
            link(V.tensor_tensor(beyond_f[:, :], last_f[0:1, :], beyond_f[:, :], ALU.is_ge))
            link(V.tensor_reduce(beyond_i[:, :], beyond_f[:, :].rearrange("o (b t) -> o b t", t=T), AX_X, ALU.max))
            ia, ib = stage_i[0][:, :, :].rearrange("p b q -> p (b q)"), stage_i[1][:, :, :].rearrange("p b q -> p (b q)")
            ic = stage_i[2][:, :, :].rearrange("p b q -> p (b q)")
            for x, row in ((src_f, src_row), (dst_f, dst_row)):
                xf = x[:, :, :].rearrange("p b q -> p (b q)")
                link(V.tensor_scalar(ia, xf, 0.0, None, ALU.max))
                link(V.tensor_scalar(ib, ia, P - 1, 3, ALU.bitwise_and, ALU.logical_shift_left))
                link(V.tensor_scalar(ic, ia, 7, T - 1, ALU.arith_shift_right, ALU.bitwise_and))
                link(V.tensor_tensor(ib, ib, ic, ALU.add))
                link(V.tensor_scalar(ic, ia, 10, None, ALU.arith_shift_right))
                link(V.tensor_scalar(ic, ic, P * T, None, ALU.mult))
                link(V.tensor_tensor(row[:, :], ib, ic, ALU.add))
            link(V.tensor_copy(ia, src_f[:, :, :].rearrange("p b q -> p (b q)")))
            link(V.tensor_scalar(ib, ia, P - 1, None, ALU.bitwise_and))
            link(V.tensor_copy(src_lo[:, :], ib))
            link(V.tensor_scalar(ib, ia, 7, None, ALU.arith_shift_right))
            link(V.tensor_copy(src_hi[:, :], ib))
            sf = src_f[:, :, :].rearrange("p b q -> p (b q)")
            dve.wait_ge(s_in, 16 * N_LOADS)
            link(V.tensor_reduce(par_w[:, 0:1], par[:, 2:5], AX_X, ALU.max))
            link(V.tensor_scalar(par_w[:, 8:11], par[:, 2:5], par_w[:, 0:1], None, ALU.subtract))
            link(V.tensor_scalar(par_w[:, 12:13], par[:, 5:6], -1.0, None, ALU.mult))
            link(V.tensor_tensor(par_w[:, 11:12], par_w[:, 12:13], par[:, 5:6], ALU.min))
            link(V.tensor_scalar(par_w[:, 13:14], par[:, 5:6], 0.0, None, ALU.max))
            link(V.tensor_scalar(buf[6][:, 0, :], buf[5][:, 1, :], par[:, 0:1], par[:, 1:2], ALU.mult, ALU.add))
            link(V.tensor_scalar(buf[6][:, 1, :], buf[6][:, 0, :], -1.0, None, ALU.mult))
            link(V.tensor_tensor(buf[4][:, 0, :], buf[6][:, 0, :], buf[6][:, 1, :], ALU.min))
            dve.sem_inc(s_exp_args, 1)
            dve.wait_ge(s_act_setup, 5)
            link(V.scalar_tensor_tensor(out=base[:, :], in0=buf[6][:, 0, :], scalar=0.0, in1=buf[5][:, 0, :],
                                        op0=ALU.max, op1=ALU.add))
            link(V.tensor_tensor(base[:, :], base[:, :], ew[:, :], ALU.mult))
            link(V.tensor_tensor(buf[6][:, 0, :], sf, dst_f[:, :, :].rearrange("p b q -> p (b q)"), ALU.not_equal))
            link(V.tensor_tensor(base[:, :], base[:, :], buf[6][:, 0, :], ALU.mult))
            link(V.tensor_reduce(par_w[:, 0:1], par_w[:, 2:5], AX_X, ALU.add))
            link(V.reciprocal(par_w[:, 1:2], par_w[:, 0:1]))
            link(V.tensor_tensor(par_w[:, 7:8], par_w[:, 6:7], par_w[:, 13:14], ALU.add))
            link(V.tensor_tensor(par_w[:, 1:2], par_w[:, 1:2], par_w[:, 7:8], ALU.mult))
            link(V.tensor_scalar(par_w[:, 8:11], par_w[:, 2:5], par_w[:, 1:2], None, ALU.mult))
            dve.wait_ge(s_pe_setup, 8)
            link(V.tensor_copy(wt[:, :, :], ps[6][:, 0:7 * D].rearrange("p (w d) -> p w d", d=D)))
            for h in range(2):
                r = slice(h * D, (h + 1) * D)
                link(V.tensor_copy(w_pair[r, PA:PU2 + 1, r], wt[r, WA:WU2 + 1, :]))
            link(V.tensor_copy(w1e_t[:, :], ps[7][:, 0:D]))
            dve.sem_inc(s_wt, 1)
            for t in range(T):
                link(V.tensor_scalar(w1e_diag[:, t, :], w1e_t[:, :], block_mask[:, t:t + 1], None, ALU.mult))
            dve.wait_ge(s_pe_setup, 9)
            link(V.tensor_copy(w_upd_agg[:, :], ps[7][0:AW, D:2 * D]))
            link(V.memset(deg_out[:, :], 1.0))
            dve.sem_inc(s_setup_done, 1)

            def ln_sum(st, x, i, ready):
                for u, g in pair(i):
                    ready(u, g)
                    dve.wait_ge(*reuse(st["mean"], g))
                    V.tensor_reduce(small[:, u, 0, :], slot(x, u), AX_X, ALU.add).then_inc(st["s"].sem, 1)

            def ln_var(st, self_, i, norm=False):
                for u, g in pair(i):
                    dve.wait_ge(*done(st["sq"], g))
                    dve.wait_ge(*reuse(st["r"], g))
                    V.tensor_reduce(small[:, u, 6, :], slot(buf[3], u), AX_X, ALU.add).then_inc(self_[u], 1)
                for u, g in pair(i):
                    dve.wait_ge(self_[u], (i * (2 if norm else 1)) + 1)
                    m = V.tensor_scalar(small[:, u, 2, :], small[:, u, 6, :], 1.0 / D, EPS, ALU.mult, ALU.add)
                    m.then_inc(self_[u] if norm else st["v"].sem, 1)
                if norm:
                    for u, g in pair(i):
                        dve.wait_ge(self_[u], i * 2 + 2)
                        V.tensor_tensor(small[:, u, 3, :], small[:, u, 2, :], cols(deg_out, g, T), ALU.mult
                                        ).then_inc(st["v"].sem, 1)

            def ln_out(st, i, freed):
                for u, g in pair(i):
                    dve.wait_ge(*done(st["r"], g))
                    freed(i, u, g)
                    V.scalar_tensor_tensor(out=slot(buf[4], u), in0=slot(buf[2], u), scalar=0.0,
                                           in1=over_features(small[:, u, 4, :]), op0=ALU.max, op1=ALU.mult
                                           ).then_inc(st["h"].sem, 1)

            st = NS[0]
            with dve.Fori(0, PAIRS_N) as i:
                ln_sum(st, buf[0], i, lambda u, g: dve.wait_ge(*landed(st["load"][0][u], i)))
                ln_var(st, ln_self[0], i)
                ln_out(st, i, lambda i, u, g: dve.wait_ge(*reuse(st["ht"], g)))

            slow = dve.alloc_register("slow_dve")
            dve.reg_mov(slow, 0)

            def segment(k, msg, width, weighted):
                e = E[k]

                def build(k_, t):
                    dve.wait_ge(*reuse(e["seg"], k_))
                    V.tensor_scalar(hot[:, t % 2, :], iota_node[:, :],
                                    rel[:, :, :].rearrange("p b q -> p (b q)")[:, bass.ds(k_, 1)],
                                    ew[:, bass.ds(k_, 1)] if weighted else None,
                                    ALU.is_equal, *([ALU.mult] if weighted else [])).then_inc(e["hot"].sem, 1)

                def add(k_, t):
                    first = dve.value_load(first_row[0:1, bass.ds(k_, 1)], min_val=0, max_val=NODE_TILES - 1)
                    dve.wait_ge(*done(e["seg"], k_))
                    dve.wait_ge(*done(e["added"], k_ - 1))
                    o = agg[:, bass.ds(first, WINDOW), 0:width]
                    V.tensor_tensor(o, o, ps[t % 2][:, 0:WINDOW * AW].rearrange("p (w d) -> p w d", d=AW)[:, :, 0:width],
                                    ALU.add).then_inc(e["added"].sem, 1)

                def slow_step(b, t):
                    k_ = b * T + t

                    def step(tile):
                        dve.reg_add(slow, slow, 1)
                        V.tensor_scalar(hot_x[:, :], iota_node[:, 0:P], tile_base[:, bass.ds(tile, 1)],
                                        dst_f[:, :, :].rearrange("p b q -> p (b q)")[:, bass.ds(k_, 1)],
                                        ALU.add, ALU.is_equal).then_inc(s_slow_self, 1)
                        dve.wait_ge(s_slow_self, slow)
                        if weighted:
                            V.tensor_scalar(hot_x[:, :], hot_x[:, :], ew[:, bass.ds(k_, 1)], None, ALU.mult
                                            ).then_inc(s_slow_built, 1)
                        else:
                            V.tensor_copy(hot_x[:, :], hot_x[:, :]).then_inc(s_slow_built, 1)
                        dve.wait_ge(s_slow_mul, slow)
                        o = agg[:, bass.ds(tile, 1), 0:width].rearrange("p o d -> p (o d)")
                        V.tensor_tensor(o, o, ps[2][:, 0:width], ALU.add).then_inc(s_slow_added, 1)
                        dve.wait_ge(s_slow_added, slow)
                    return step

                def body(b, u, n, tile_hook=None):
                    for t in range(n):
                        build(b * T + t, t)
                        if t:
                            add(b * T + t - 1, t - 1)
                        if tile_hook:
                            tile_hook(b * T + t, t)
                    add(b * T + n - 1, n - 1)
                    dve.wait_ge(*done(e["added"], b * T + n - 1))
                    beyond(dve, b, lambda t: slow_step(b, t), n)
                    dve.sem_inc(e["consumed"].sem, 1)
                return body

            def over_blocks(body):
                with dve.Fori(0, PAIRS_E) as i:
                    for u in range(2):
                        body(i * 2 + u, i, u, T)
                body(BLOCKS - 1, PAIRS_E, 0, TAIL)

            e = E[0]
            seg0 = segment(0, rows_u, AW, False)

            def hist_hot(k_, t):
                dve.wait_ge(*reuse(e["hist"], k_))
                V.tensor_scalar(hot_lo[:, t % 2, :], iota_node[:, 0:P], src_lo[:, bass.ds(k_, 1)], None, ALU.is_equal)
                V.tensor_scalar(hot_hi[:, t % 2, :], iota_tile[:, :], src_hi[:, bass.ds(k_, 1)], None, ALU.is_equal
                                ).then_inc(e["hist_hot"].sem, 1)

            def edge0(b, i, u, n):
                w = n * D
                dve.wait_ge(e["src_got"][u].sem, e["src_got"][u].base + gathered(i) + 16 * n)
                dve.wait_ge(e["dst_got"][u].sem, e["dst_got"][u].base + gathered(i) + 16 * n)
                dve.wait_ge(*reuse(e["act"], b))
                dve.wait_ge(*reuse(e["z"], b))
                V.tensor_tensor(buf[6][:, u, 0:w], buf[0][:, u, 0:w], buf[1][:, u, 0:w], ALU.add
                                ).then_inc(s_z_self, 1)
                dve.wait_ge(s_z_self, b + 1)
                dve.wait_ge(*done(e["z_mm"], b))
                V.tensor_tensor(buf[2][:, u, 0:w], buf[6][:, u, 0:w], ps[3 + u][:, 0:w], ALU.add).then_inc(e["z"].sem, 1)
                dve.wait_ge(*done(e["act"], b))
                V.tensor_scalar(buf[3][:, u, 0:w], buf[3][:, u, 0:w], 1.0, -1.0, ALU.min, ALU.add
                                ).then_inc(s_elu_self, 1)
                dve.wait_ge(s_elu_self, b + 1)
                dve.wait_ge(*reuse(e["consumed"], b))
                V.tensor_tensor(rows_u[:, u, 0:n, 0:D], buf[3][:, u, 0:w].rearrange("p (t d) -> p t d", d=D),
                                buf[4][:, u, 0:w].rearrange("p (t d) -> p t d", d=D), ALU.add).then_inc(e["msg"].sem, 1)
                seg0(b, u, n, hist_hot)

            dve.wait_ge(s_agg0, 1)
            over_blocks(edge0)
            dve.wait_ge(*done(e["hist"], ET))
            V.tensor_scalar(deg_out[:, 0:NODE_TILES], ps[6][:, 0:NODE_TILES], 1.0, None, ALU.max).then_inc(s_degrees, 1)
            V.tensor_scalar(deg_in[:, :], agg[:, :, D:AW].rearrange("p t o -> p (t o)"), 1.0, None, ALU.max
                            ).then_inc(s_degrees, 1)
            dve.wait_ge(s_degrees, 2)
            dve.sem_inc(e["sums_done"], 1)

            st = NS[1]
            dve.wait_ge(s_norms, 2)
            with dve.Fori(0, PAIRS_N) as i:
                for u, g in pair(i):
                    dve.wait_ge(*done(st["zmm"], g))
                    dve.wait_ge(*landed(st["load"][1][u], i))
                    dve.wait_ge(*reuse(st["act"], g))
                    dve.wait_ge(*reuse(st["h"], g))
                    V.tensor_tensor(buf[2][:, u, :], ps[4 + u][:, :], buf[1][:, u, :], ALU.add).then_inc(st["z"].sem, 1)
                for u, g in pair(i):
                    dve.wait_ge(*done(st["act"], g))
                    V.tensor_scalar(buf[3][:, u, :], buf[3][:, u, :], 1.0, -1.0, ALU.min, ALU.add
                                    ).then_inc(s_elu1_self, 1)
                for u, g in pair(i):
                    dve.wait_ge(s_elu1_self, g + 1)
                    dve.wait_ge(*reuse(st["et"], g))
                    V.tensor_tensor(buf[5][:, u, :], buf[3][:, u, :], buf[4][:, u, :], ALU.add).then_inc(st["e"].sem, 1)
                for u, g in pair(i):
                    dve.wait_ge(*done(st["xmm"], g))
                    dve.wait_ge(*landed(st["load"][0][u], i))
                    dve.wait_ge(*landed_before(st["store"][0][u], i))
                    V.tensor_tensor(buf[6][:, u, :], ps[6 + u][:, :], buf[0][:, u, :], ALU.add).then_inc(st["x"].sem, 1)
                ln_sum(st, buf[6], i, lambda u, g: dve.wait_ge(*done(st["x"], g)))
                ln_var(st, ln_self[1], i, True)
                ln_out(st, i, lambda i, u, g: dve.wait_ge(*landed_before(st["store"][1][u], i)))

            def plain_segment(k, weighted):
                seg = segment(k, rows_u, D, weighted)
                over_blocks(lambda b, i, u, n: seg(b, u, n))

            def sums_cleared(st):
                dve.wait_ge(*done(st["zero"], GROUPS - 1))

            def scaled_sums(st, i):
                for u, g in pair(i):
                    dve.wait_ge(*reuse(st["st"], g))
                    V.tensor_tensor(slot(buf[5], u), agg[:, bass.ds(g * T, T), 0:D],
                                    over_features(cols(norm_in, g, T)), ALU.mult).then_inc(st["sc"].sem, 1)

            sums_cleared(NS[1])
            plain_segment(1, False)
            st = NS[2]
            with dve.Fori(0, PAIRS_N) as i:
                scaled_sums(st, i)
                for u, g in pair(i):
                    dve.wait_ge(*done(st["mm"], g))
                    dve.wait_ge(*landed_before(st["store"][0][u], i))
                    V.scalar_tensor_tensor(out=slot(buf[7], u), in0=ps[4 + u][:, :].rearrange("p (t d) -> p t d", d=D),
                                           scalar=0.0, in1=over_features(cols(norm_out, g, T)),
                                           op0=ALU.max, op1=ALU.mult).then_inc(st["o"].sem, 1)
            sums_cleared(NS[2])
            plain_segment(2, False)
            st = NS[3]
            with dve.Fori(0, PAIRS_N) as i:
                scaled_sums(st, i)
                for u, g in pair(i):
                    dve.wait_ge(*done(st["mm"], g))
                    dve.wait_ge(*landed(st["load"][0][u], i))
                    dve.wait_ge(*landed_before(st["store"][0][u], i))
                    dve.wait_ge(*reuse(st["xc"], g))
                    V.scalar_tensor_tensor(out=buf[6][:, u, :], in0=ps[4 + u][:, :], scalar=0.0, in1=buf[0][:, u, :],
                                           op0=ALU.max, op1=ALU.add).then_inc(st["x"].sem, 1)
                ln_sum(st, buf[6], i, lambda u, g: dve.wait_ge(*done(st["x"], g)))
                ln_var(st, ln_self[2], i)
                ln_out(st, i, lambda i, u, g: dve.wait_ge(*landed_before(st["store"][1][u], i)))
            sums_cleared(NS[3])
            plain_segment(3, True)

            def cat(st, i):
                for u, g in pair(i):
                    dve.wait_ge(*reuse(st["ct"], g))
                    V.tensor_copy(wide[:, u, :].rearrange("p (t c) -> p t c", c=P)[:, :, 0:D],
                                  agg[:, bass.ds(g * T, T), 0:D]).then_inc(st["cat"].sem, 1)

            st = NS[4]
            with dve.Fori(0, PAIRS_N) as i:
                cat(st, i)
            sums_cleared(NS[4])
            plain_segment(4, True)
            st = NS[5]
            with dve.Fori(0, PAIRS_N) as i:
                cat(st, i)
                for u, g in pair(i):
                    dve.wait_ge(*done(st["mm"], g))
                    dve.wait_ge(*landed(st["load"][1][u], i))
                    dve.wait_ge(*reuse(st["t0"], g))
                    V.tensor_tensor(buf[6][:, u, :], ps[4 + u][:, :], buf[0][:, u, :], ALU.add).then_inc(st["x"].sem, 1)
                ln_sum(st, buf[6], i, lambda u, g: dve.wait_ge(*done(st["x"], g)))
                ln_var(st, ln_self[3], i)
                ln_out(st, i, lambda i, u, g: dve.wait_ge(*reuse(st["ht"], g)))
                for u, g in pair(i):
                    dve.wait_ge(*done(st["wh"], g))
                    dve.wait_ge(*done(st["v"], g))
                    V.tensor_tensor(slot(buf[3], u), rows_u[:, u, :, 0:D], rows_u[:, u, :, 0:D], ALU.mult
                                    ).then_inc(s_sq_self, 1)
                for u, g in pair(i):
                    dve.wait_ge(s_sq_self, g + 1)
                    dve.wait_ge(*reuse(st["nrm2"], g))
                    V.tensor_reduce(small[:, u, 5, :], slot(buf[3], u), AX_X, ALU.add).then_inc(st["nrm"].sem, 1)
                for u, g in pair(i):
                    dve.wait_ge(*landed_before(st["store"][1][u], i))
                    V.scalar_tensor_tensor(out=slot(buf[7], u), in0=rows_u[:, u, :, 0:D], scalar=par_w[:, 10:11],
                                           in1=slot(buf[6], u), op0=ALU.mult, op1=ALU.add).then_inc(st["t0"].sem, 1)

            e = E[5]
            s5 = [0]

            def edge5(b, i, u, n):
                s = small[:, u, :, 0:n]
                step = [0]

                def mine(ins):
                    step[0] += 1
                    ins.then_inc(s_e5[u], 1)
                    dve.wait_ge(s_e5[u], i * E5_STEPS + step[0])

                wr, wc = rows_u[:, u, 0:n, :], rows_v[:, u, 0:n, :]
                c = lambda x: x[:, u, 0:n * D].rearrange("p (t d) -> p t d", d=D)
                dve.wait_ge(e["src_got"][u].sem, e["src_got"][u].base + gathered(i) + 16 * n)
                dve.wait_ge(e["dst_got"][u].sem, e["dst_got"][u].base + gathered(i) + 16 * n)
                mine(V.tensor_tensor(c(buf[2]), wr[:, :, 0:D], wc[:, :, 0:D], ALU.mult))
                mine(V.tensor_reduce(s[:, 0, :], c(buf[2]), AX_X, ALU.add))
                mine(V.tensor_tensor(s[:, 1, :].unsqueeze(2), wr[:, :, D:AW], wc[:, :, D:AW], ALU.mult))
                mine(V.tensor_scalar(s[:, 1, :], s[:, 1, :], SIM_EPS, None, ALU.max))
                mine(V.reciprocal(s[:, 2, :], s[:, 1, :]))
                mine(V.tensor_tensor(s[:, 3, :], s[:, 0, :], s[:, 2, :], ALU.mult))
                mine(V.tensor_scalar(s[:, 4, :], s[:, 3, :], 0.0, par_w[:, 8:9], ALU.max, ALU.mult))
                mine(V.tensor_scalar(s[:, 5, :], s[:, 3, :], 0.0, par_w[:, 9:10], ALU.min, ALU.mult))
                mine(V.tensor_tensor(s[:, 4, :], s[:, 4, :], s[:, 5, :], ALU.add))
                mine(V.tensor_tensor(s[:, 6, :], s[:, 4, :], cols(base, b, n), ALU.mult))
                dve.wait_ge(*reuse(e["dedup"], b))
                V.tensor_tensor(c(buf[4]), wc[:, :, 0:D], s[:, 6, :].unsqueeze(2).to_broadcast([P, n, D]),
                                ALU.mult).then_inc(e["contrib"].sem, 1)
                dve.wait_ge(*done(e["contrib"], b))
                dve.wait_ge(*landed(e["row_got"][u], i))
                for t in range(n):
                    k_ = b * T + t
                    dve.wait_ge(*reuse(e["same_used"], k_))
                    V.tensor_scalar(same[:, t % 2, 0:P], wide[:, u, t * P:(t + 1) * P].bitcast(I32), sf[:, bass.ds(k_, 1)],
                                    None, ALU.is_equal).then_inc(e["same"].sem, 1)
                    dve.wait_ge(*done(e["same"], k_))
                    mine(V.tensor_tensor_reduce(junk[:, :], same[:, t % 2, 0:P], below[:, :], 1.0, 0.0,
                                                ALU.mult, ALU.add, s[:, 7, t:t + 1]))
                dve.sem_inc(e["rows_used"].sem, 1)
                mine(V.tensor_scalar(s[:, 8, :], s[:, 7, :], 0.5, None, ALU.is_lt))
                mine(V.tensor_scalar(s[:, 9, :], cols(sf, b, n), 0.0, None, ALU.is_ge))
                mine(V.tensor_tensor(s[:, 8, :], s[:, 8, :], s[:, 9, :], ALU.mult))
                mine(V.tensor_scalar(s[:, 9, :], cols(src_row, b, n), lane_dump[:, 0:1], None, ALU.subtract))
                mine(V.tensor_tensor(s[:, 8, :], s[:, 8, :], s[:, 9, :], ALU.mult))
                dve.wait_ge(*done(e["sum"], b))
                V.tensor_scalar(idx_o[:, u, 0:n], s[:, 8, :], lane_dump[:, 0:1], None, ALU.add).then_inc(e["oidx"].sem, 1)
                assert n != T or step[0] == E5_STEPS, step

            over_blocks(edge5)

            st = NS[6]

            def total(g, i, u):
                dve.wait_ge(st["load"][0][u].sem, st["load"][0][u].base + 16 * (TABLES * (i + 1) + 1))
                V.tensor_tensor(buf[4][:, u, :], buf[0][:, u, :], buf[1][:, u, :], ALU.add).then_inc(s_total_self[u], 1)
                V.tensor_tensor(buf[5][:, u, :], buf[2][:, u, :], buf[3][:, u, :], ALU.add).then_inc(s_total_self[u], 1)
                dve.wait_ge(s_total_self[u], i * 2 + 2)
                dve.wait_ge(*landed_before(st["store"][0][u], i))
                V.tensor_tensor(buf[7][:, u, :], buf[4][:, u, :], buf[5][:, u, :], ALU.add).then_inc(st["sum"].sem, 1)

            with dve.Fori(0, FULL_GROUPS // 2) as i:
                for u, g in pair(i):
                    total(g, i, u)
            total(FULL_GROUPS, FULL_GROUPS // 2, 0)


_INS = ['x', 'src', 'dst', 'edge_attr_16', 'edge_weight', 'edge_weight_n2', 'L0_gnn_W1m', 'L0_gnn_b1m', 'L0_gnn_W2m',
        'L0_gnn_b2m', 'L0_gnn_W1u', 'L0_gnn_b1u', 'L0_gnn_W2u', 'L0_gnn_b2u', 'L1_gnn_W1', 'L1_gnn_b1', 'L1_gnn_W2',
        'L1_gnn_b2', 'L2_gnn_W_rel1', 'L2_gnn_b_rel1', 'L2_gnn_W_root1', 'L2_gnn_W_rel2', 'L2_gnn_b_rel2',
        'L2_gnn_W_root2', 'L3_gnn_W', 'L3_gnn_b', 'L3_gnn_deg_coeff', 'L3_gnn_coeff_param', 'L3_gnn_scale_param']


def kernel(**inputs):
    import numpy as _np
    import concourse.bacc as _bacc
    from concourse import mybir as _mybir
    from concourse.bass_utils import run_bass_kernel_spmd as _run

    nc = _bacc.Bacc("TRN2", target_bir_lowering=False, num_devices=1)
    arrays, args = {}, {}
    for name in _INS:
        v = _np.ascontiguousarray(inputs[name])
        arrays[f"in_{name}_dram"] = v
        args[name] = nc.dram_tensor(f"in_{name}_dram", v.shape, _mybir.dt.from_np(v.dtype), kind="ExternalInput").ap()
    result = nc.dram_tensor("out_0_dram", (N, D), _mybir.dt.float32, kind="ExternalOutput").ap()
    program(nc, args, result)
    r = _run(nc, [arrays], core_ids=[0])
    return r.results[0]["out_0_dram"]
```

```python
from contextlib import ExitStack

import concourse.bass as bass
from concourse import mybir
from concourse.alu_op_type import AluOpType as ALU

F32 = mybir.dt.float32
I32 = mybir.dt.int32
BF16 = mybir.dt.bfloat16
ACT = mybir.ActivationFunctionType
AX_X = mybir.AxisListType.X

P = 128
D = 64
FE = 16
T = 8
N = 50000
EDGES = 50000
ET = -(-EDGES // P)
LAST = EDGES - (ET - 1) * P
BLOCKS = -(-ET // T)
PAIRS_E = (BLOCKS - 1) // 2
TAIL = ET - (BLOCKS - 1) * T
GROUPS = 50
NT = GROUPS * T
NP = NT * P
NODE_TILES = -(-N // P)
FULL_GROUPS = N // (P * T)
PAIRS_N = GROUPS // 2
AW = D + 1
WINDOW = 3
TABLES = 4
CREDIT = 2
EPS = 1e-5
SIM_EPS = 1e-8


N_LOADS = 16 + 4 + T + 2 + 8 + 3 + 2
E5_STEPS = 15 + T


def gathered(i):
    return 16 * T * i


def scatters(j):
    return sum(1 for t in range((BLOCKS - 1) * T + TAIL) if t % T % TABLES == j)


def done(c, k):
    return c.sem, c.base + k + 1 + CREDIT


def reuse(c, k):
    return c.sem, c.base + k - 1 + CREDIT


def landed(c, i):
    return c.sem, c.base + 16 * (i + 2)


def landed_before(c, i):
    return c.sem, c.base + 16 * (i + 1)


def program(nc, a, out):
    with ExitStack() as ctx:
        def sb(name, shape, dt=F32):
            return ctx.enter_context(nc.sbuf_tensor(name, shape, dt))

        ring_sems, dma_rings = [], []

        def sem(name):
            return ctx.enter_context(nc.semaphore(name))

        def ring(name):
            s = sem(name)
            ring_sems.append(s)
            return s

        def dma_ring(name, n=2):
            s = [sem(f"{name}{u}") for u in range(n)]
            dma_rings.extend(s)
            return s

        def dram(name, rows=NP, width=D):
            return nc.dram_tensor(name, (rows, width), F32).ap()

        tab_a, tab_b, tab_q = dram("tab_a"), dram("tab_b"), dram("tab_q")
        tab_x1, tab_x2 = dram("tab_x1"), dram("tab_x2")
        tab_g1, tab_g2, tab_h2, tab_h3 = dram("tab_g1"), dram("tab_g2"), dram("tab_h2"), dram("tab_h3")
        tab_wh = dram("tab_wh", NP, AW)
        acc = [dram(f"acc{j}", NP + P) for j in range(TABLES)]

        def group(table, g, n=1):
            w = table.shape[1]
            return table[0:NP, :].rearrange("(g p j) d -> g p (j d)", p=P, j=T)[g]

        agg = sb("agg", [P, NT, AW])
        zeros = sb("zeros", [P, T * D // 2])
        zeros_b = sb("zeros_b", [P, NODE_TILES], BF16)
        ident = sb("ident", [P, P])
        ones = sb("ones", [P, P])
        iota_node = sb("iota_node", [P, WINDOW * P])
        iota_tile = sb("iota_tile", [P, NODE_TILES])
        tile_base = sb("tile_base", [P, NT])
        below = sb("below", [P, P])
        lane_dump = sb("lane_dump", [P, 1])
        power = sb("power", [P, 1])
        half = sb("half", [P, 1])
        block_mask = sb("block_mask", [P, T])
        src_f = sb("src_f", [P, 4, P])
        dst_f = sb("dst_f", [P, 4, P])
        rel = sb("rel", [P, 4, P])
        src_row = sb("src_row", [P, 4 * P], I32)
        dst_row = sb("dst_row", [P, 4 * P], I32)
        ew = sb("ew", [P, 4 * P])
        base = sb("base", [P, 4 * P])
        first_i = sb("first_i", [P, 4], I32)
        last_i = sb("last_i", [P, 4], I32)
        span_f = sb("span_f", [P, 4, 2])
        first_row = sb("first_row", [1, 4 * P], I32)
        xhi_row = sb("xhi_row", [1, 4 * P], I32)
        beyond_i = sb("beyond_i", [1, 4 * P // T], I32)
        deg_out = sb("deg_out", [P, NT])
        deg_in = sb("deg_in", [P, NT])
        norm_in = sb("norm_in", [P, NT])
        norm_out = sb("norm_out", [P, NT])
        w1e_nat = sb("w1e_nat", [D, T, FE])
        w2m_nat = sb("w2m_nat", [D, AW])
        wt = sb("wt", [P, 7, D])
        w_upd_agg = sb("w_upd_agg", [AW, D])
        w_pair = sb("w_pair", [P, 7, 2 * D])
        w1e_t = sb("w1e_t", [P, D])
        w1e_diag = sb("w1e_diag", [P, T, D])
        bias = sb("bias", [1, 8, D])
        bias_rows = sb("bias_rows", [P, 2, D])
        par = sb("par", [P, 8])
        par_w = sb("par_w", [P, 16])
        buf = [sb(f"buf{j}", [P, 2, T * D]) for j in range(8)]
        wide = sb("wide", [P, 2, T * P])
        wide_t = sb("wide_t", [P, 2, T * P])
        rows_u = sb("rows_u", [P, 2, T, AW])
        rows_v = sb("rows_v", [P, 2, T, AW])
        hot = sb("hot", [P, 2, WINDOW * P])
        hot_x = sb("hot_x", [P, P])
        hot_lo = sb("hot_lo", [P, 2, P], BF16)
        hot_hi = sb("hot_hi", [P, 2, NODE_TILES], BF16)
        idx_s = sb("idx_s", [P, 2, T], I32)
        idx_d = sb("idx_d", [P, 2, T], I32)
        idx_o = sb("idx_o", [P, 2, T], I32)
        edge_io = rows_v[:, :, :, :].rearrange("p u t d -> p u (t d)")
        edge_in, edge_t = edge_io[:, :, 0:T * FE], edge_io[:, :, T * FE:T * FE + P]
        small = sb("small", [P, 2, 10, T])
        four = lambda x: x.rearrange("p (b q) -> p b q", b=4)
        stage_i = [four(buf[2 + j // 2][:, j % 2, :].bitcast(I32)) for j in range(3)]
        stage_f = four(buf[3][:, 1, :])
        first_f, last_f = buf[7][:, 0, :], buf[7][:, 1, :]
        beyond_f = buf[6][0:1, 0, :]
        nat = buf[1][0:D, :, :].rearrange("p u (w k) -> p (u w) k", k=2 * D)
        rows_u_flat = rows_u[:, :, :, :].rearrange("p u t d -> p u (t d)")
        src_lo, src_hi = wide[:, 0, 0:4 * P], wide[:, 1, 0:4 * P]
        same = hot
        junk = hot_x
        ps = [ctx.enter_context(nc.psum_tensor(f"ps{j}", [P, 512], F32)) for j in range(8)]

        WA, WB, WQ, WU2, WC1, WC2, WUM = range(7)
        PA, PB, PQ, PU2, PG1, PG2, PL3 = range(7)
        B1M, B1U, B2U, BG1, BG2, BR1, BR2, BL3 = range(8)

        s_in = sem("s_in")
        s_stage_clear = sem("s_stage_clear")
        s_idx_in = sem("s_idx_in")
        s_const = sem("s_const")
        s_pool_self = sem("s_pool_self")
        s_credit = sem("s_credit")
        s_agg0 = sem("s_agg0")
        s_pe_setup = sem("s_pe_setup")
        s_dve = sem("s_dve")
        s_act_setup = sem("s_act_setup")
        s_setup_done = sem("s_setup_done")
        s_pool_hold = sem("s_pool_hold")
        s_slow_built = sem("s_slow_built")
        s_slow_mul = sem("s_slow_mul")
        s_slow_added = sem("s_slow_added")
        s_degrees = sem("s_degrees")
        s_norms = sem("s_norms")
        s_acc_zero = sem("s_acc_zero")
        s_out = sem("s_out")
        s_rest = sem("s_rest")
        s_src_staged, s_dst_staged, s_spans = sem("s_src_staged"), sem("s_dst_staged"), sem("s_spans")
        s_exp_args, s_wt = sem("s_exp_args"), sem("s_wt")
        s_slow_self = sem("s_slow_self")
        s_z_self, s_elu_self = sem("s_z_self"), sem("s_elu_self")
        s_e5 = [sem(f"s_e5_self{u}") for u in range(2)]
        s_norm_self = sem("s_norm_self")

        class Count:
            def __init__(self, sem_, base):
                self.sem, self.base = sem_, base

        totals = {}

        def counted(name, n, per=1):
            if name not in totals:
                totals[name] = [sem(name), 0]
                if "_got" not in name or name[:3] in ("edg", "row"):
                    (ring_sems if per == 1 else dma_rings).append(totals[name][0])
            c = Count(totals[name][0], totals[name][1])
            totals[name][1] += n * per
            return c

        def edge_stage(per_block, per_tile, dmas, **more):
            names = {n: counted(f"{n}_done", BLOCKS) for n in per_block.split()}
            names.update({n: counted(f"{n}_done", ET) for n in per_tile.split()})
            for n in dmas.split():
                one = n in ("edge_got", "row_got")
                names[n] = [counted(f"{n}{u}", (PAIRS_E + 1 - u) if one else
                                    PAIRS_E * T + (TAIL if u == 0 else 0), 16) for u in range(2)]
            return {**names, **more}

        def node_stage(steps, loads=0, stores=1, groups=GROUPS):
            names = {n: counted(f"{n}_done", groups) for n in steps.split()}
            names["load"] = [[counted(f"load{j}_{u}", PAIRS_N, 16) for u in range(2)] for j in range(loads)]
            names["store"] = [[counted(f"store{j}_{u}", PAIRS_N, 16) for u in range(2)] for j in range(stores)]
            return names

        LN = "s xc sq v2 v r h "
        E, NS = [None] * 6, [None] * 7
        NS[0] = node_stage(LN + "ht htc mm o o2", 1, 3)
        E[0] = edge_stage("idx edge_t edge_c z_mm z act msg consumed", "hot seg added hist_hot hist",
                          "src_got dst_got edge_got", sums_done=sem("sums_done"))
        NS[1] = node_stage(LN + "ag at atc zmm z act e1 e et etc xmm x zero", 2, 2)
        E[1] = edge_stage("idx consumed", "hot seg added", "src_got")
        NS[2] = node_stage("sc st stc mm o zero", 0, 1)
        E[2] = edge_stage("idx consumed", "hot seg added", "src_got")
        NS[3] = node_stage(LN + "sc st stc mm x zero", 1, 2)
        E[3] = edge_stage("idx consumed", "hot seg added", "src_got")
        NS[4] = node_stage("cat ct ctc mm o zero", 1, 1)
        E[4] = edge_stage("idx consumed", "hot seg added", "src_got")
        NS[5] = node_stage(LN + "cat ct ctc mm x ht htc wmm wh nrm nrm2", 2, 3)
        E[5] = edge_stage("idx contrib dedup rows_used sum oidx", "same same_used", "src_got dst_got row_got",
                          table=[sem(f"scattered{j}") for j in range(TABLES)])
        NS[6] = node_stage("sum1 sum", 1, 1, FULL_GROUPS + 1)

        def slot(b, u, width=D, at=0):
            return b[:, u, at:at + T * width].rearrange("p (t d) -> p t d", d=width)

        def over_features(v):
            return v.unsqueeze(2).to_broadcast([P, v.shape[1], D])

        def over_groups(eng, lag, body, count=GROUPS):
            def fixed(j):
                return lambda l: [((j - l) % 2, j - l, (j - l) // 2)] if 0 <= j - l < count else []

            def rolled(i, v):
                return lambda l: [((v - l) % 2, i * 2 + (v - l), i + (v - l) // 2)]

            start = lag + lag % 2
            for j in range(start):
                body(fixed(j))
            with eng.Fori(start // 2, FULL_GROUPS // 2) as i:
                for v in range(2):
                    body(rolled(i, v))
            for j in range(FULL_GROUPS, count + lag):
                body(fixed(j))

        def cols(x, b, n):
            return x[:, bass.ds(b * T, n)]

        def beyond(eng, b, step, n):
            some = eng.value_load(beyond_i[0:1, bass.ds(b, 1)], min_val=0, max_val=1)
            with eng.If(some > 0):
                for t in range(n):
                    k = b * T + t
                    lo = eng.value_load(first_row[0:1, bass.ds(k, 1)], min_val=0, max_val=NODE_TILES) + WINDOW
                    hi = eng.value_load(xhi_row[0:1, bass.ds(k, 1)], min_val=1, max_val=NODE_TILES + WINDOW + 1)
                    with eng.Fori(lo, hi) as tile:
                        step(t)(tile)

        block = ctx.enter_context(nc.Block())

        @block.sync
        def _(sp):
            sp.wait_ge(s_stage_clear, 7)
            n_load = n_rest = 0
            for j, v in enumerate((a["src"], a["dst"], a["dst"])):
                sp.dma_start(stage_i[j][:, 0:3, :],
                             v[0:3 * P * P].rearrange("(b t p) -> t b p", t=P, p=P)).then_inc(s_idx_in, 16)
                sp.dma_start(stage_i[j][0:ET - 1 - 3 * P, 3, :],
                             v[3 * P * P:(ET - 1) * P].rearrange("(t p) -> t p", p=P)).then_inc(s_idx_in, 16)
                sp.dma_start(stage_i[j][ET - 1 - 3 * P:ET - 3 * P, 3, 0:LAST],
                             v[(ET - 1) * P:EDGES].rearrange("(t p) -> t p", t=1)).then_inc(s_idx_in, 16)
            for j, v in enumerate((a["edge_weight"], a["edge_weight_n2"])):
                w = wide[:, j, 0:4 * P].rearrange("p (b q) -> p b q", b=4)
                sp.dma_start(w[:, 0:3, :],
                             v[0:3 * P * P].rearrange("(b t p) -> t b p", t=P, p=P)).then_inc(s_idx_in, 16)
                sp.dma_start(w[0:ET - 1 - 3 * P, 3, :],
                             v[3 * P * P:(ET - 1) * P].rearrange("(t p) -> t p", p=P)).then_inc(s_idx_in, 16)
                sp.dma_start(w[ET - 1 - 3 * P:ET - 3 * P, 3, 0:LAST],
                             v[(ET - 1) * P:EDGES].rearrange("(t p) -> t p", t=1)).then_inc(s_idx_in, 16)

            def load(dst, src):
                nonlocal n_load
                sp.dma_start(dst, src).then_inc(s_in, 16)
                n_load += 1

            w1m, w1u = a["L0_gnn_W1m"], a["L0_gnn_W1u"]
            for h in range(2):
                load(nat[:, WA, h * D:(h + 1) * D], w1m[:, 0:D])
                load(nat[:, WB, h * D:(h + 1) * D], w1m[:, D:2 * D])
                load(nat[:, WQ, h * D:(h + 1) * D], w1u[:, 0:D])
                load(nat[:, WU2, h * D:(h + 1) * D], a["L0_gnn_W2u"])
                load(nat[:, WUM, h * D:(h + 1) * D], w1u[:, D:2 * D])
                load(w_pair[h * D:(h + 1) * D, PG1, h * D:(h + 1) * D], a["L1_gnn_W1"])
                load(w_pair[h * D:(h + 1) * D, PG2, h * D:(h + 1) * D], a["L1_gnn_W2"])
                load(w_pair[h * D:(h + 1) * D, PL3, h * D:(h + 1) * D], a["L3_gnn_W"])
            load(nat[:, WC1, 0:D], a["L2_gnn_W_rel1"])
            load(nat[:, WC1, D:2 * D], a["L2_gnn_W_root1"])
            load(nat[:, WC2, 0:D], a["L2_gnn_W_rel2"])
            load(nat[:, WC2, D:2 * D], a["L2_gnn_W_root2"])
            for t in range(T):
                load(w1e_nat[:, t, :], w1m[:, 2 * D:2 * D + FE])
            load(w2m_nat[:, 0:D], a["L0_gnn_W2m"])
            load(w2m_nat[:, D:D + 1], a["L0_gnn_b2m"].rearrange("(p o) -> p o", o=1))
            for j, n in enumerate(("L0_gnn_b1m", "L0_gnn_b1u", "L0_gnn_b2u", "L1_gnn_b1", "L1_gnn_b2",
                                   "L2_gnn_b_rel1", "L2_gnn_b_rel2", "L3_gnn_b")):
                load(bias[0:1, j, :], a[n].rearrange("(o d) -> o d", o=1))
            for c0, n, w in ((0, "L3_gnn_deg_coeff", 2), (2, "L3_gnn_coeff_param", 3), (5, "L3_gnn_scale_param", 1)):
                load(par[:, c0:c0 + w], a[n].rearrange("(o d) -> o d", o=1).to_broadcast([P, w]))
            for j, n in enumerate(("L0_gnn_b1m", "L0_gnn_b1u")):
                load(bias_rows[:, j, :], a[n].rearrange("(o d) -> o d", o=1).to_broadcast([P, D]))
            assert n_load == N_LOADS

            def load_to(st, j, u, g, dst, table, *readers):
                for r in readers:
                    sp.wait_ge(*reuse(r, g))
                sp.dma_start(dst, group(table, g)).then_inc(st["load"][j][u].sem, 16)

            def store_from(st, j, u, g, srcb, table, writer):
                sp.wait_ge(*done(writer, g))
                sp.dma_start(group(table, g), srcb).then_inc(st["store"][j][u].sem, 16)

            x_in = a["x"]
            whole = (N - FULL_GROUPS * P * T) // P
            rest = N - FULL_GROUPS * P * T - whole * P

            def load_x(st, u, g, reader):
                nonlocal n_rest
                sp.wait_ge(*reuse(reader, g))
                to = slot(buf[0], u)
                if not isinstance(g, int) or g < FULL_GROUPS:
                    rows = x_in[bass.ds(g * (P * T), P * T), :] if not isinstance(g, int) else \
                        x_in[g * P * T:(g + 1) * P * T, :]
                    sp.dma_start(to, rows.rearrange("(t p) d -> p t d", p=P)).then_inc(st["load"][0][u].sem, 16)
                elif g == FULL_GROUPS:
                    r0 = g * P * T
                    sp.dma_start(to[0:rest, whole, :], x_in[r0 + whole * P:N, :]).then_inc(s_rest, 16)
                    n_rest += 1
                    sp.wait_ge(s_rest, 16 * n_rest)
                    sp.dma_start(to[:, 0:whole, :], x_in[r0:r0 + whole * P, :]
                                 .rearrange("(t p) d -> p t d", p=P)).then_inc(st["load"][0][u].sem, 16)
                else:
                    sp.sem_inc(st["load"][0][u].sem, 16)

            sp.wait_ge(s_credit, 1)
            sp.wait_ge(s_const, 1)
            st = NS[0]

            def node0(at):
                for u, g, i in at(0):
                    load_x(NS[0], u, g, NS[0]["xc"])
                for u, g, i in at(7):
                    store_from(NS[0], 0, u, g, buf[5][:, u, :], tab_a, NS[0]["o"])
                    store_from(NS[0], 1, u, g, buf[6][:, u, :], tab_b, NS[0]["o2"])
                    store_from(NS[0], 2, u, g, buf[7][:, u, :], tab_q, NS[0]["o2"])
            over_groups(sp, 7, node0)

            e = E[0]
            with sp.Fori(0, PAIRS_E) as i:
                for u in range(2):
                    b = i * 2 + u
                    sp.wait_ge(*reuse(e["edge_t"], b))
                    sp.dma_start(edge_in[:, u, :].rearrange("p (t f) -> p t f", f=FE),
                                 a["edge_attr_16"][bass.ds(b * (P * T), P * T), :]
                                 .rearrange("(t p) f -> p t f", p=P)).then_inc(e["edge_got"][u].sem, 16)
            b = BLOCKS - 1
            r0 = b * P * T
            sp.wait_ge(*reuse(e["edge_t"], b))
            sp.dma_start(edge_in[0:LAST, 0, (TAIL - 1) * FE:TAIL * FE],
                         a["edge_attr_16"][EDGES - LAST:EDGES, :]).then_inc(s_rest, 16)
            n_rest += 1
            sp.wait_ge(s_rest, 16 * n_rest)
            sp.dma_start(edge_in[:, 0, 0:(TAIL - 1) * FE].rearrange("p (t f) -> p t f", f=FE),
                         a["edge_attr_16"][r0:r0 + (TAIL - 1) * P, :]
                         .rearrange("(t p) f -> p t f", p=P)).then_inc(e["edge_got"][0].sem, 16)

            sp.wait_ge(*done(E[0]["z"], BLOCKS - 1))
            for u in range(2):
                sp.wait_ge(*landed_before(NS[0]["store"][2][u], PAIRS_N))

            def node1(at):
                for u, g, i in at(10):
                    store_from(NS[1], 1, u, g, wide[:, u, 512:1024], tab_g1, NS[1]["h"])
                for u, g, i in at(8):
                    store_from(NS[1], 0, u, g, buf[6][:, u, :], tab_x1, NS[1]["x"])
                for u, g, i in at(5):
                    load_x(NS[1], u, g, NS[1]["x"])
                for u, g, i in at(1):
                    load_to(NS[1], 1, u, g, buf[1][:, u, :], tab_q, NS[1]["z"])
            over_groups(sp, 10, node1)

            for j in range(TABLES):
                sp.dma_start(acc[j][NP:NP + P, :], zeros[:, 0:D]).then_inc(s_acc_zero, 16)
            for j in range(2, TABLES):
                sp.dma_start(acc[j][0:NP, :].rearrange("(p g j) d -> p g (j d)", p=P, j=T // 2),
                             zeros[:, :].unsqueeze(1).to_broadcast([P, 2 * NT // T, T * D // 2])
                             ).then_inc(s_acc_zero, 16)

            def node2(at):
                for u, g, i in at(4):
                    store_from(NS[2], 0, u, g, buf[7][:, u, :], tab_g2, NS[2]["o"])
            over_groups(sp, 4, node2)

            for u in range(2):
                sp.wait_ge(*landed_before(NS[1]["store"][0][u], PAIRS_N))

            def node3(at):
                for u, g, i in at(6):
                    store_from(NS[3], 1, u, g, buf[4][:, u, :], tab_h2, NS[3]["h"])
                for u, g, i in at(4):
                    store_from(NS[3], 0, u, g, buf[6][:, u, :], tab_x2, NS[3]["x"])
                for u, g, i in at(1):
                    load_to(NS[3], 0, u, g, buf[0][:, u, :], tab_x1, NS[3]["x"])
            over_groups(sp, 6, node3)
            for u in range(2):
                for j in range(2):
                    sp.wait_ge(*landed_before(NS[3]["store"][j][u], PAIRS_N))

            def cat_h(u):
                return wide[:, u, :].rearrange("p (t c) -> p t c", c=P)[:, :, D:P]

            def node4(at):
                for u, g, i in at(4):
                    store_from(NS[4], 0, u, g, buf[7][:, u, :], tab_h3, NS[4]["o"])
                for u, g, i in at(0):
                    load_to(NS[4], 0, u, g, cat_h(u), tab_h2, NS[4]["ct"])
            over_groups(sp, 4, node4)
            for u in range(2):
                sp.wait_ge(*landed_before(NS[4]["store"][0][u], PAIRS_N))

            def node5(at):
                for u, g, i in at(10):
                    store_from(NS[5], 0, u, g, rows_u[:, u, :, :].rearrange("p t d -> p (t d)"), tab_wh,
                               NS[5]["nrm2"])
                    store_from(NS[5], 2, u, g, buf[1][:, u, :], acc[1], NS[5]["wh"])
                for u, g, i in at(4):
                    store_from(NS[5], 1, u, g, buf[6][:, u, :], acc[0], NS[5]["x"])
                for u, g, i in at(1):
                    load_to(NS[5], 1, u, g, buf[0][:, u, :], tab_x2, NS[5]["x"])
                for u, g, i in at(0):
                    load_to(NS[5], 0, u, g, cat_h(u), tab_h3, NS[5]["ct"])
            over_groups(sp, 10, node5)

            e = E[5]

            def src_rows(b, u, n):
                sp.wait_ge(*reuse(e["rows_used"], b))
                v = a["src"][bass.ds(b * (P * T), n * P)] if n == T else a["src"][b * P * T:b * P * T + n * P]
                sp.dma_start(wide[:, u, 0:n * P].bitcast(I32),
                             v.rearrange("(o q) -> o q", o=1).to_broadcast([P, n * P])).then_inc(e["row_got"][u].sem, 16)

            with sp.Fori(0, PAIRS_E) as i:
                for u in range(2):
                    src_rows(i * 2 + u, u, T)
            b_ = BLOCKS - 1
            sp.wait_ge(*reuse(e["rows_used"], b_))
            left = EDGES - b_ * P * T
            sp.dma_start(wide[:, 0, 0:left].bitcast(I32),
                         a["src"][b_ * P * T:EDGES].rearrange("(o q) -> o q", o=1).to_broadcast([P, left])
                         ).then_inc(e["row_got"][0].sem, 16)

            for j in range(TABLES):
                sp.wait_ge(e["table"][j], 16 * scatters(j))

            def node6(at):
                for u, g, i in at(2):
                    sp.wait_ge(*done(NS[6]["sum"], g))
                    rows = slot(buf[7], u)
                    if not isinstance(g, int) or g < FULL_GROUPS:
                        to = out[bass.ds(g * (P * T), P * T), :] if not isinstance(g, int) else \
                            out[g * P * T:(g + 1) * P * T, :]
                        sp.dma_start(to.rearrange("(t p) d -> p t d", p=P), rows).then_inc(NS[6]["store"][0][u].sem, 16)
                    else:
                        r0 = g * P * T
                        sp.dma_start(out[r0:r0 + whole * P, :].rearrange("(t p) d -> p t d", p=P),
                                     rows[:, 0:whole, :]).then_inc(s_out, 16)
                        sp.dma_start(out[r0 + whole * P:N, :], rows[0:rest, whole, :]).then_inc(s_out, 16)
                for u, g, i in at(0):
                    sp.wait_ge(*reuse(NS[6]["sum"], g))
                    for j in range(TABLES):
                        sp.dma_start(buf[j][:, u, :], group(acc[j], g)).then_inc(NS[6]["load"][0][u].sem, 16)
            over_groups(sp, 2, node6, FULL_GROUPS + 1)
            sp.wait_ge(s_out, 32)
            for u in range(2):
                sp.wait_ge(*landed_before(NS[6]["store"][0][u], FULL_GROUPS // 2))

        @block.gpsimd
        def _(pool):
            count = [0]

            def hold(*waits):
                for s, v in waits:
                    pool.wait_ge(s, v)
                pool.sem_inc(s_pool_hold, 1)

            def chain(ins):
                count[0] += 1
                ins.then_inc(s_pool_self, 1)
                pool.wait_ge(s_pool_self, count[0])

            for j, v in ((0, -1), (1, -1), (2, 1 << 20)):
                pool.memset(stage_i[j][:, 3, :], v).then_inc(s_stage_clear, 1)
            pool.memset(wide[:, :, 0:4 * P], 0.0).then_inc(s_stage_clear, 1)
            for j in (0, 1):
                pool.memset(buf[j][:, :, :], 0.0).then_inc(s_stage_clear, 1)
            pool.memset(w_pair[:, :, :], 0.0).then_inc(s_stage_clear, 1)
            for s_ in ring_sems:
                pool.sem_inc(s_, CREDIT)
            for s_ in dma_rings:
                pool.sem_inc(s_, 16)
            pool.sem_inc(s_credit, 1)
            chain(pool.memset(ident[:, :], 0.0))
            chain(pool.affine_select(out=ident[:, :], in_=ident[:, :], compare_op=ALU.not_equal, fill=1.0,
                                     base=0, pattern=[[-1, P]], channel_multiplier=1))
            chain(pool.memset(below[:, :], 1.0))
            chain(pool.affine_select(out=below[:, :], in_=below[:, :], compare_op=ALU.is_gt, fill=0.0,
                                     base=0, pattern=[[-1, P]], channel_multiplier=1))
            chain(pool.memset(block_mask[:, :], 1.0))
            chain(pool.affine_select(out=block_mask[:, :], in_=block_mask[:, :], compare_op=ALU.is_ge, fill=0.0,
                                     base=0, pattern=[[-FE, T]], channel_multiplier=1))
            chain(pool.affine_select(out=block_mask[:, :], in_=block_mask[:, :], compare_op=ALU.is_ge, fill=0.0,
                                     base=FE - 1, pattern=[[FE, T]], channel_multiplier=-1))
            small_ok = dict(allow_small_or_imprecise_dtypes=True)
            chain(pool.iota(iota_node[:, :], pattern=[[1, WINDOW * P]], base=0, channel_multiplier=0, **small_ok))
            chain(pool.iota(iota_tile[:, :], pattern=[[1, NODE_TILES]], base=0, channel_multiplier=0, **small_ok))
            chain(pool.iota(tile_base[:, :], pattern=[[P, NT]], base=0, channel_multiplier=0, **small_ok))
            chain(pool.iota(lane_dump[:, :], pattern=[[0, 1]], base=NP, channel_multiplier=1, **small_ok))
            chain(pool.memset(zeros[:, :], 0.0))
            chain(pool.memset(zeros_b[:, :], 0.0))
            chain(pool.memset(ones[:, :], 1.0))
            chain(pool.memset(power[:, :], -0.5))
            chain(pool.memset(half[:, :], 0.5))
            for u in range(2):
                chain(pool.memset(rows_u[:, u, :, :], 1.0))
                chain(pool.memset(rows_v[:, u, :, :], 0.0))
            pool.sem_inc(s_const, 1)
            pool.memset(agg[:, :, :], 0.0).then_inc(s_agg0, 1)

            def ln_root(st, lag):
                def part(at):
                    for u, g, i in at(lag):
                        hold(done(st["v"], g), reuse(st["h"], g))
                        pool.tensor_tensor(small[:, u, 4, :], small[:, u, 3, :], power[:, :].to_broadcast([P, T]),
                                           ALU.pow).then_inc(st["r"].sem, 1)
                return part

            def clear_sums(st, used, lag):
                def part(at):
                    for u, g, i in at(lag):
                        hold(done(used, g))
                        pool.tensor_copy(agg[:, bass.ds(g * T, T), :],
                                         zeros[:, 0:AW].unsqueeze(1).to_broadcast([P, T, AW])
                                         ).then_inc(st["zero"].sem, 1)
                return part

            def gathers(k, table, b, u, n, to, got, idx, width=D):
                for t in range(n):
                    pool.indirect_dma_start(
                        out=to[:, u, t, 0:width] if len(to.shape) == 4 else to[:, u, t * width:(t + 1) * width],
                        out_offset=None, in_=table[:, :],
                        in_offset=bass.IndirectOffsetOnAxis(ap=idx[:, u, t:t + 1], axis=0),
                        bounds_check=NP - 1, oob_is_err=False).then_inc(got[u].sem, 16)

            def over_blocks(body):
                with pool.Fori(0, PAIRS_E) as i:
                    for u in range(2):
                        body(i * 2 + u, u, T)
                body(BLOCKS - 1, 0, TAIL)

            def table_stored(st, j):
                for u in range(2):
                    pool.wait_ge(*landed_before(st["store"][j][u], PAIRS_N))

            over_groups(pool, 1, ln_root(NS[0], 1))
            table_stored(NS[0], 0)
            table_stored(NS[0], 1)

            def edge0(b, u, n):
                e = E[0]
                hold(done(e["idx"], b), reuse(e["z"], b))
                gathers(0, tab_a, b, u, n, buf[0], e["src_got"], idx_s)
                gathers(0, tab_b, b, u, n, buf[1], e["dst_got"], idx_d)

            over_blocks(edge0)
            pool.wait_ge(s_degrees, 2)
            pool.tensor_tensor(norm_out[:, :], deg_out[:, :], power[:, :].to_broadcast([P, NT]),
                               ALU.pow).then_inc(s_norms, 1)
            pool.tensor_tensor(norm_in[:, :], deg_in[:, :], power[:, :].to_broadcast([P, NT]),
                               ALU.pow).then_inc(s_norms, 1)
            root1, clear1 = ln_root(NS[1], 8), clear_sums(NS[1], NS[1]["ag"], 1)

            def node1(at):
                root1(at)
                clear1(at)
            over_groups(pool, 8, node1)

            def plain_gather(k, table):
                def body(b, u, n):
                    kb = b
                    hold(done(E[k]["idx"], kb), reuse(E[k]["consumed"], kb))
                    gathers(k, table, b, u, n, rows_u, E[k]["src_got"], idx_s)
                over_blocks(body)

            table_stored(NS[1], 1)
            plain_gather(1, tab_g1)
            over_groups(pool, 1, clear_sums(NS[2], NS[2]["sc"], 1))
            table_stored(NS[2], 0)
            plain_gather(2, tab_g2)
            root3, clear3 = ln_root(NS[3], 4), clear_sums(NS[3], NS[3]["sc"], 1)

            def node3(at):
                root3(at)
                clear3(at)
            over_groups(pool, 4, node3)
            table_stored(NS[3], 1)
            plain_gather(3, tab_h2)
            over_groups(pool, 1, clear_sums(NS[4], NS[4]["cat"], 1))
            table_stored(NS[4], 0)
            plain_gather(4, tab_h3)
            root5 = ln_root(NS[5], 4)

            def node5(at):
                for u, g, i in at(9):
                    hold(done(NS[5]["nrm"], g), landed_before(NS[5]["store"][0][u], i))
                    pool.tensor_tensor(rows_u[:, u, :, D:AW], small[:, u, 5, :].unsqueeze(2),
                                       half[:, :].to_broadcast([P, T]).unsqueeze(2), ALU.pow
                                       ).then_inc(NS[5]["nrm2"].sem, 1)
                root5(at)
            over_groups(pool, 9, node5)
            table_stored(NS[5], 0)
            table_stored(NS[5], 1)
            table_stored(NS[5], 2)
            pool.wait_ge(s_acc_zero, 16 * (2 * TABLES - 2))

            e = E[5]

            def pull(b, u, n):
                hold(done(e["idx"], b), reuse(e["contrib"], b))
                gathers(5, tab_wh, b, u, n, rows_u, e["src_got"], idx_s, AW)
                gathers(5, tab_wh, b, u, n, rows_v, e["dst_got"], idx_d, AW)

            def push(b, u, n):
                hold(done(e["oidx"], b), done(e["sum"], b))
                for t in range(n):
                    j = t % TABLES
                    if not (isinstance(b, int) and b == 0 and t < TABLES):
                        hold((e["table"][j], 16 * (b * (T // TABLES) + t // TABLES)))
                    pool.indirect_dma_start(
                        out=acc[j][:, :], out_offset=bass.IndirectOffsetOnAxis(ap=idx_o[:, u, t:t + 1], axis=0),
                        in_=buf[5][:, u, t * D:(t + 1) * D], in_offset=None,
                        bounds_check=NP + P - 1, oob_is_err=True, compute_op=ALU.add).then_inc(e["table"][j], 16)

            pull(0, 0, T)
            pull(1, 1, T)
            for b in range(2):
                push(b, b, T)
                pull(b + 2, b, T)
            with pool.Fori(1, PAIRS_E - 1) as i:
                for u in range(2):
                    push(i * 2 + u, u, T)
                    pull(i * 2 + u + 2, u, T)
            push(BLOCKS - 3, 0, T)
            pull(BLOCKS - 1, 0, TAIL)
            push(BLOCKS - 2, 1, T)
            push(BLOCKS - 1, 0, TAIL)

        @block.scalar
        def _(act):
            act.wait_ge(s_credit, 1)

            def copy(o, i):
                return act.activation(o, i, ACT.Copy)

            def ln_square(st, lag, xc, sq):
                def part(at):
                    for u, g, i in at(lag):
                        act.wait_ge(*done(st["xc"], g))
                        act.wait_ge(*reuse(st["v2"], g))
                        act.activation(slot(sq, u), slot(xc, u), ACT.Square).then_inc(st["sq"].sem, 1)
                return part

            act.wait_ge(s_exp_args, 1)
            act.activation(par_w[:, 2:5], par_w[:, 8:11], ACT.Exp).then_inc(s_act_setup, 1)
            act.activation(par_w[:, 5:6], par_w[:, 11:12], ACT.Exp).then_inc(s_act_setup, 1)
            act.activation(buf[4][:, 1, :], buf[4][:, 0, :], ACT.Exp).then_inc(s_act_setup, 1)
            act.wait_ge(s_act_setup, 3)
            act.activation(par_w[:, 6:7], par_w[:, 5:6], ACT.Ln, bias=1.0).then_inc(s_act_setup, 1)
            act.activation(buf[5][:, 0, :], buf[4][:, 1, :], ACT.Ln, bias=1.0).then_inc(s_act_setup, 1)

            act.wait_ge(s_setup_done, 1)
            square0 = ln_square(NS[0], 0, buf[2], buf[3])

            def node0(at):
                st = NS[0]
                for u, g, i in at(4):
                    act.wait_ge(*done(st["ht"], g))
                    act.wait_ge(*reuse(st["mm"], g))
                    copy(wide_t[:, u, 0:512], ps[u][:, :]).then_inc(st["htc"].sem, 1)
                for u, g, i in at(5):
                    act.wait_ge(*done(st["mm"], g))
                    act.wait_ge(*landed_before(st["store"][0][u], i))
                    copy(buf[5][:, u, :], ps[2 + u][:, :]).then_inc(st["o"].sem, 1)
                square0(at)
            over_groups(act, 5, node0)

            def copy_indices(k, used, both=False):
                e = E[k]

                def body(b, i, u, n):
                    act.wait_ge(*reuse(used, b))
                    if both:
                        copy(idx_d[:, u, 0:n], cols(dst_row, b, n))
                    copy(idx_s[:, u, 0:n], cols(src_row, b, n)).then_inc(e["idx"].sem, 1)
                return body

            def over_blocks(body):
                with act.Fori(0, PAIRS_E) as i:
                    for u in range(2):
                        body(i * 2 + u, i, u, T)
                body(BLOCKS - 1, PAIRS_E, 0, TAIL)

            e = E[0]
            copy0 = copy_indices(0, e["z"], True)

            def edge0(b, i, u, n):
                if n == T:
                    copy0(b + 1, i + u, 1 - u, T)
                act.wait_ge(*done(e["edge_t"], b))
                act.wait_ge(*reuse(e["z_mm"], b))
                copy(edge_t[:, u, :], ps[5][:, 0:P]).then_inc(e["edge_c"].sem, 1)
                act.wait_ge(*done(e["z"], b))
                act.wait_ge(*reuse(e["msg"], b))
                w = n * D
                act.activation(buf[3][:, u, 0:w], buf[2][:, u, 0:w], ACT.Exp)
                act.activation(buf[4][:, u, 0:w], buf[2][:, u, 0:w], ACT.Relu).then_inc(e["act"].sem, 1)

            copy0(0, 0, 0, T)
            over_blocks(edge0)

            act.wait_ge(E[0]["sums_done"], 1)
            square1 = ln_square(NS[1], 7, buf[7], rows_u_flat)

            def node1(at):
                st = NS[1]
                square1(at)
                for u, g, i in at(6):
                    act.wait_ge(*done(st["et"], g))
                    act.wait_ge(*reuse(st["xmm"], g))
                    copy(wide[:, u, 0:512], ps[5][:, :]).then_inc(st["etc"].sem, 1)
                for u, g, i in at(3):
                    act.wait_ge(*done(st["z"], g))
                    act.wait_ge(*reuse(st["e"], g))
                    act.activation(buf[3][:, u, :], buf[2][:, u, :], ACT.Exp)
                    act.activation(buf[4][:, u, :], buf[2][:, u, :], ACT.Relu).then_inc(st["act"].sem, 1)
                for u, g, i in at(2):
                    act.wait_ge(*done(st["at"], g))
                    act.wait_ge(*reuse(st["zmm"], g))
                    copy(wide_t[0:AW, u, 0:512], ps[u][0:AW, :])
                    copy(wide_t[0:AW, u, 512:1024], ps[2 + u][0:AW, :]).then_inc(st["atc"].sem, 1)
                for u, g, i in at(0):
                    act.wait_ge(*reuse(st["at"], g))
                    copy(rows_v[:, u, :, :], agg[:, bass.ds(g * T, T), :]).then_inc(st["ag"].sem, 1)
            over_groups(act, 7, node1)

            over_blocks(copy_indices(1, E[1]["consumed"]))
            def evac_paired(st, lag):
                def part(at):
                    for u, g, i in at(lag):
                        act.wait_ge(*done(st["st"], g))
                        act.wait_ge(*reuse(st["mm"], g))
                        copy(wide_t[:, u, 0:512], ps[u][:, :]).then_inc(st["stc"].sem, 1)
                return part

            over_groups(act, 2, evac_paired(NS[2], 2))
            over_blocks(copy_indices(2, E[2]["consumed"]))
            square3, evac3 = ln_square(NS[3], 3, buf[7], buf[3]), evac_paired(NS[3], 2)

            def node3(at):
                square3(at)
                evac3(at)
            over_groups(act, 3, node3)
            over_blocks(copy_indices(3, E[3]["consumed"]))

            def evac_cat(st, lag):
                def part(at):
                    for u, g, i in at(lag):
                        act.wait_ge(*done(st["ct"], g))
                        act.wait_ge(*reuse(st["mm"], g))
                        copy(wide_t[:, u, 0:512], ps[u][:, :])
                        copy(wide_t[:, u, 512:1024], ps[2 + u][:, :]).then_inc(st["ctc"].sem, 1)
                return part

            over_groups(act, 2, evac_cat(NS[4], 2))
            over_blocks(copy_indices(4, E[4]["consumed"]))
            square5, evac5 = ln_square(NS[5], 3, buf[7], buf[3]), evac_cat(NS[5], 2)

            def node5(at):
                st = NS[5]
                for u, g, i in at(8):
                    act.wait_ge(*done(st["wmm"], g))
                    act.wait_ge(*reuse(st["nrm"], g))
                    act.wait_ge(*landed_before(st["store"][0][u], i))
                    act.wait_ge(*landed_before(st["store"][2][u], i))
                    act.activation(buf[5][:, u, :], ps[7][:, :], ACT.Square)
                    act.activation(buf[1][:, u, :], ps[7][:, :], ACT.Copy, scale=par_w[:, 10:11])
                    copy(rows_u[:, u, :, 0:D], ps[7][:, :].rearrange("p (t d) -> p t d", d=D)
                         ).then_inc(st["wh"].sem, 1)
                for u, g, i in at(7):
                    act.wait_ge(*done(st["ht"], g))
                    act.wait_ge(*reuse(st["wmm"], g))
                    copy(buf[2][:, u, :], ps[6][:, :]).then_inc(st["htc"].sem, 1)
                square5(at)
                evac5(at)
            over_groups(act, 8, node5)

            e = E[5]
            copy5 = copy_indices(5, e["contrib"], True)

            def edge5(b, i, u, n):
                copy5(b, i, u, n)

            def edge5_out(b, u, n):
                act.wait_ge(*done(e["dedup"], b))
                for j in range(TABLES):
                    act.wait_ge(e["table"][j], 16 * (b * (T // TABLES) - T // TABLES))
                copy(buf[5][:, u, 0:n * D], ps[u][:, 0:n * D]).then_inc(e["sum"].sem, 1)

            edge5(0, 0, 0, T)
            edge5(1, 0, 1, T)
            for b in range(2):
                act.wait_ge(*done(e["dedup"], b))
                copy(buf[5][:, b, :], ps[b][:, :]).then_inc(e["sum"].sem, 1)
                edge5(b + 2, 1, b, T)
            with act.Fori(1, PAIRS_E - 1) as i:
                for u in range(2):
                    edge5_out(i * 2 + u, u, T)
                    edge5(i * 2 + u + 2, i + 1, u, T)
            edge5_out(BLOCKS - 3, 0, T)
            edge5(BLOCKS - 1, PAIRS_E, 0, TAIL)
            edge5_out(BLOCKS - 2, 1, T)
            edge5_out(BLOCKS - 1, 0, TAIL)

        @block.tensor
        def _(pe):
            def pair(i):
                return [(u, i * 2 + u) for u in range(2)]

            pe.wait_ge(s_const, 1)
            for j in range(4):
                pe.wait_ge((s_src_staged, s_dst_staged)[min(j, 1)], 1)
                w = stage_f if j < 2 else wide[:, j - 2, 0:512].rearrange("p (b q) -> p b q", b=4)
                for q in range(4):
                    m = pe.transpose(ps[j][:, q * P:(q + 1) * P], w[:, q, :], ident[:, :])
                m.then_inc(s_pe_setup, 1)
            for j in range(2):
                pe.wait_ge(s_spans, j + 1)
                w = wide_t[:, j, 0:512].rearrange("p (b q) -> p b q", b=4)
                for q in range(4):
                    m = pe.matmul(ps[4 + j][:, q * P:(q + 1) * P], w[:, q, :], ident[:, :], start=True, stop=True)
                m.then_inc(s_pe_setup, 1)
            pe.wait_ge(s_in, 16 * N_LOADS)
            for q in range(4):
                m = pe.transpose(ps[6][:, q * D:(q + 1) * D], nat[:, q, :], ident[0:D, 0:D])
            for q in range(4, 7):
                m = pe.transpose(ps[6][:, q * D:(q + 1) * D], nat[:, q, :], ident[0:D, 0:D])
            m.then_inc(s_pe_setup, 1)
            pe.transpose(ps[7][:, 0:D], w1e_nat[:, :, :].rearrange("p t f -> p (t f)"), ident[0:D, 0:D]
                         ).then_inc(s_pe_setup, 1)
            pe.wait_ge(s_wt, 1)
            pe.matmul(ps[7][0:AW, D:2 * D], w2m_nat[:, :], wt[0:D, WUM, :], start=True, stop=True
                      ).then_inc(s_pe_setup, 1)

            def add_bias(o, row, n=T):
                pe.matmul(o[:, 0:n * D], ones[0:1, :], bias[0:1, row:row + 1, :].to_broadcast([1, n, D]),
                          start=True, stop=False, skip_group_check=True)

            def products_paired(o, lhs, w, row=None):
                if row is not None:
                    add_bias(o, row)
                for q in range(T // 2):
                    m = pe.matmul(o[:, q * P:(q + 1) * P], lhs[:, q * P:(q + 1) * P], w,
                                  start=row is None, stop=True, skip_group_check=True)
                return m

            def products(o, lhs, k, w, row=None):
                if row is not None:
                    add_bias(o, row)
                for t in range(T):
                    m = pe.matmul(o[:, t * D:(t + 1) * D], lhs[0:k, t * P:(t + 1) * P], w,
                                  start=row is None, stop=True, skip_group_check=True)
                return m

            def transposes_paired(o, x):
                for q in range(T // 2):
                    m = pe.transpose(o[:, q * P:(q + 1) * P], x[:, q * P:(q + 1) * P], ident[:, :])
                return m

            pe.wait_ge(s_setup_done, 1)
            def node0(at):
                st = NS[0]
                for u, g, i in at(3):
                    pe.wait_ge(*done(st["h"], g))
                    pe.wait_ge(*reuse(st["htc"], g))
                    transposes_paired(ps[u], buf[4][:, u, :]).then_inc(st["ht"].sem, 1)
                for u, g, i in at(4):
                    pe.wait_ge(*done(st["htc"], g))
                    pe.wait_ge(*reuse(st["o"], g))
                    pe.wait_ge(*reuse(st["o2"], g))
                    products_paired(ps[2 + u], wide_t[:, u, 0:512], w_pair[:, PA, :])
                    products_paired(ps[4 + u], wide_t[:, u, 0:512], w_pair[:, PB, :])
                    products_paired(ps[6 + u], wide_t[:, u, 0:512], w_pair[:, PQ, :]).then_inc(st["mm"].sem, 1)
            over_groups(pe, 4, node0)

            slow = pe.alloc_register("slow_pe")
            pe.reg_mov(slow, 0)

            def segment(k, msg, width, weights=False):
                e = E[k]

                def body(b, u, n, tile_hook=None):
                    for t in range(n):
                        k_ = b * T + t
                        kt = k_
                        pe.wait_ge(*done(e["hot"], kt))
                        pe.wait_ge(*reuse(e["added"], kt))
                        for w in range(WINDOW):
                            m = pe.matmul(ps[t % 2][:, w * AW:w * AW + width],
                                          hot[:, t % 2, w * P:(w + 1) * P], msg[:, u, t, 0:width],
                                          start=True, stop=True)
                        m.then_inc(e["seg"].sem, 1)
                        if tile_hook:
                            tile_hook(k_, t)
                    beyond(pe, b, lambda t: slow_step(msg, u, t, width), n)
                return body

            def slow_step(msg, u, t, width):
                def step(tile):
                    pe.reg_add(slow, slow, 1)
                    pe.wait_ge(s_slow_built, slow)
                    pe.matmul(ps[2][:, 0:width], hot_x[:, :], msg[:, u, t, 0:width], start=True, stop=True
                              ).then_inc(s_slow_mul, 1)
                return step

            def over_blocks(body):
                with pe.Fori(0, PAIRS_E) as i:
                    for u in range(2):
                        body(i * 2 + u, i, u, T)
                body(BLOCKS - 1, PAIRS_E, 0, TAIL)

            e = E[0]
            seg0 = segment(0, rows_u, AW)
            pe.wait_ge(*done(NS[0]["o"], GROUPS - 1))
            pe.wait_ge(*done(NS[0]["o2"], GROUPS - 1))
            pe.matmul(ps[6][:, 0:NODE_TILES], zeros_b[:, 0:P], zeros_b[:, 0:NODE_TILES],
                      start=True, stop=False, skip_group_check=True)

            def hist(k_, t):
                pe.wait_ge(*done(e["hist_hot"], k_))
                pe.matmul(ps[6][:, 0:NODE_TILES], hot_lo[:, t % 2, :], hot_hi[:, t % 2, :],
                          start=False, stop=False, skip_group_check=True).then_inc(e["hist"].sem, 1)

            def edge0(b, i, u, n):
                pe.wait_ge(*landed(e["edge_got"][u], i))
                pe.wait_ge(*done(e["edge_c"], b - 1))
                pe.transpose(ps[5][:, 0:P], edge_in[:, u, :], ident[:, :]).then_inc(e["edge_t"].sem, 1)
                pe.wait_ge(*done(e["edge_c"], b))
                pe.wait_ge(*reuse(e["z"], b))
                pe.matmul(ps[3 + u][:, 0:n * D], edge_t[:, u, :],
                          w1e_diag[:, 0:n, :].rearrange("p t d -> p (t d)"), start=True, stop=True
                          ).then_inc(e["z_mm"].sem, 1)
                pe.wait_ge(*done(e["msg"], b))
                seg0(b, u, n, hist)

            over_blocks(edge0)
            pe.matmul(ps[6][:, 0:NODE_TILES], zeros_b[:, 0:P], zeros_b[:, 0:NODE_TILES],
                      start=False, stop=True, skip_group_check=True).then_inc(e["hist"].sem, 1)

            def node1(at):
                st = NS[1]
                for u, g, i in at(6):
                    pe.wait_ge(*done(st["etc"], g))
                    pe.wait_ge(*reuse(st["x"], g))
                    products_paired(ps[6 + u], wide[:, u, 0:512], w_pair[:, PU2, :], B2U).then_inc(st["xmm"].sem, 1)
                for u, g, i in at(5):
                    pe.wait_ge(*done(st["e"], g))
                    pe.wait_ge(*done(st["etc"], g - 1))
                    transposes_paired(ps[5], buf[5][:, u, :]).then_inc(st["et"].sem, 1)
                for u, g, i in at(2):
                    pe.wait_ge(*done(st["atc"], g))
                    pe.wait_ge(*done(st["z"], g - 1))
                    products(ps[4], wide_t[:, u, :], AW, w_upd_agg[:, :]).then_inc(st["zmm"].sem, 1)
                for u, g, i in at(1):
                    pe.wait_ge(*done(st["ag"], g))
                    pe.wait_ge(*reuse(st["atc"], g))
                    for t in range(T):
                        m = pe.transpose(ps[(t // 4) * 2 + u][0:AW, (t % 4) * P:(t % 4 + 1) * P],
                                         rows_v[:, u, t, :], ident[:, :])
                    m.then_inc(st["at"].sem, 1)
            over_groups(pe, 6, node1)

            def plain_segment(k):
                seg = segment(k, rows_u, D)

                def body(b, i, u, n):
                    pe.wait_ge(E[k]["src_got"][u].sem, E[k]["src_got"][u].base + gathered(i) + 16 * n)
                    seg(b, u, n)
                over_blocks(body)

            def graph_conv(st, row, w, used):
                def part(at):
                    for u, g, i in at(2):
                        pe.wait_ge(*done(st["stc"], g))
                        pe.wait_ge(*reuse(used, g))
                        products_paired(ps[4 + u], wide_t[:, u, 0:512], w_pair[:, w, :], row
                                        ).then_inc(st["mm"].sem, 1)
                    for u, g, i in at(1):
                        pe.wait_ge(*done(st["sc"], g))
                        pe.wait_ge(*reuse(st["stc"], g))
                        transposes_paired(ps[u], buf[5][:, u, :]).then_inc(st["st"].sem, 1)
                over_groups(pe, 2, part)

            plain_segment(1)
            graph_conv(NS[2], BG1, PG1, NS[2]["o"])
            plain_segment(2)
            graph_conv(NS[3], BG2, PG2, NS[3]["x"])
            plain_segment(3)

            def conv_cat(st, w, row, used):
                def part(at):
                    for u, g, i in at(2):
                        pe.wait_ge(*done(st["ctc"], g))
                        pe.wait_ge(*reuse(used, g))
                        products(ps[4 + u], wide_t[:, u, :], P, wt[:, w, :], row).then_inc(st["mm"].sem, 1)
                    for u, g, i in at(1):
                        pe.wait_ge(*done(st["cat"], g))
                        pe.wait_ge(*landed(st["load"][0][u], i))
                        pe.wait_ge(*reuse(st["ctc"], g))
                        for t in range(T):
                            m = pe.transpose(ps[(t // 4) * 2 + u][:, (t % 4) * P:(t % 4 + 1) * P],
                                             wide[:, u, t * P:(t + 1) * P], ident[:, :])
                        m.then_inc(st["ct"].sem, 1)
                return part

            over_groups(pe, 2, conv_cat(NS[4], WC1, BR1, NS[4]["o"]))
            plain_segment(4)
            conv5 = conv_cat(NS[5], WC2, BR2, NS[5]["x"])

            def node5(at):
                st = NS[5]
                for u, g, i in at(7):
                    pe.wait_ge(*done(st["htc"], g))
                    pe.wait_ge(*done(st["wh"], g - 1))
                    products_paired(ps[7], buf[2][:, u, :], w_pair[:, PL3, :], BL3).then_inc(st["wmm"].sem, 1)
                for u, g, i in at(6):
                    pe.wait_ge(*done(st["h"], g))
                    pe.wait_ge(*done(st["htc"], g - 1))
                    transposes_paired(ps[6], buf[4][:, u, :]).then_inc(st["ht"].sem, 1)
                conv5(at)
            over_groups(pe, 7, node5)

            e = E[5]

            def edge5(b, i, u, n):
                pe.wait_ge(*reuse(e["sum"], b))
                for t in range(n):
                    pe.wait_ge(*done(e["same"], b * T + t))
                    m = pe.matmul(ps[u][:, t * D:(t + 1) * D], same[:, t % 2, 0:P], buf[4][:, u, t * D:(t + 1) * D],
                                  start=True, stop=True)
                    m.then_inc(e["same_used"].sem, 1)
                pe.wait_ge(*done(e["same_used"], b * T + n - 1))
                pe.sem_inc(e["dedup"].sem, 1)
            over_blocks(edge5)

        @block.vector
        def _(dve):
            count = [0]

            def link(ins, wait=True):
                count[0] += 1
                ins.then_inc(s_dve, 1)
                if wait:
                    dve.wait_ge(s_dve, count[0])
                return count[0]

            def pair(i):
                return [(u, i * 2 + u) for u in range(2)]

            V = nc.vector
            dve.wait_ge(s_credit, 1)
            dve.wait_ge(s_const, 1)
            dve.wait_ge(s_idx_in, 16 * 15)
            link(V.tensor_copy(stage_f[:, :, :], stage_i[0][:, :, :]))
            dve.sem_inc(s_src_staged, 1)
            dve.wait_ge(s_pe_setup, 1)
            link(V.tensor_copy(src_f[:, :, :], ps[0][:, :].rearrange("p (b q) -> p b q", b=4)))
            link(V.tensor_copy(stage_f[:, :, :], stage_i[1][:, :, :]))
            dve.sem_inc(s_dst_staged, 1)
            dve.wait_ge(s_pe_setup, 2)
            link(V.tensor_copy(dst_f[:, :, :], ps[1][:, :].rearrange("p (b q) -> p b q", b=4)))
            dve.wait_ge(s_pe_setup, 4)
            link(V.tensor_copy(ew[:, :], ps[2][:, :]))
            link(V.tensor_copy(buf[5][:, 1, :], ps[3][:, :]))
            link(V.tensor_reduce(first_i[:, :], stage_i[2][:, :, :], AX_X, ALU.min))
            link(V.tensor_reduce(last_i[:, :], stage_i[1][:, :, :], AX_X, ALU.max))
            link(V.tensor_scalar(first_i[:, :], first_i[:, :], float(N - 1), None, ALU.min))
            link(V.tensor_scalar(last_i[:, :], last_i[:, :], 0.0, None, ALU.max))
            for k_, x in enumerate((first_i, last_i)):
                link(V.tensor_scalar(x[:, :], x[:, :], 7, None, ALU.arith_shift_right))
                link(V.tensor_copy(span_f[:, :, k_], x[:, :]))
                w = wide_t[:, k_, 0:512].rearrange("p (b q) -> p b q", b=4)
                for q in range(4):
                    link(V.tensor_scalar(w[:, q, :], ones[:, :], span_f[:, q, k_:k_ + 1], None, ALU.mult))
                dve.sem_inc(s_spans, 1)
            dve.wait_ge(s_pe_setup, 6)
            link(V.tensor_copy(first_f[:, :], ps[4][:, :]))
            link(V.tensor_copy(last_f[:, :], ps[5][:, :]))
            link(V.tensor_copy(first_row[:, :], first_f[0:1, :]))
            link(V.scalar_tensor_tensor(out=rel[:, :, :].rearrange("p b q -> p (b q)"), in0=first_f[:, :],
                                        scalar=float(-P), in1=dst_f[:, :, :].rearrange("p b q -> p (b q)"),
                                        op0=ALU.mult, op1=ALU.add))
            link(V.tensor_scalar(beyond_f[:, :], first_f[0:1, :], float(WINDOW + 1), None, ALU.add))
            link(V.tensor_scalar(last_f[0:1, :], last_f[0:1, :], 1.0, None, ALU.add))
            link(V.tensor_tensor(xhi_row[:, :], beyond_f[:, :], last_f[0:1, :], ALU.max))
            link(V.tensor_tensor(beyond_f[:, :], last_f[0:1, :], beyond_f[:, :], ALU.is_ge))
            link(V.tensor_reduce(beyond_i[:, :], beyond_f[:, :].rearrange("o (b t) -> o b t", t=T), AX_X, ALU.max))
            ia, ib = stage_i[0][:, :, :].rearrange("p b q -> p (b q)"), stage_i[1][:, :, :].rearrange("p b q -> p (b q)")
            ic = stage_i[2][:, :, :].rearrange("p b q -> p (b q)")
            for x, row in ((src_f, src_row), (dst_f, dst_row)):
                xf = x[:, :, :].rearrange("p b q -> p (b q)")
                link(V.tensor_scalar(ia, xf, 0.0, None, ALU.max))
                link(V.tensor_scalar(ib, ia, P - 1, 3, ALU.bitwise_and, ALU.logical_shift_left))
                link(V.tensor_scalar(ic, ia, 7, T - 1, ALU.arith_shift_right, ALU.bitwise_and))
                link(V.tensor_tensor(ib, ib, ic, ALU.add))
                link(V.tensor_scalar(ic, ia, 10, None, ALU.arith_shift_right))
                link(V.tensor_scalar(ic, ic, P * T, None, ALU.mult))
                link(V.tensor_tensor(row[:, :], ib, ic, ALU.add))
            link(V.tensor_copy(ia, src_f[:, :, :].rearrange("p b q -> p (b q)")))
            link(V.tensor_scalar(ib, ia, P - 1, None, ALU.bitwise_and))
            link(V.tensor_copy(src_lo[:, :], ib))
            link(V.tensor_scalar(ib, ia, 7, None, ALU.arith_shift_right))
            link(V.tensor_copy(src_hi[:, :], ib))
            sf = src_f[:, :, :].rearrange("p b q -> p (b q)")
            dve.wait_ge(s_in, 16 * N_LOADS)
            link(V.tensor_reduce(par_w[:, 0:1], par[:, 2:5], AX_X, ALU.max))
            link(V.tensor_scalar(par_w[:, 8:11], par[:, 2:5], par_w[:, 0:1], None, ALU.subtract))
            link(V.tensor_scalar(par_w[:, 12:13], par[:, 5:6], -1.0, None, ALU.mult))
            link(V.tensor_tensor(par_w[:, 11:12], par_w[:, 12:13], par[:, 5:6], ALU.min))
            link(V.tensor_scalar(par_w[:, 13:14], par[:, 5:6], 0.0, None, ALU.max))
            link(V.tensor_scalar(buf[6][:, 0, :], buf[5][:, 1, :], par[:, 0:1], par[:, 1:2], ALU.mult, ALU.add))
            link(V.tensor_scalar(buf[6][:, 1, :], buf[6][:, 0, :], -1.0, None, ALU.mult))
            link(V.tensor_tensor(buf[4][:, 0, :], buf[6][:, 0, :], buf[6][:, 1, :], ALU.min))
            dve.sem_inc(s_exp_args, 1)
            dve.wait_ge(s_act_setup, 5)
            link(V.scalar_tensor_tensor(out=base[:, :], in0=buf[6][:, 0, :], scalar=0.0, in1=buf[5][:, 0, :],
                                        op0=ALU.max, op1=ALU.add))
            link(V.tensor_tensor(base[:, :], base[:, :], ew[:, :], ALU.mult))
            link(V.tensor_tensor(buf[6][:, 0, :], sf, dst_f[:, :, :].rearrange("p b q -> p (b q)"), ALU.not_equal))
            link(V.tensor_tensor(base[:, :], base[:, :], buf[6][:, 0, :], ALU.mult))
            link(V.tensor_reduce(par_w[:, 0:1], par_w[:, 2:5], AX_X, ALU.add))
            link(V.reciprocal(par_w[:, 1:2], par_w[:, 0:1]))
            link(V.tensor_tensor(par_w[:, 7:8], par_w[:, 6:7], par_w[:, 13:14], ALU.add))
            link(V.tensor_tensor(par_w[:, 1:2], par_w[:, 1:2], par_w[:, 7:8], ALU.mult))
            link(V.tensor_scalar(par_w[:, 8:11], par_w[:, 2:5], par_w[:, 1:2], None, ALU.mult))
            dve.wait_ge(s_pe_setup, 8)
            link(V.tensor_copy(wt[:, :, :], ps[6][:, 0:7 * D].rearrange("p (w d) -> p w d", d=D)))
            for h in range(2):
                r = slice(h * D, (h + 1) * D)
                link(V.tensor_copy(w_pair[r, PA:PU2 + 1, r], wt[r, WA:WU2 + 1, :]))
            link(V.tensor_copy(w1e_t[:, :], ps[7][:, 0:D]))
            dve.sem_inc(s_wt, 1)
            for t in range(T):
                link(V.tensor_scalar(w1e_diag[:, t, :], w1e_t[:, :], block_mask[:, t:t + 1], None, ALU.mult))
            dve.wait_ge(s_pe_setup, 9)
            link(V.tensor_copy(w_upd_agg[:, :], ps[7][0:AW, D:2 * D]))
            link(V.memset(deg_out[:, :], 1.0))
            dve.sem_inc(s_setup_done, 1)

            def ln_centre(st, lag, x, xc, ready=None):
                def part(at):
                    for u, g, i in at(lag):
                        if ready:
                            ready(u, g, i)
                        V.tensor_reduce(small[:, u, 0, :], slot(x, u), AX_X, ALU.add).then_inc(st["s"].sem, 1)
                        dve.wait_ge(*done(st["s"], g))
                        dve.wait_ge(*reuse(st["sq"], g))
                        V.scalar_tensor_tensor(out=slot(xc, u), in0=slot(x, u), scalar=float(D),
                                               in1=over_features(small[:, u, 0, :]), op0=ALU.mult,
                                               op1=ALU.subtract).then_inc(st["xc"].sem, 1)
                return part

            def ln_var(st, lag, sq, norm=False):
                def part(at):
                    for u, g, i in at(lag):
                        dve.wait_ge(*done(st["sq"], g))
                        V.tensor_reduce(small[:, u, 6, :], slot(sq, u), AX_X, ALU.add).then_inc(st["v2"].sem, 1)
                        dve.wait_ge(*done(st["v2"], g))
                        dve.wait_ge(*reuse(st["r"], g))
                        if not norm:
                            V.tensor_scalar(small[:, u, 3, :], small[:, u, 6, :], 1.0 / D, D * D * EPS,
                                            ALU.mult, ALU.add).then_inc(st["v"].sem, 1)
                        else:
                            V.tensor_scalar(small[:, u, 2, :], small[:, u, 6, :], 1.0 / D, D * D * EPS,
                                            ALU.mult, ALU.add).then_inc(s_norm_self, 1)
                            dve.wait_ge(s_norm_self, g + 1)
                            V.tensor_tensor(small[:, u, 3, :], small[:, u, 2, :], cols(deg_out, g, T), ALU.mult
                                            ).then_inc(st["v"].sem, 1)
                return part

            def ln_out(st, lag, xc, to, freed):
                def part(at):
                    for u, g, i in at(lag):
                        dve.wait_ge(*done(st["r"], g))
                        freed(u, g, i)
                        V.scalar_tensor_tensor(out=to(u), in0=slot(xc, u), scalar=0.0,
                                               in1=over_features(small[:, u, 4, :]), op0=ALU.max, op1=ALU.mult
                                               ).then_inc(st["h"].sem, 1)
                return part

            centre0 = ln_centre(NS[0], 0, buf[0], buf[2], lambda u, g, i: dve.wait_ge(*landed(NS[0]["load"][0][u], i)))
            var0 = ln_var(NS[0], 1, buf[3])
            out0 = ln_out(NS[0], 2, buf[2], lambda u: slot(buf[4], u), lambda u, g, i: dve.wait_ge(*reuse(NS[0]["ht"], g)))

            def node0(at):
                st = NS[0]
                out0(at)
                var0(at)
                centre0(at)
                for u, g, i in at(5):
                    dve.wait_ge(*done(st["mm"], g))
                    dve.wait_ge(*landed_before(st["store"][1][u], i))
                    dve.wait_ge(*landed_before(st["store"][2][u], i))
                    for j, row in ((6, 0), (7, 1)):
                        m = V.tensor_tensor(slot(buf[j], u), ps[2 * (j - 4) + u][:, :].rearrange("p (t d) -> p t d", d=D),
                                            bias_rows[:, row:row + 1, :].to_broadcast([P, T, D]), ALU.add)
                    m.then_inc(st["o2"].sem, 1)
            over_groups(dve, 5, node0)

            slow = dve.alloc_register("slow_dve")
            dve.reg_mov(slow, 0)

            def segment(k, msg, width, weighted):
                e = E[k]

                def build(k_, t):
                    dve.wait_ge(*reuse(e["seg"], k_))
                    V.tensor_scalar(hot[:, t % 2, :], iota_node[:, :],
                                    rel[:, :, :].rearrange("p b q -> p (b q)")[:, bass.ds(k_, 1)],
                                    ew[:, bass.ds(k_, 1)] if weighted else None,
                                    ALU.is_equal, *([ALU.mult] if weighted else [])).then_inc(e["hot"].sem, 1)

                def add(k_, t):
                    first = dve.value_load(first_row[0:1, bass.ds(k_, 1)], min_val=0, max_val=NODE_TILES - 1)
                    dve.wait_ge(*done(e["seg"], k_))
                    dve.wait_ge(*done(e["added"], k_ - 1))
                    o = agg[:, bass.ds(first, WINDOW), 0:width]
                    V.tensor_tensor(o, o, ps[t % 2][:, 0:WINDOW * AW].rearrange("p (w d) -> p w d", d=AW)[:, :, 0:width],
                                    ALU.add).then_inc(e["added"].sem, 1)

                def slow_step(b, t):
                    k_ = b * T + t

                    def step(tile):
                        dve.reg_add(slow, slow, 1)
                        V.tensor_scalar(hot_x[:, :], iota_node[:, 0:P], tile_base[:, bass.ds(tile, 1)],
                                        dst_f[:, :, :].rearrange("p b q -> p (b q)")[:, bass.ds(k_, 1)],
                                        ALU.add, ALU.is_equal).then_inc(s_slow_self, 1)
                        dve.wait_ge(s_slow_self, slow)
                        if weighted:
                            V.tensor_scalar(hot_x[:, :], hot_x[:, :], ew[:, bass.ds(k_, 1)], None, ALU.mult
                                            ).then_inc(s_slow_built, 1)
                        else:
                            V.tensor_copy(hot_x[:, :], hot_x[:, :]).then_inc(s_slow_built, 1)
                        dve.wait_ge(s_slow_mul, slow)
                        o = agg[:, bass.ds(tile, 1), 0:width].rearrange("p o d -> p (o d)")
                        V.tensor_tensor(o, o, ps[2][:, 0:width], ALU.add).then_inc(s_slow_added, 1)
                        dve.wait_ge(s_slow_added, slow)
                    return step

                def body(b, u, n, tile_hook=None):
                    for t in range(n):
                        build(b * T + t, t)
                        if t:
                            add(b * T + t - 1, t - 1)
                        if tile_hook:
                            tile_hook(b * T + t, t)
                    add(b * T + n - 1, n - 1)
                    dve.wait_ge(*done(e["added"], b * T + n - 1))
                    beyond(dve, b, lambda t: slow_step(b, t), n)
                    dve.sem_inc(e["consumed"].sem, 1)
                return body

            def over_blocks(body):
                with dve.Fori(0, PAIRS_E) as i:
                    for u in range(2):
                        body(i * 2 + u, i, u, T)
                body(BLOCKS - 1, PAIRS_E, 0, TAIL)

            e = E[0]
            seg0 = segment(0, rows_u, AW, False)

            def hist_hot(k_, t):
                dve.wait_ge(*reuse(e["hist"], k_))
                V.tensor_scalar(hot_lo[:, t % 2, :], iota_node[:, 0:P], src_lo[:, bass.ds(k_, 1)], None, ALU.is_equal)
                V.tensor_scalar(hot_hi[:, t % 2, :], iota_tile[:, :], src_hi[:, bass.ds(k_, 1)], None, ALU.is_equal
                                ).then_inc(e["hist_hot"].sem, 1)

            def edge0(b, i, u, n):
                w = n * D
                dve.wait_ge(e["src_got"][u].sem, e["src_got"][u].base + gathered(i) + 16 * n)
                dve.wait_ge(e["dst_got"][u].sem, e["dst_got"][u].base + gathered(i) + 16 * n)
                dve.wait_ge(*reuse(e["act"], b))
                dve.wait_ge(*reuse(e["z"], b))
                V.tensor_tensor(buf[6][:, u, 0:w], buf[0][:, u, 0:w], buf[1][:, u, 0:w], ALU.add
                                ).then_inc(s_z_self, 1)
                dve.wait_ge(s_z_self, b + 1)
                dve.wait_ge(*done(e["z_mm"], b))
                V.tensor_tensor(buf[2][:, u, 0:w], buf[6][:, u, 0:w], ps[3 + u][:, 0:w], ALU.add).then_inc(e["z"].sem, 1)
                dve.wait_ge(*done(e["act"], b))
                V.tensor_scalar(buf[3][:, u, 0:w], buf[3][:, u, 0:w], 1.0, -1.0, ALU.min, ALU.add
                                ).then_inc(s_elu_self, 1)
                dve.wait_ge(s_elu_self, b + 1)
                dve.wait_ge(*reuse(e["consumed"], b))
                V.tensor_tensor(rows_u[:, u, 0:n, 0:D], buf[3][:, u, 0:w].rearrange("p (t d) -> p t d", d=D),
                                buf[4][:, u, 0:w].rearrange("p (t d) -> p t d", d=D), ALU.add).then_inc(e["msg"].sem, 1)
                seg0(b, u, n, hist_hot)

            dve.wait_ge(s_agg0, 1)
            over_blocks(edge0)
            dve.wait_ge(*done(e["hist"], ET))
            V.tensor_scalar(deg_out[:, 0:NODE_TILES], ps[6][:, 0:NODE_TILES], 1.0, None, ALU.max).then_inc(s_degrees, 1)
            V.tensor_scalar(deg_in[:, :], agg[:, :, D:AW].rearrange("p t o -> p (t o)"), 1.0, None, ALU.max
                            ).then_inc(s_degrees, 1)
            dve.wait_ge(s_degrees, 2)
            dve.sem_inc(e["sums_done"], 1)

            dve.wait_ge(s_norms, 2)
            centre1 = ln_centre(NS[1], 7, buf[6], buf[7], lambda u, g, i: dve.wait_ge(*done(NS[1]["x"], g)))
            var1 = ln_var(NS[1], 8, rows_u_flat, True)
            out1 = ln_out(NS[1], 9, buf[7], lambda u: slot(wide, u, D, 512),
                          lambda u, g, i: dve.wait_ge(*landed_before(NS[1]["store"][1][u], i)))

            def node1(at):
                st = NS[1]
                out1(at)
                var1(at)
                for u, g, i in at(7):
                    dve.wait_ge(*done(st["xmm"], g))
                    dve.wait_ge(*landed(st["load"][0][u], i))
                    dve.wait_ge(*landed_before(st["store"][0][u], i))
                    V.tensor_tensor(buf[6][:, u, :], ps[6 + u][:, :], buf[0][:, u, :], ALU.add
                                    ).then_inc(st["x"].sem, 1)
                for u, g, i in at(4):
                    dve.wait_ge(*done(st["act"], g))
                    V.tensor_scalar(buf[3][:, u, :], buf[3][:, u, :], 1.0, -1.0, ALU.min, ALU.add
                                    ).then_inc(st["e1"].sem, 1)
                centre1(at)
                for u, g, i in at(4):
                    dve.wait_ge(*done(st["e1"], g))
                    dve.wait_ge(*reuse(st["et"], g))
                    V.tensor_tensor(buf[5][:, u, :], buf[3][:, u, :], buf[4][:, u, :], ALU.add
                                    ).then_inc(st["e"].sem, 1)
                for u, g, i in at(3):
                    dve.wait_ge(*done(st["zmm"], g))
                    dve.wait_ge(*landed(st["load"][1][u], i))
                    dve.wait_ge(*reuse(st["act"], g))
                    V.tensor_tensor(buf[2][:, u, :], ps[4][:, :], buf[1][:, u, :], ALU.add).then_inc(st["z"].sem, 1)
            over_groups(dve, 9, node1)

            def plain_segment(k, weighted):
                seg = segment(k, rows_u, D, weighted)
                over_blocks(lambda b, i, u, n: seg(b, u, n))

            def sums_cleared(st):
                dve.wait_ge(*done(st["zero"], GROUPS - 1))

            def scaled_sums(st):
                def part(at):
                    for u, g, i in at(0):
                        dve.wait_ge(*reuse(st["st"], g))
                        V.tensor_tensor(slot(buf[5], u), agg[:, bass.ds(g * T, T), 0:D],
                                        over_features(cols(norm_in, g, T)), ALU.mult).then_inc(st["sc"].sem, 1)
                return part

            sums_cleared(NS[1])
            plain_segment(1, False)
            scaled2 = scaled_sums(NS[2])

            def node2(at):
                st = NS[2]
                for u, g, i in at(3):
                    dve.wait_ge(*done(st["mm"], g))
                    dve.wait_ge(*landed_before(st["store"][0][u], i))
                    V.scalar_tensor_tensor(out=slot(buf[7], u), in0=ps[4 + u][:, :].rearrange("p (t d) -> p t d", d=D),
                                           scalar=0.0, in1=over_features(cols(norm_out, g, T)),
                                           op0=ALU.max, op1=ALU.mult).then_inc(st["o"].sem, 1)
                scaled2(at)
            over_groups(dve, 3, node2)
            sums_cleared(NS[2])
            plain_segment(2, False)
            scaled3 = scaled_sums(NS[3])
            centre3 = ln_centre(NS[3], 3, buf[6], buf[7], lambda u, g, i: dve.wait_ge(*done(NS[3]["x"], g)))
            var3 = ln_var(NS[3], 4, buf[3])
            out3 = ln_out(NS[3], 5, buf[7], lambda u: slot(buf[4], u),
                          lambda u, g, i: dve.wait_ge(*landed_before(NS[3]["store"][1][u], i)))

            def node3(at):
                st = NS[3]
                out3(at)
                for u, g, i in at(3):
                    dve.wait_ge(*done(st["mm"], g))
                    dve.wait_ge(*landed(st["load"][0][u], i))
                    dve.wait_ge(*landed_before(st["store"][0][u], i))
                    V.scalar_tensor_tensor(out=buf[6][:, u, :], in0=ps[4 + u][:, :], scalar=0.0, in1=buf[0][:, u, :],
                                           op0=ALU.max, op1=ALU.add).then_inc(st["x"].sem, 1)
                var3(at)
                centre3(at)
                scaled3(at)
            over_groups(dve, 5, node3)
            sums_cleared(NS[3])
            plain_segment(3, True)

            def cat(st):
                def part(at):
                    for u, g, i in at(0):
                        dve.wait_ge(*reuse(st["ct"], g))
                        V.tensor_copy(wide[:, u, :].rearrange("p (t c) -> p t c", c=P)[:, :, 0:D],
                                      agg[:, bass.ds(g * T, T), 0:D]).then_inc(st["cat"].sem, 1)
                return part

            cat4 = cat(NS[4])

            def node4(at):
                st = NS[4]
                for u, g, i in at(3):
                    dve.wait_ge(*done(st["mm"], g))
                    dve.wait_ge(*landed_before(st["store"][0][u], i))
                    V.tensor_scalar(buf[7][:, u, :], ps[4 + u][:, :], 0.0, None, ALU.max).then_inc(st["o"].sem, 1)
                cat4(at)
            over_groups(dve, 3, node4)
            sums_cleared(NS[4])
            plain_segment(4, True)
            cat5 = cat(NS[5])
            centre5 = ln_centre(NS[5], 3, buf[6], buf[7], lambda u, g, i: dve.wait_ge(*done(NS[5]["x"], g)))
            var5 = ln_var(NS[5], 4, buf[3])
            out5 = ln_out(NS[5], 5, buf[7], lambda u: slot(buf[4], u), lambda u, g, i: dve.wait_ge(*reuse(NS[5]["ht"], g)))

            def node5(at):
                st = NS[5]
                out5(at)
                for u, g, i in at(3):
                    dve.wait_ge(*done(st["mm"], g))
                    dve.wait_ge(*landed(st["load"][1][u], i))
                    dve.wait_ge(*landed_before(st["store"][1][u], i))
                    V.tensor_tensor(buf[6][:, u, :], ps[4 + u][:, :], buf[0][:, u, :], ALU.add
                                    ).then_inc(st["x"].sem, 1)
                var5(at)
                centre5(at)
                for u, g, i in at(9):
                    dve.wait_ge(*done(st["wh"], g))
                    dve.wait_ge(*reuse(st["nrm2"], g))
                    V.tensor_reduce(small[:, u, 5, :], slot(buf[5], u), AX_X, ALU.add).then_inc(st["nrm"].sem, 1)
                cat5(at)
            over_groups(dve, 9, node5)

            e = E[5]
            s5 = [0]

            def edge5(b, i, u, n):
                s = small[:, u, :, 0:n]
                step = [0]

                def mine(ins):
                    step[0] += 1
                    ins.then_inc(s_e5[u], 1)
                    dve.wait_ge(s_e5[u], i * E5_STEPS + step[0])

                wr, wc = rows_u[:, u, 0:n, :], rows_v[:, u, 0:n, :]
                c = lambda x: x[:, u, 0:n * D].rearrange("p (t d) -> p t d", d=D)
                dve.wait_ge(e["src_got"][u].sem, e["src_got"][u].base + gathered(i) + 16 * n)
                dve.wait_ge(e["dst_got"][u].sem, e["dst_got"][u].base + gathered(i) + 16 * n)
                mine(V.tensor_tensor(c(buf[2]), wr[:, :, 0:D], wc[:, :, 0:D], ALU.mult))
                mine(V.tensor_reduce(s[:, 0, :], c(buf[2]), AX_X, ALU.add))
                mine(V.tensor_tensor(s[:, 1, :].unsqueeze(2), wr[:, :, D:AW], wc[:, :, D:AW], ALU.mult))
                mine(V.tensor_scalar(s[:, 1, :], s[:, 1, :], SIM_EPS, None, ALU.max))
                mine(V.reciprocal(s[:, 2, :], s[:, 1, :]))
                mine(V.tensor_tensor(s[:, 3, :], s[:, 0, :], s[:, 2, :], ALU.mult))
                mine(V.tensor_scalar(s[:, 4, :], s[:, 3, :], 0.0, par_w[:, 8:9], ALU.max, ALU.mult))
                mine(V.tensor_scalar(s[:, 5, :], s[:, 3, :], 0.0, par_w[:, 9:10], ALU.min, ALU.mult))
                mine(V.tensor_tensor(s[:, 4, :], s[:, 4, :], s[:, 5, :], ALU.add))
                mine(V.tensor_tensor(s[:, 6, :], s[:, 4, :], cols(base, b, n), ALU.mult))
                dve.wait_ge(*reuse(e["dedup"], b))
                V.tensor_tensor(c(buf[4]), wc[:, :, 0:D], s[:, 6, :].unsqueeze(2).to_broadcast([P, n, D]),
                                ALU.mult).then_inc(e["contrib"].sem, 1)
                dve.wait_ge(*done(e["contrib"], b))
                dve.wait_ge(*landed(e["row_got"][u], i))
                for t in range(n):
                    k_ = b * T + t
                    dve.wait_ge(*reuse(e["same_used"], k_))
                    V.tensor_scalar(same[:, t % 2, 0:P], wide[:, u, t * P:(t + 1) * P].bitcast(I32), sf[:, bass.ds(k_, 1)],
                                    None, ALU.is_equal).then_inc(e["same"].sem, 1)
                    dve.wait_ge(*done(e["same"], k_))
                    mine(V.tensor_tensor_reduce(junk[:, :], same[:, t % 2, 0:P], below[:, :], 1.0, 0.0,
                                                ALU.mult, ALU.add, s[:, 7, t:t + 1]))
                dve.sem_inc(e["rows_used"].sem, 1)
                mine(V.tensor_scalar(s[:, 8, :], s[:, 7, :], 0.5, None, ALU.is_lt))
                mine(V.tensor_scalar(s[:, 9, :], cols(sf, b, n), 0.0, None, ALU.is_ge))
                mine(V.tensor_tensor(s[:, 8, :], s[:, 8, :], s[:, 9, :], ALU.mult))
                mine(V.tensor_scalar(s[:, 9, :], cols(src_row, b, n), lane_dump[:, 0:1], None, ALU.subtract))
                mine(V.tensor_tensor(s[:, 8, :], s[:, 8, :], s[:, 9, :], ALU.mult))
                dve.wait_ge(*done(e["sum"], b))
                V.tensor_scalar(idx_o[:, u, 0:n], s[:, 8, :], lane_dump[:, 0:1], None, ALU.add).then_inc(e["oidx"].sem, 1)
                assert n != T or step[0] == E5_STEPS, step

            over_blocks(edge5)

            def node6(at):
                st = NS[6]
                for u, g, i in at(1):
                    dve.wait_ge(*done(st["sum1"], g))
                    dve.wait_ge(*landed_before(st["store"][0][u], i))
                    V.tensor_tensor(buf[7][:, u, :], buf[4][:, u, :], buf[5][:, u, :], ALU.add
                                    ).then_inc(st["sum"].sem, 1)
                for u, g, i in at(0):
                    c = st["load"][0][u]
                    dve.wait_ge(c.sem, c.base + 16 * (TABLES * (i + 1) + 1))
                    V.tensor_tensor(buf[4][:, u, :], buf[0][:, u, :], buf[1][:, u, :], ALU.add)
                    V.tensor_tensor(buf[5][:, u, :], buf[2][:, u, :], buf[3][:, u, :], ALU.add
                                    ).then_inc(st["sum1"].sem, 1)
            over_groups(dve, 1, node6, FULL_GROUPS + 1)

_INS = ['x', 'src', 'dst', 'edge_attr_16', 'edge_weight', 'edge_weight_n2', 'L0_gnn_W1m', 'L0_gnn_b1m', 'L0_gnn_W2m',
        'L0_gnn_b2m', 'L0_gnn_W1u', 'L0_gnn_b1u', 'L0_gnn_W2u', 'L0_gnn_b2u', 'L1_gnn_W1', 'L1_gnn_b1', 'L1_gnn_W2',
        'L1_gnn_b2', 'L2_gnn_W_rel1', 'L2_gnn_b_rel1', 'L2_gnn_W_root1', 'L2_gnn_W_rel2', 'L2_gnn_b_rel2',
        'L2_gnn_W_root2', 'L3_gnn_W', 'L3_gnn_b', 'L3_gnn_deg_coeff', 'L3_gnn_coeff_param', 'L3_gnn_scale_param']


def kernel(**inputs):
    import numpy as _np
    import concourse.bacc as _bacc
    from concourse import mybir as _mybir
    from concourse.bass_utils import run_bass_kernel_spmd as _run

    nc = _bacc.Bacc("TRN2", target_bir_lowering=False, num_devices=1)
    arrays, args = {}, {}
    for name in _INS:
        v = _np.ascontiguousarray(inputs[name])
        arrays[f"in_{name}_dram"] = v
        args[name] = nc.dram_tensor(f"in_{name}_dram", v.shape, _mybir.dt.from_np(v.dtype), kind="ExternalInput").ap()
    result = nc.dram_tensor("out_0_dram", (N, D), _mybir.dt.float32, kind="ExternalOutput").ap()
    program(nc, args, result)
    r = _run(nc, [arrays], core_ids=[0])
    return r.results[0]["out_0_dram"]
```

```python
from contextlib import ExitStack

import concourse.bass as bass
from concourse import mybir
from concourse.alu_op_type import AluOpType as ALU

F32 = mybir.dt.float32
I32 = mybir.dt.int32
BF16 = mybir.dt.bfloat16
ACT = mybir.ActivationFunctionType
AX_X = mybir.AxisListType.X

P = 128
D = 64
FE = 16
T = 8
HALF = T // 2
N = 50000
EDGES = 50000
ET = -(-EDGES // P)
LAST = EDGES - (ET - 1) * P
BLOCKS = -(-ET // T)
PAIRS_E = (BLOCKS - 1) // 2
ROW_SLOTS = 4
QUADS = (BLOCKS - 1) // ROW_SLOTS
assert QUADS * ROW_SLOTS == BLOCKS - 1
TAIL = ET - (BLOCKS - 1) * T
GROUPS = 50
NT = GROUPS * T
NP = NT * P
NODE_TILES = -(-N // P)
FULL_GROUPS = N // (P * T)
PAIRS_N = GROUPS // 2
AW = D + 1
WINDOW = 3
TABLES = 4
CREDIT = 4
CLEARS = 20
EPS = 1e-5
SIM_EPS = 1e-8


N_LOADS = 16 + 4 + T + 2 + 8 + 3
E5_STEPS = 15 + T


def gathered(i):
    return 16 * T * i


def scatters(j):
    return sum(1 for t in range((BLOCKS - 1) * T + TAIL) if t % T % TABLES == j)


def done(c, k):
    return c.sem, c.base + (k + 1 + CREDIT)


def reuse(c, k, slots=2):
    return c.sem, c.base + (k + 1 - slots + CREDIT)


def landed(c, i):
    return c.sem, c.base + 16 * (i + 2)


def landed_before(c, i):
    return c.sem, c.base + 16 * (i + 1)


def program(nc, a, out):
    with ExitStack() as ctx:
        def sb(name, shape, dt=F32):
            return ctx.enter_context(nc.sbuf_tensor(name, shape, dt))

        ring_sems, dma_rings = [], []

        def sem(name):
            return ctx.enter_context(nc.semaphore(name))

        def ring(name):
            s = sem(name)
            ring_sems.append(s)
            return s

        def dma_ring(name, n=2):
            s = [sem(f"{name}{u}") for u in range(n)]
            dma_rings.extend(s)
            return s

        def dram(name, rows=NP, width=D):
            return nc.dram_tensor(name, (rows, width), F32).ap()

        tab_a, tab_b, tab_q = dram("tab_a"), dram("tab_b"), dram("tab_q")
        tab_x1, tab_x2 = dram("tab_x1"), dram("tab_x2")
        tab_g1, tab_g2, tab_h2, tab_h3 = dram("tab_g1"), dram("tab_g2"), dram("tab_h2"), dram("tab_h3")
        tab_wh = dram("tab_wh", NP, AW)
        acc = [dram(f"acc{j}", NP + P) for j in range(TABLES)]

        def group(table, g):
            w = table.shape[1]
            return table[0:NP, :].rearrange("(g p j) d -> g p (j d)", p=P, j=T)[g]

        def natural(table, g):
            return table[bass.ds(g * (P * T), P * T), :].rearrange("(t p) d -> p t d", p=P)

        agg = sb("agg", [P, NT, AW])
        zeros = sb("zeros", [P, T * D // 2])
        zeros_b = sb("zeros_b", [P, NODE_TILES], BF16)
        ident = sb("ident", [P, P])
        ones = sb("ones", [P, P])
        iota_node = sb("iota_node", [P, P])
        iota_tile = sb("iota_tile", [P, NODE_TILES])
        tile_base = sb("tile_base", [P, NT])
        below = sb("below", [P, P])
        lane_dump = sb("lane_dump", [P, 1])
        power = sb("power", [P, 1])
        half = sb("half", [P, 1])
        block_mask = sb("block_mask", [P, T])
        src_f = sb("src_f", [P, 4, P])
        dst_f = sb("dst_f", [P, 4, P])
        lane = sb("lane", [P, 4 * P])
        window_tile = sb("window_tile", [P, 4 * P])
        in_tile = sb("in_tile", [P, WINDOW, T])
        src_row = sb("src_row", [P, 4 * P], I32)
        dst_row = sb("dst_row", [P, 4 * P], I32)
        ew = sb("ew", [P, 4 * P])
        base = sb("base", [P, 4 * P])
        first_i = sb("first_i", [P, 4], I32)
        last_i = sb("last_i", [P, 4], I32)
        span_f = sb("span_f", [P, 4, 2])
        first_row = sb("first_row", [1, 4 * P], I32)
        xhi_row = sb("xhi_row", [1, 4 * P], I32)
        beyond_i = sb("beyond_i", [1, 4 * P // T], I32)
        degrees = sb("degrees", [P, 2, NT])
        norms = sb("norms", [P, 2, NT])
        deg_out, deg_in = degrees[:, 0, :], degrees[:, 1, :]
        norm_out, norm_in = norms[:, 0, :], norms[:, 1, :]
        w1e_nat = sb("w1e_nat", [D, T, FE])
        w2m_nat = sb("w2m_nat", [D, AW])
        wt = sb("wt", [P, 7, D])
        w_upd_agg = sb("w_upd_agg", [AW, D])
        w_pair = sb("w_pair", [P, 7, 2 * D])
        w1e_t = sb("w1e_t", [P, D])
        w1e_diag = sb("w1e_diag", [P, T, D])
        bias3 = sb("bias3", [3, 8, D], BF16)
        ones_b = sb("ones_b", [P, P], BF16)
        par = sb("par", [P, 8])
        par_w = sb("par_w", [P, 16])
        buf = [sb(f"buf{j}", [P, 2, T * D]) for j in range(8)]
        wide = sb("wide", [P, 2, T * P])
        wide_t = sb("wide_t", [P, 2, T * P])
        rows_u = sb("rows_u", [P, 2, T, AW])
        rows_v = sb("rows_v", [P, 2, T, AW])
        hot = sb("hot", [P, 4, P])
        hot_x = sb("hot_x", [P, P])
        hot_lo = sb("hot_lo", [P, 2, P], BF16)
        hot_hi = sb("hot_hi", [P, 2, NODE_TILES], BF16)
        idx_s = sb("idx_s", [P, 2, T], I32)
        idx_d = sb("idx_d", [P, 2, T], I32)
        idx_o = sb("idx_o", [P, 2, T], I32)
        edge_io = rows_v[:, :, :, :].rearrange("p u t d -> p u (t d)")
        edge_in, edge_t = edge_io[:, :, 0:T * FE], edge_io[:, :, T * FE:T * FE + P]
        small = sb("small", [P, 2, 10, T])
        four = lambda x: x.rearrange("p (b q) -> p b q", b=4)
        stage_i = [four(buf[2 + j // 2][:, j % 2, :].bitcast(I32)) for j in range(3)]
        stage_f = four(buf[3][:, 1, :])
        first_f, last_f = buf[7][:, 0, :], buf[7][:, 1, :]
        beyond_f = buf[6][0:1, 0, :]
        nat = buf[1][0:D, :, :].rearrange("p u (w k) -> p (u w) k", k=2 * D)
        rows_u_flat = rows_u[:, :, :, :].rearrange("p u t d -> p u (t d)")
        src_lo, src_hi = wide[:, 0, 0:4 * P], wide[:, 1, 0:4 * P]
        bias = hot[0:1, :, :].rearrange("o a (b d) -> o (a b) d", d=D)
        bias_parts = norms[0:1, :, :].rearrange("o a n -> o (a n)")[:, 0:3 * 4 * D].bitcast(BF16)
        dst_hot = [buf[j][:, u, 0:WINDOW * P] for j in (3, 7) for u in range(2)]
        hot_half = [hot[:, :, :], buf[5][:, 0, :].rearrange("p (t q) -> p t q", q=P)]
        same = hot
        earlier = [buf[0][:, t // 4, t % 4 * P:(t % 4 + 1) * P] for t in range(T)]
        ps = [ctx.enter_context(nc.psum_tensor(f"ps{j}", [P, 512], F32)) for j in range(8)]

        seg_ps = [ps[0], ps[1], ps[2], ps[7]]
        SEG = len(seg_ps)
        rows_slot = [r[:, u, :, :] for r in (rows_u, rows_v) for u in range(2)]
        idx_slot = [x[:, u, :] for x in (idx_s, idx_d) for u in range(2)]
        WA, WB, WQ, WU2, WC1, WC2, WUM = range(7)
        PA, PB, PQ, PU2, PG1, PG2, PL3 = range(7)
        B1M, B1U, B2U, BG1, BG2, BR1, BR2, BL3 = range(8)

        s_in = sem("s_in")
        s_stage_clear = sem("s_stage_clear")
        s_idx_in = sem("s_idx_in")
        s_const = sem("s_const")
        s_pool_self = sem("s_pool_self")
        s_credit = sem("s_credit")
        s_agg0 = sem("s_agg0")
        s_pe_setup = sem("s_pe_setup")
        s_dve = sem("s_dve")
        s_act_setup = sem("s_act_setup")
        s_setup_done = sem("s_setup_done")
        s_pool_hold = sem("s_pool_hold")
        s_slow_built = sem("s_slow_built")
        s_slow_mul = sem("s_slow_mul")
        s_slow_added = sem("s_slow_added")
        s_degrees = sem("s_degrees")
        s_norms = sem("s_norms")
        s_bias_split = sem("s_bias_split")
        s_beyond_rows = sem("s_beyond_rows")
        s_rows_copied = sem("s_rows_copied")
        s_act_hold = sem("s_act_hold")
        s_dve_hold = sem("s_dve_hold")
        s_bias_in = sem("s_bias_in")
        s_acc_zero = sem("s_acc_zero")
        s_out = sem("s_out")
        s_rest = sem("s_rest")
        s_src_staged, s_dst_staged, s_spans = sem("s_src_staged"), sem("s_dst_staged"), sem("s_spans")
        s_exp_args, s_wt = sem("s_exp_args"), sem("s_wt")
        s_slow_self = sem("s_slow_self")
        s_z_self, s_elu_self = sem("s_z_self"), sem("s_elu_self")
        s_e5 = [sem(f"s_e5_self{u}") for u in range(2)]
        s_norm_self = sem("s_norm_self")

        class Count:
            def __init__(self, sem_, base):
                self.sem, self.base = sem_, base

        totals = {}

        def counted(name, n, per=1):
            if name not in totals:
                totals[name] = [sem(name), 0]
                if "_got" not in name or name[:3] in ("edg", "row"):
                    (ring_sems if per == 1 else dma_rings).append(totals[name][0])
            c = Count(totals[name][0], totals[name][1])
            totals[name][1] += n * per
            return c

        def edge_stage(per_block, per_tile, dmas, **more):
            names = {n: counted(f"{n}_done", BLOCKS) for n in per_block.split()}
            names.update({n: counted(f"{n}_done", ET) for n in per_tile.split()})
            for n in dmas.split():
                one = n in ("edge_got", "row_got", "row_dst_got")
                names[n] = [counted(f"{n}{u}", (PAIRS_E + 1 - u) if one else
                                    PAIRS_E * T + (TAIL if u == 0 else 0), 16) for u in range(2)]
            return {**names, **more}

        def plain_stage():
            names = edge_stage("idx consumed mask", "seg added", "")
            names["hot"] = counted("hot_done", 2 * BLOCKS)
            names["spread"] = counted("spread_done", 2 * BLOCKS)
            names["got"] = [counted(f"{n}{u}", QUADS * T + (TAIL if n == "src_got" and u == 0 else 0), 16)
                            for n in ("src_got", "dst_got") for u in range(2)]
            return names

        def node_stage(steps, loads=0, stores=1, groups=GROUPS):
            names = {n: counted(f"{n}_done", groups) for n in steps.split()}
            names["load"] = [[counted(f"load{j}_{u}", PAIRS_N, 16) for u in range(2)] for j in range(loads)]
            names["store"] = [[counted(f"store{j}_{u}", PAIRS_N, 16) for u in range(2)] for j in range(stores)]
            return names

        LN = "s xc sq v2 v r h "
        E, NS = [None] * 6, [None] * 7
        NS[0] = node_stage(LN + "ht htc mm o", 1, 3)
        E[0] = edge_stage("idx edge_t edge_c z_mm z act msg consumed mask", "seg added hist_hot hist",
                          "src_got dst_got edge_got", hot=counted("hot_done", 2 * BLOCKS),
                          spread=counted("spread_done", 2 * BLOCKS),
                          sums_done=sem("sums_done"))
        NS[1] = node_stage(LN + "ag at atc zmm z act e1 e et etc xmm x zero", 2, 2)
        E[1] = plain_stage()
        NS[2] = node_stage("sc st stc mm o zero", 0, 1)
        E[2] = plain_stage()
        NS[3] = node_stage(LN + "sc st stc mm x zero", 1, 2)
        E[3] = plain_stage()
        NS[4] = node_stage("cat ct ctc mm o zero", 1, 1)
        E[4] = plain_stage()
        NS[5] = node_stage(LN + "cat ct ctc mm x ht htc wmm wh nrm nrm2", 2, 3)
        E[5] = edge_stage("idx contrib dedup rows_used sum oidx target dst_rows dst_gathered", "same same_used",
                          "src_got row_got row_dst_got", dst_hot=counted("dst_hot_done", BLOCKS * T),
                          dst_mm=counted("dst_mm_done", BLOCKS * T),
                          table=[sem(f"scattered{j}") for j in range(TABLES)])
        NS[6] = node_stage("sum1 sum", 1, 1, FULL_GROUPS + 1)

        def slot(b, u, width=D, at=0):
            return b[:, u, at:at + T * width].rearrange("p (t d) -> p t d", d=width)

        def over_features(v):
            return v.unsqueeze(2).to_broadcast([P, v.shape[1], D])

        def over_groups(eng, lag, body, count=GROUPS):
            def fixed(j):
                return lambda l: [((j - l) % 2, j - l, (j - l) // 2)] if 0 <= j - l < count else []

            def rolled(i, v):
                return lambda l: [((v - l) % 2, i * 2 + (v - l), i + (v - l) // 2)]

            start = lag + lag % 2
            for j in range(start):
                body(fixed(j))
            with eng.Fori(start // 2, FULL_GROUPS // 2) as i:
                for v in range(2):
                    body(rolled(i, v))
            for j in range(FULL_GROUPS, count + lag):
                body(fixed(j))

        def cols(x, b, n):
            return x[:, bass.ds(b * T, n)]

        def beyond_flag(eng, b):
            return eng.value_load(beyond_i[0:1, bass.ds(b, 1)], min_val=0, max_val=1)

        def beyond(eng, b, some, step, n):
            with eng.If(some > 0):
                for t in range(n):
                    k = b * T + t
                    lo = eng.value_load(first_row[0:1, bass.ds(k, 1)], min_val=0, max_val=NODE_TILES) + WINDOW
                    hi = eng.value_load(xhi_row[0:1, bass.ds(k, 1)], min_val=1, max_val=NODE_TILES + WINDOW + 1)
                    with eng.Fori(lo, hi) as tile:
                        step(t)(tile)

        block = ctx.enter_context(nc.Block())

        @block.sync
        def _(sp):
            sp.wait_ge(s_stage_clear, 7)
            n_load = n_rest = 0
            for j, v in enumerate((a["src"], a["dst"], a["dst"])):
                sp.dma_start(stage_i[j][:, 0:3, :],
                             v[0:3 * P * P].rearrange("(b t p) -> t b p", t=P, p=P)).then_inc(s_idx_in, 16)
                sp.dma_start(stage_i[j][0:ET - 1 - 3 * P, 3, :],
                             v[3 * P * P:(ET - 1) * P].rearrange("(t p) -> t p", p=P)).then_inc(s_idx_in, 16)
                sp.dma_start(stage_i[j][ET - 1 - 3 * P:ET - 3 * P, 3, 0:LAST],
                             v[(ET - 1) * P:EDGES].rearrange("(t p) -> t p", t=1)).then_inc(s_idx_in, 16)
            for j, v in enumerate((a["edge_weight"], a["edge_weight_n2"])):
                w = wide[:, j, 0:4 * P].rearrange("p (b q) -> p b q", b=4)
                sp.dma_start(w[:, 0:3, :],
                             v[0:3 * P * P].rearrange("(b t p) -> t b p", t=P, p=P)).then_inc(s_idx_in, 16)
                sp.dma_start(w[0:ET - 1 - 3 * P, 3, :],
                             v[3 * P * P:(ET - 1) * P].rearrange("(t p) -> t p", p=P)).then_inc(s_idx_in, 16)
                sp.dma_start(w[ET - 1 - 3 * P:ET - 3 * P, 3, 0:LAST],
                             v[(ET - 1) * P:EDGES].rearrange("(t p) -> t p", t=1)).then_inc(s_idx_in, 16)

            def load(dst, src):
                nonlocal n_load
                sp.dma_start(dst, src).then_inc(s_in, 16)
                n_load += 1

            w1m, w1u = a["L0_gnn_W1m"], a["L0_gnn_W1u"]
            for h in range(2):
                load(nat[:, WA, h * D:(h + 1) * D], w1m[:, 0:D])
                load(nat[:, WB, h * D:(h + 1) * D], w1m[:, D:2 * D])
                load(nat[:, WQ, h * D:(h + 1) * D], w1u[:, 0:D])
                load(nat[:, WU2, h * D:(h + 1) * D], a["L0_gnn_W2u"])
                load(nat[:, WUM, h * D:(h + 1) * D], w1u[:, D:2 * D])
                load(w_pair[h * D:(h + 1) * D, PG1, h * D:(h + 1) * D], a["L1_gnn_W1"])
                load(w_pair[h * D:(h + 1) * D, PG2, h * D:(h + 1) * D], a["L1_gnn_W2"])
                load(w_pair[h * D:(h + 1) * D, PL3, h * D:(h + 1) * D], a["L3_gnn_W"])
            load(nat[:, WC1, 0:D], a["L2_gnn_W_rel1"])
            load(nat[:, WC1, D:2 * D], a["L2_gnn_W_root1"])
            load(nat[:, WC2, 0:D], a["L2_gnn_W_rel2"])
            load(nat[:, WC2, D:2 * D], a["L2_gnn_W_root2"])
            for t in range(T):
                load(w1e_nat[:, t, :], w1m[:, 2 * D:2 * D + FE])
            load(w2m_nat[:, 0:D], a["L0_gnn_W2m"])
            load(w2m_nat[:, D:D + 1], a["L0_gnn_b2m"].rearrange("(p o) -> p o", o=1))
            for j, n in enumerate(("L0_gnn_b1m", "L0_gnn_b1u", "L0_gnn_b2u", "L1_gnn_b1", "L1_gnn_b2",
                                   "L2_gnn_b_rel1", "L2_gnn_b_rel2", "L3_gnn_b")):
                load(bias[0:1, j, :], a[n].rearrange("(o d) -> o d", o=1))
            for c0, n, w in ((0, "L3_gnn_deg_coeff", 2), (2, "L3_gnn_coeff_param", 3), (5, "L3_gnn_scale_param", 1)):
                load(par[:, c0:c0 + w], a[n].rearrange("(o d) -> o d", o=1).to_broadcast([P, w]))
            assert n_load == N_LOADS

            def load_to(st, j, u, g, dst, table, *readers):
                for r in readers:
                    sp.wait_ge(*reuse(r, g))
                sp.dma_start(dst, group(table, g)).then_inc(st["load"][j][u].sem, 16)

            def store_from(st, j, u, g, srcb, table, writer):
                sp.wait_ge(*done(writer, g))
                sp.dma_start(group(table, g), srcb).then_inc(st["store"][j][u].sem, 16)

            def store_natural(st, j, u, g, srcb, table, writer):
                sp.wait_ge(*done(writer, g))
                sp.dma_start(natural(table, g), slot(srcb, u)).then_inc(st["store"][j][u].sem, 16)

            x_in = a["x"]
            whole = (N - FULL_GROUPS * P * T) // P
            rest = N - FULL_GROUPS * P * T - whole * P

            def load_x(st, u, g, reader):
                nonlocal n_rest
                sp.wait_ge(*reuse(reader, g))
                to = slot(buf[0], u)
                if not isinstance(g, int) or g < FULL_GROUPS:
                    rows = x_in[bass.ds(g * (P * T), P * T), :] if not isinstance(g, int) else \
                        x_in[g * P * T:(g + 1) * P * T, :]
                    sp.dma_start(to, rows.rearrange("(t p) d -> p t d", p=P)).then_inc(st["load"][0][u].sem, 16)
                elif g == FULL_GROUPS:
                    r0 = g * P * T
                    sp.dma_start(to[0:rest, whole, :], x_in[r0 + whole * P:N, :]).then_inc(s_rest, 16)
                    n_rest += 1
                    sp.wait_ge(s_rest, 16 * n_rest)
                    sp.dma_start(to[:, 0:whole, :], x_in[r0:r0 + whole * P, :]
                                 .rearrange("(t p) d -> p t d", p=P)).then_inc(st["load"][0][u].sem, 16)
                else:
                    sp.sem_inc(st["load"][0][u].sem, 16)

            sp.wait_ge(s_credit, 1)
            sp.wait_ge(s_const, 1)
            sp.wait_ge(s_bias_split, 1)
            for k in range(3):
                sp.dma_start(bias3[k:k + 1, :, :].rearrange("o b d -> o (b d)"),
                             bias_parts[:, k * 8 * D:(k + 1) * 8 * D]).then_inc(s_bias_in, 16)
            st = NS[0]

            def node0(at):
                for u, g, i in at(0):
                    load_x(NS[0], u, g, NS[0]["xc"])
                for u, g, i in at(7):
                    store_from(NS[0], 0, u, g, buf[5][:, u, :], tab_a, NS[0]["o"])
                    store_from(NS[0], 1, u, g, buf[6][:, u, :], tab_b, NS[0]["o"])
                    store_from(NS[0], 2, u, g, buf[7][:, u, :], tab_q, NS[0]["o"])
            over_groups(sp, 7, node0)

            e = E[0]
            with sp.Fori(0, PAIRS_E) as i:
                for u in range(2):
                    b = i * 2 + u
                    sp.wait_ge(*reuse(e["edge_t"], b))
                    sp.dma_start(edge_in[:, u, :].rearrange("p (t f) -> p t f", f=FE),
                                 a["edge_attr_16"][bass.ds(b * (P * T), P * T), :]
                                 .rearrange("(t p) f -> p t f", p=P)).then_inc(e["edge_got"][u].sem, 16)
            b = BLOCKS - 1
            r0 = b * P * T
            sp.wait_ge(*reuse(e["edge_t"], b))
            sp.dma_start(edge_in[0:LAST, 0, (TAIL - 1) * FE:TAIL * FE],
                         a["edge_attr_16"][EDGES - LAST:EDGES, :]).then_inc(s_rest, 16)
            n_rest += 1
            sp.wait_ge(s_rest, 16 * n_rest)
            sp.dma_start(edge_in[:, 0, 0:(TAIL - 1) * FE].rearrange("p (t f) -> p t f", f=FE),
                         a["edge_attr_16"][r0:r0 + (TAIL - 1) * P, :]
                         .rearrange("(t p) f -> p t f", p=P)).then_inc(e["edge_got"][0].sem, 16)

            sp.wait_ge(*done(E[0]["z"], BLOCKS - 1))
            for u in range(2):
                sp.wait_ge(*landed_before(NS[0]["store"][2][u], PAIRS_N))

            def node1(at):
                for u, g, i in at(10):
                    store_from(NS[1], 1, u, g, wide[:, u, 512:1024], tab_g1, NS[1]["h"])
                for u, g, i in at(8):
                    store_from(NS[1], 0, u, g, buf[6][:, u, :], tab_x1, NS[1]["x"])
                for u, g, i in at(5):
                    load_x(NS[1], u, g, NS[1]["x"])
                for u, g, i in at(1):
                    load_to(NS[1], 1, u, g, buf[1][:, u, :], tab_q, NS[1]["z"])
            over_groups(sp, 10, node1)

            for j in range(TABLES):
                sp.dma_start(acc[j][NP:NP + P, :], zeros[:, 0:D]).then_inc(s_acc_zero, 16)
            part = 2 * NT // T // CLEARS
            for q in range(CLEARS):
                sp.wait_ge(*done(E[1]["consumed"], 1 + q * (BLOCKS - 2) // CLEARS))
                for j in range(2, TABLES):
                    sp.dma_start(acc[j][0:NP, :].rearrange("(p g j) d -> p g (j d)", p=P, j=T // 2)
                                 [:, q * part:(q + 1) * part, :],
                                 zeros[:, :].unsqueeze(1).to_broadcast([P, part, T * D // 2])
                                 ).then_inc(s_acc_zero, 16)

            def node2(at):
                for u, g, i in at(4):
                    store_from(NS[2], 0, u, g, buf[7][:, u, :], tab_g2, NS[2]["o"])
            over_groups(sp, 4, node2)

            for u in range(2):
                sp.wait_ge(*landed_before(NS[1]["store"][0][u], PAIRS_N))

            def node3(at):
                for u, g, i in at(6):
                    store_from(NS[3], 1, u, g, buf[4][:, u, :], tab_h2, NS[3]["h"])
                for u, g, i in at(4):
                    store_from(NS[3], 0, u, g, buf[6][:, u, :], tab_x2, NS[3]["x"])
                for u, g, i in at(1):
                    load_to(NS[3], 0, u, g, buf[0][:, u, :], tab_x1, NS[3]["x"])
            over_groups(sp, 6, node3)
            for u in range(2):
                for j in range(2):
                    sp.wait_ge(*landed_before(NS[3]["store"][j][u], PAIRS_N))

            def cat_h(u):
                return wide[:, u, :].rearrange("p (t c) -> p t c", c=P)[:, :, D:P]

            def node4(at):
                for u, g, i in at(4):
                    store_from(NS[4], 0, u, g, buf[7][:, u, :], tab_h3, NS[4]["o"])
                for u, g, i in at(0):
                    load_to(NS[4], 0, u, g, cat_h(u), tab_h2, NS[4]["ct"])
            over_groups(sp, 4, node4)
            for u in range(2):
                sp.wait_ge(*landed_before(NS[4]["store"][0][u], PAIRS_N))

            def node5(at):
                for u, g, i in at(9):
                    store_natural(NS[5], 2, u, g, buf[1], acc[1], NS[5]["wh"])
                for u, g, i in at(10):
                    store_from(NS[5], 0, u, g, agg[:, bass.ds(g * T, T), :].rearrange("p t d -> p (t d)"), tab_wh,
                               NS[5]["nrm2"])
                for u, g, i in at(4):
                    store_natural(NS[5], 1, u, g, buf[6], acc[0], NS[5]["x"])
                for u, g, i in at(1):
                    load_to(NS[5], 1, u, g, buf[0][:, u, :], tab_x2, NS[5]["x"])
                for u, g, i in at(0):
                    load_to(NS[5], 0, u, g, cat_h(u), tab_h3, NS[5]["ct"])
            over_groups(sp, 10, node5)

            e = E[5]

            def ids(x, to, b, u, got):
                n = T * P if not isinstance(b, int) or b < BLOCKS - 1 else EDGES - b * P * T
                sp.dma_start(to[:, u, 0:n].bitcast(I32),
                             x[bass.ds(b * (P * T), n)].rearrange("(o q) -> o q", o=1).to_broadcast([P, n])
                             ).then_inc(e[got][u].sem, 16)

            def dst_ids(b, u):
                if not (isinstance(b, int) and b < 2):
                    sp.wait_ge(*done(e["dst_hot"], b * T - T - 1))
                ids(a["dst"], wide_t, b, u, "row_dst_got")

            def src_ids(b, u):
                sp.wait_ge(*reuse(e["rows_used"], b))
                ids(a["src"], wide, b, u, "row_got")

            dst_ids(0, 0)
            dst_ids(1, 1)
            src_ids(0, 0)
            with sp.Fori(1, PAIRS_E) as i:
                for u in range(2):
                    dst_ids(i * 2 + u, u)
                    src_ids(i * 2 + u - 1, 1 - u)
            dst_ids(BLOCKS - 1, 0)
            src_ids(BLOCKS - 2, 1)
            src_ids(BLOCKS - 1, 0)

            for j in range(TABLES):
                sp.wait_ge(e["table"][j], 16 * scatters(j))

            def node6(at):
                for u, g, i in at(2):
                    sp.wait_ge(*done(NS[6]["sum"], g))
                    if not isinstance(g, int) or g < FULL_GROUPS:
                        sp.dma_start(out[bass.ds(g * (P * T), P * T), :].rearrange("(p j) d -> p (j d)", j=T),
                                     buf[7][:, u, :]).then_inc(NS[6]["store"][0][u].sem, 16)
                    else:
                        r0 = g * P * T
                        sp.dma_start(out[r0:N, :].rearrange("(p j) d -> p (j d)", j=T),
                                     buf[7][0:(N - r0) // T, u, :]).then_inc(s_out, 16)
                for u, g, i in at(0):
                    sp.wait_ge(*reuse(NS[6]["sum"], g))
                    for j in range(TABLES):
                        sp.dma_start(buf[j][:, u, :],
                                     acc[j][bass.ds(g * (P * T), P * T), :].rearrange("(p j) d -> p (j d)", j=T)).then_inc(NS[6]["load"][0][u].sem, 16)
            over_groups(sp, 2, node6, FULL_GROUPS + 1)
            sp.wait_ge(s_out, 16)
            for u in range(2):
                sp.wait_ge(*landed_before(NS[6]["store"][0][u], FULL_GROUPS // 2))

        @block.gpsimd
        def _(pool):
            count = [0]

            def hold(*waits):
                for s, v in waits:
                    pool.wait_ge(s, v)
                pool.sem_inc(s_pool_hold, 1)

            def chain(ins):
                count[0] += 1
                ins.then_inc(s_pool_self, 1)
                pool.wait_ge(s_pool_self, count[0])

            for j, v in ((0, -1), (1, -1), (2, 1 << 20)):
                pool.memset(stage_i[j][:, 3, :], v).then_inc(s_stage_clear, 1)
            pool.memset(wide[:, :, 0:4 * P], 0.0).then_inc(s_stage_clear, 1)
            for j in (0, 1):
                pool.memset(buf[j][:, :, :], 0.0).then_inc(s_stage_clear, 1)
            pool.memset(w_pair[:, :, :], 0.0).then_inc(s_stage_clear, 1)
            for s_ in ring_sems:
                pool.sem_inc(s_, CREDIT)
            for s_ in dma_rings:
                pool.sem_inc(s_, 16)
            pool.sem_inc(s_credit, 1)
            chain(pool.memset(ident[:, :], 0.0))
            chain(pool.affine_select(out=ident[:, :], in_=ident[:, :], compare_op=ALU.not_equal, fill=1.0,
                                     base=0, pattern=[[-1, P]], channel_multiplier=1))
            chain(pool.memset(below[:, :], 1.0))
            chain(pool.affine_select(out=below[:, :], in_=below[:, :], compare_op=ALU.is_gt, fill=0.0,
                                     base=0, pattern=[[-1, P]], channel_multiplier=1))
            chain(pool.memset(block_mask[:, :], 1.0))
            chain(pool.affine_select(out=block_mask[:, :], in_=block_mask[:, :], compare_op=ALU.is_ge, fill=0.0,
                                     base=0, pattern=[[-FE, T]], channel_multiplier=1))
            chain(pool.affine_select(out=block_mask[:, :], in_=block_mask[:, :], compare_op=ALU.is_ge, fill=0.0,
                                     base=FE - 1, pattern=[[FE, T]], channel_multiplier=-1))
            small_ok = dict(allow_small_or_imprecise_dtypes=True)
            chain(pool.iota(iota_node[:, :], pattern=[[1, P]], base=0, channel_multiplier=0, **small_ok))
            chain(pool.iota(iota_tile[:, :], pattern=[[1, NODE_TILES]], base=0, channel_multiplier=0, **small_ok))
            chain(pool.iota(tile_base[:, :], pattern=[[P, NT]], base=0, channel_multiplier=0, **small_ok))
            chain(pool.iota(lane_dump[:, :], pattern=[[0, 1]], base=NP, channel_multiplier=1, **small_ok))
            chain(pool.memset(zeros[:, :], 0.0))
            chain(pool.memset(zeros_b[:, :], 0.0))
            chain(pool.memset(ones[:, :], 1.0))
            chain(pool.memset(ones_b[:, :], 1.0))
            chain(pool.memset(power[:, :], -0.5))
            chain(pool.memset(half[:, :], 0.5))
            for u in range(2):
                chain(pool.memset(rows_u[:, u, :, :], 1.0))
                chain(pool.memset(rows_v[:, u, :, :], 0.0))
            pool.sem_inc(s_const, 1)
            pool.memset(agg[:, :, :], 0.0).then_inc(s_agg0, 1)

            def ln_root(st, lag):
                def part(at):
                    for u, g, i in at(lag):
                        hold(done(st["v"], g), reuse(st["h"], g))
                        pool.tensor_tensor(small[:, u, 4, :], small[:, u, 3, :], power[:, :].to_broadcast([P, T]),
                                           ALU.pow).then_inc(st["r"].sem, 1)
                return part

            def clear_sums(st, used, lag):
                def part(at):
                    for u, g, i in at(lag):
                        hold(done(used, g))
                        pool.tensor_copy(agg[:, bass.ds(g * T, T), :],
                                         zeros[:, 0:AW].unsqueeze(1).to_broadcast([P, T, AW])
                                         ).then_inc(st["zero"].sem, 1)
                return part

            def gathers(k, table, b, u, n, to, got, idx, width=D):
                for t in range(n):
                    pool.indirect_dma_start(
                        out=to[:, u, t, 0:width] if len(to.shape) == 4 else to[:, u, t * width:(t + 1) * width],
                        out_offset=None, in_=table[:, :],
                        in_offset=bass.IndirectOffsetOnAxis(ap=idx[:, u, t:t + 1], axis=0),
                        bounds_check=NP - 1, oob_is_err=False).then_inc(got[u].sem, 16)

            def over_blocks(body):
                with pool.Fori(0, PAIRS_E) as i:
                    for u in range(2):
                        body(i * 2 + u, u, T)
                body(BLOCKS - 1, 0, TAIL)

            def table_stored(st, j):
                for u in range(2):
                    pool.wait_ge(*landed_before(st["store"][j][u], PAIRS_N))

            over_groups(pool, 1, ln_root(NS[0], 1))
            table_stored(NS[0], 0)
            table_stored(NS[0], 1)

            def edge0(b, u, n):
                e = E[0]
                hold(done(e["idx"], b), reuse(e["z"], b))
                gathers(0, tab_a, b, u, n, buf[0], e["src_got"], idx_s)
                gathers(0, tab_b, b, u, n, buf[1], e["dst_got"], idx_d)

            over_blocks(edge0)
            pool.wait_ge(s_degrees, 2)
            pool.wait_ge(s_bias_in, 48)

            def norms1(at):
                for u, g, i in at(0):
                    pool.tensor_tensor(norms[:, :, bass.ds(g * T, T)], degrees[:, :, bass.ds(g * T, T)],
                                       power[:, :].unsqueeze(2).to_broadcast([P, 2, T]), ALU.pow).then_inc(s_norms, 1)

            root1 = ln_root(NS[1], 8)

            def node1(at):
                root1(at)
                norms1(at)
            over_groups(pool, 8, node1)

            def plain_gather(k, table):
                def body(b, q, n):
                    hold(done(E[k]["idx"], b), reuse(E[k]["consumed"], b, ROW_SLOTS))
                    for t in range(n):
                        pool.indirect_dma_start(
                            out=rows_slot[q][:, t, 0:D], out_offset=None, in_=table[:, :],
                            in_offset=bass.IndirectOffsetOnAxis(ap=idx_slot[q][:, t:t + 1], axis=0),
                            bounds_check=NP - 1, oob_is_err=False).then_inc(E[k]["got"][q].sem, 16)

                with pool.Fori(0, QUADS) as i:
                    for q in range(ROW_SLOTS):
                        body(i * ROW_SLOTS + q, q, T)
                body(BLOCKS - 1, 0, TAIL)

            table_stored(NS[1], 1)
            plain_gather(1, tab_g1)
            over_groups(pool, 1, clear_sums(NS[2], NS[2]["sc"], 1))
            table_stored(NS[2], 0)
            plain_gather(2, tab_g2)
            root3, clear3 = ln_root(NS[3], 4), clear_sums(NS[3], NS[3]["sc"], 1)

            def node3(at):
                root3(at)
                clear3(at)
            over_groups(pool, 4, node3)
            table_stored(NS[3], 1)
            plain_gather(3, tab_h2)
            over_groups(pool, 1, clear_sums(NS[4], NS[4]["cat"], 1))
            table_stored(NS[4], 0)
            plain_gather(4, tab_h3)
            root5 = ln_root(NS[5], 4)

            def node5(at):
                root5(at)
                for u, g, i in at(9):
                    hold(done(NS[5]["nrm"], g))
                    pool.tensor_tensor(agg[:, bass.ds(g * T, T), D:AW], small[:, u, 5, :].unsqueeze(2),
                                       half[:, :].to_broadcast([P, T]).unsqueeze(2), ALU.pow
                                       ).then_inc(NS[5]["nrm2"].sem, 1)
            over_groups(pool, 9, node5)
            table_stored(NS[5], 0)
            table_stored(NS[5], 1)
            table_stored(NS[5], 2)
            pool.wait_ge(s_acc_zero, 16 * (TABLES + (TABLES - 2) * CLEARS))

            e = E[5]
            beyond_rows = pool.alloc_register("beyond_rows")
            pool.reg_mov(beyond_rows, 0)

            def pull(b, u, n):
                hold(done(e["idx"], b), reuse(e["contrib"], b))
                gathers(5, tab_wh, b, u, n, rows_u, e["src_got"], idx_s, AW)
                some = pool.value_load(beyond_i[0:1, bass.ds(b, 1)], min_val=0, max_val=1)
                with pool.If(some > 0):
                    for t in range(n):
                        pool.indirect_dma_start(
                            out=rows_v[:, u, t, :], out_offset=None, in_=tab_wh[:, :],
                            in_offset=bass.IndirectOffsetOnAxis(ap=idx_d[:, u, t:t + 1], axis=0),
                            bounds_check=NP - 1, oob_is_err=False).then_inc(s_beyond_rows, 16)
                    pool.reg_add(beyond_rows, beyond_rows, 16 * n)
                    hold((s_beyond_rows, beyond_rows))
                pool.sem_inc(e["dst_gathered"].sem, 1)

            def push(b, u, n):
                hold(done(e["oidx"], b), done(e["sum"], b))
                for t in range(n):
                    j = t % TABLES
                    if not (isinstance(b, int) and b == 0 and t < TABLES):
                        hold((e["table"][j], 16 * (b * (T // TABLES) + t // TABLES)))
                    pool.indirect_dma_start(
                        out=acc[j][:, :], out_offset=bass.IndirectOffsetOnAxis(ap=idx_o[:, u, t:t + 1], axis=0),
                        in_=buf[5][:, u, t * D:(t + 1) * D], in_offset=None,
                        bounds_check=NP + P - 1, oob_is_err=True, compute_op=ALU.add).then_inc(e["table"][j], 16)

            pull(0, 0, T)
            pull(1, 1, T)
            for b in range(2):
                push(b, b, T)
                pull(b + 2, b, T)
            with pool.Fori(1, PAIRS_E - 1) as i:
                for u in range(2):
                    push(i * 2 + u, u, T)
                    pull(i * 2 + u + 2, u, T)
            push(BLOCKS - 3, 0, T)
            pull(BLOCKS - 1, 0, TAIL)
            push(BLOCKS - 2, 1, T)
            push(BLOCKS - 1, 0, TAIL)

        @block.scalar
        def _(act):
            act.wait_ge(s_credit, 1)

            def copy(o, i):
                return act.activation(o, i, ACT.Copy)

            def ln_square(st, lag, xc, sq):
                def part(at):
                    for u, g, i in at(lag):
                        act.wait_ge(*done(st["xc"], g))
                        act.wait_ge(*reuse(st["v2"], g))
                        act.activation(slot(sq, u), slot(xc, u), ACT.Square).then_inc(st["sq"].sem, 1)
                return part

            act.wait_ge(s_exp_args, 1)
            act.activation(par_w[:, 2:5], par_w[:, 8:11], ACT.Exp).then_inc(s_act_setup, 1)
            act.activation(par_w[:, 5:6], par_w[:, 11:12], ACT.Exp).then_inc(s_act_setup, 1)
            act.activation(buf[4][:, 1, :], buf[4][:, 0, :], ACT.Exp).then_inc(s_act_setup, 1)
            act.wait_ge(s_act_setup, 3)
            act.activation(par_w[:, 6:7], par_w[:, 5:6], ACT.Ln, bias=1.0).then_inc(s_act_setup, 1)
            act.activation(buf[5][:, 0, :], buf[4][:, 1, :], ACT.Ln, bias=1.0).then_inc(s_act_setup, 1)

            act.wait_ge(s_setup_done, 1)
            square0 = ln_square(NS[0], 0, buf[2], buf[3])

            def node0(at):
                st = NS[0]
                for u, g, i in at(4):
                    act.wait_ge(*done(st["ht"], g))
                    act.wait_ge(*reuse(st["mm"], g))
                    copy(wide_t[:, u, 0:512], ps[u][:, :]).then_inc(st["htc"].sem, 1)
                for u, g, i in at(5):
                    act.wait_ge(*done(st["mm"], g))
                    act.wait_ge(*landed_before(st["store"][0][u], i))
                    act.wait_ge(*landed_before(st["store"][1][u], i))
                    act.wait_ge(*landed_before(st["store"][2][u], i))
                    copy(buf[5][:, u, :], ps[2 + u][:, :])
                    copy(buf[6][:, u, :], ps[4 + u][:, :])
                    copy(buf[7][:, u, :], ps[6 + u][:, :]).then_inc(st["o"].sem, 1)
                square0(at)
            over_groups(act, 5, node0)

            def copy_indices(k, used, both=False):
                e = E[k]

                def body(b, i, u, n):
                    act.wait_ge(*reuse(used, b))
                    if both:
                        copy(idx_d[:, u, 0:n], cols(dst_row, b, n))
                    copy(idx_s[:, u, 0:n], cols(src_row, b, n)).then_inc(e["idx"].sem, 1)
                return body

            def over_blocks(body):
                with act.Fori(0, PAIRS_E) as i:
                    for u in range(2):
                        body(i * 2 + u, i, u, T)
                body(BLOCKS - 1, PAIRS_E, 0, TAIL)

            e = E[0]
            copy0 = copy_indices(0, e["z"], True)

            def edge0(b, i, u, n):
                if n == T:
                    copy0(b + 1, i + u, 1 - u, T)
                act.wait_ge(*done(e["edge_t"], b))
                act.wait_ge(*reuse(e["z_mm"], b))
                copy(edge_t[:, u, :], ps[5][:, 0:P]).then_inc(e["edge_c"].sem, 1)
                act.wait_ge(*done(e["z"], b))
                act.wait_ge(*reuse(e["msg"], b))
                w = n * D
                act.activation(buf[3][:, u, 0:w], buf[2][:, u, 0:w], ACT.Exp)
                act.activation(buf[4][:, u, 0:w], buf[2][:, u, 0:w], ACT.Relu).then_inc(e["act"].sem, 1)

            copy0(0, 0, 0, T)
            over_blocks(edge0)

            act.wait_ge(E[0]["sums_done"], 1)

            def copy_plain_indices(k):
                def body(b, q, n):
                    act.wait_ge(*reuse(E[k]["consumed"], b, ROW_SLOTS))
                    copy(idx_slot[q][:, 0:n], cols(src_row, b, n)).then_inc(E[k]["idx"].sem, 1)

                with act.Fori(0, QUADS) as i:
                    for q in range(ROW_SLOTS):
                        body(i * ROW_SLOTS + q, q, T)
                body(BLOCKS - 1, 0, TAIL)

            square1 = ln_square(NS[1], 7, buf[7], rows_u_flat)

            def node1(at):
                st = NS[1]
                for u, g, i in at(6):
                    act.wait_ge(*done(st["et"], g))
                    act.wait_ge(*reuse(st["xmm"], g))
                    copy(wide[:, u, 0:512], ps[5][:, :]).then_inc(st["etc"].sem, 1)
                for u, g, i in at(2):
                    act.wait_ge(*done(st["at"], g))
                    act.wait_ge(*reuse(st["zmm"], g))
                    copy(wide_t[0:AW, u, 0:512], ps[u][0:AW, :])
                    copy(wide_t[0:AW, u, 512:1024], ps[2 + u][0:AW, :]).then_inc(st["atc"].sem, 1)
                for u, g, i in at(0):
                    act.wait_ge(*reuse(st["at"], g))
                    copy(rows_v[:, u, :, :], agg[:, bass.ds(g * T, T), :]).then_inc(st["ag"].sem, 1)
                for u, g, i in at(1):
                    act.wait_ge(*done(st["ag"], g))
                    act.sem_inc(s_act_hold, 1)
                    copy(agg[:, bass.ds(g * T, T), :], zeros[:, 0:AW].unsqueeze(1).to_broadcast([P, T, AW])
                         ).then_inc(st["zero"].sem, 1)
                for u, g, i in at(3):
                    act.wait_ge(*done(st["z"], g))
                    act.wait_ge(*reuse(st["e"], g))
                    act.activation(buf[3][:, u, :], buf[2][:, u, :], ACT.Exp)
                    act.activation(buf[4][:, u, :], buf[2][:, u, :], ACT.Relu).then_inc(st["act"].sem, 1)
                square1(at)
            over_groups(act, 7, node1)

            copy_plain_indices(1)
            def evac_paired(st, lag):
                def part(at):
                    for u, g, i in at(lag):
                        act.wait_ge(*done(st["st"], g))
                        act.wait_ge(*reuse(st["mm"], g))
                        copy(wide_t[:, u, 0:512], ps[u][:, :]).then_inc(st["stc"].sem, 1)
                return part

            over_groups(act, 2, evac_paired(NS[2], 2))
            copy_plain_indices(2)
            square3, evac3 = ln_square(NS[3], 3, buf[7], buf[3]), evac_paired(NS[3], 2)

            def node3(at):
                evac3(at)
                square3(at)
            over_groups(act, 3, node3)
            copy_plain_indices(3)

            def evac_cat(st, lag):
                def part(at):
                    for u, g, i in at(lag):
                        act.wait_ge(*done(st["ct"], g))
                        act.wait_ge(*reuse(st["mm"], g))
                        copy(wide_t[:, u, 0:512], ps[u][:, :])
                        copy(wide_t[:, u, 512:1024], ps[2 + u][:, :]).then_inc(st["ctc"].sem, 1)
                return part

            over_groups(act, 2, evac_cat(NS[4], 2))
            copy_plain_indices(4)
            square5, evac5 = ln_square(NS[5], 3, buf[7], buf[3]), evac_cat(NS[5], 2)

            def node5(at):
                st = NS[5]
                for u, g, i in at(7):
                    act.wait_ge(*done(st["ht"], g))
                    act.wait_ge(*reuse(st["wmm"], g))
                    copy(buf[2][:, u, :], ps[6][:, :]).then_inc(st["htc"].sem, 1)
                for u, g, i in at(8):
                    act.wait_ge(*done(st["wmm"], g))
                    act.wait_ge(*reuse(st["nrm"], g))
                    act.wait_ge(*landed_before(st["store"][2][u], i))
                    act.activation(buf[5][:, u, :], ps[7][:, :], ACT.Square)
                    act.activation(buf[1][:, u, :], ps[7][:, :], ACT.Copy, scale=par_w[:, 10:11])
                    copy(agg[:, bass.ds(g * T, T), 0:D], ps[7][:, :].rearrange("p (t d) -> p t d", d=D)
                         ).then_inc(st["wh"].sem, 1)
                evac5(at)
                square5(at)
            over_groups(act, 8, node5)

            e = E[5]
            copy5 = copy_indices(5, e["contrib"], True)

            def edge5(b, i, u, n):
                copy5(b, i, u, n)

            def edge5_out(b, u, n):
                act.wait_ge(*done(e["dedup"], b))
                for j in range(TABLES):
                    act.wait_ge(e["table"][j], 16 * (b * (T // TABLES) - T // TABLES))
                copy(buf[5][:, u, 0:n * D], ps[u][:, 0:n * D]).then_inc(e["sum"].sem, 1)

            def dst_rows(b, u):
                act.wait_ge(*done(e["dst_mm"], b * T + T - 1))
                act.wait_ge(*reuse(e["contrib"], b))
                some = act.value_load(beyond_i[0:1, bass.ds(b, 1)], min_val=0, max_val=1)
                with act.If(some < 1):
                    for h in range(2):
                        copy(rows_v[:, u, h * HALF:(h + 1) * HALF, :],
                             ps[2 + 2 * u + h][:, 0:HALF * AW].rearrange("p (t d) -> p t d", d=AW)
                             ).then_inc(s_rows_copied, 1)
                with act.If(some > 0):
                    act.sem_inc(s_rows_copied, 2)
                act.wait_ge(s_rows_copied, b * 2 + 2)
                act.sem_inc(e["dst_rows"].sem, 1)

            dst_rows(0, 0)
            edge5(0, 0, 0, T)
            edge5(1, 0, 1, T)
            for b in range(2):
                dst_rows(b + 1, 1 - b)
                act.wait_ge(*done(e["dedup"], b))
                copy(buf[5][:, b, :], ps[b][:, :]).then_inc(e["sum"].sem, 1)
                edge5(b + 2, 1, b, T)
            with act.Fori(1, PAIRS_E - 1) as i:
                for u in range(2):
                    dst_rows(i * 2 + u + 1, 1 - u)
                    edge5_out(i * 2 + u, u, T)
                    edge5(i * 2 + u + 2, i + 1, u, T)
            dst_rows(BLOCKS - 2, 1)
            edge5_out(BLOCKS - 3, 0, T)
            edge5(BLOCKS - 1, PAIRS_E, 0, TAIL)
            dst_rows(BLOCKS - 1, 0)
            edge5_out(BLOCKS - 2, 1, T)
            edge5_out(BLOCKS - 1, 0, TAIL)

        @block.tensor
        def _(pe):
            def pair(i):
                return [(u, i * 2 + u) for u in range(2)]

            pe.wait_ge(s_const, 1)
            for j in range(4):
                pe.wait_ge((s_src_staged, s_dst_staged)[min(j, 1)], 1)
                w = stage_f if j < 2 else wide[:, j - 2, 0:512].rearrange("p (b q) -> p b q", b=4)
                for q in range(4):
                    m = pe.transpose(ps[j][:, q * P:(q + 1) * P], w[:, q, :], ident[:, :])
                m.then_inc(s_pe_setup, 1)
            for j in range(2):
                pe.wait_ge(s_spans, j + 1)
                w = wide_t[:, j, 0:512].rearrange("p (b q) -> p b q", b=4)
                for q in range(4):
                    m = pe.matmul(ps[4 + j][:, q * P:(q + 1) * P], w[:, q, :], ident[:, :], start=True, stop=True)
                m.then_inc(s_pe_setup, 1)
            pe.wait_ge(s_in, 16 * N_LOADS)
            for q in range(4):
                m = pe.transpose(ps[6][:, q * D:(q + 1) * D], nat[:, q, :], ident[0:D, 0:D])
            for q in range(4, 7):
                m = pe.transpose(ps[6][:, q * D:(q + 1) * D], nat[:, q, :], ident[0:D, 0:D])
            m.then_inc(s_pe_setup, 1)
            pe.transpose(ps[7][:, 0:D], w1e_nat[:, :, :].rearrange("p t f -> p (t f)"), ident[0:D, 0:D]
                         ).then_inc(s_pe_setup, 1)
            pe.wait_ge(s_wt, 1)
            pe.matmul(ps[7][0:AW, D:2 * D], w2m_nat[:, :], wt[0:D, WUM, :], start=True, stop=True
                      ).then_inc(s_pe_setup, 1)

            def add_bias(o, row, n=T):
                pe.matmul(o[:, 0:n * D], ones_b[0:3, :], bias3[:, row:row + 1, :].to_broadcast([3, n, D]),
                          start=True, stop=False, skip_group_check=True)

            def products_paired(o, lhs, w, row=None):
                if row is not None:
                    add_bias(o, row)
                for q in range(T // 2):
                    m = pe.matmul(o[:, q * P:(q + 1) * P], lhs[:, q * P:(q + 1) * P], w,
                                  start=row is None, stop=True, skip_group_check=True)
                return m

            def products(o, lhs, k, w, row=None):
                if row is not None:
                    add_bias(o, row)
                for t in range(T):
                    m = pe.matmul(o[:, t * D:(t + 1) * D], lhs[0:k, t * P:(t + 1) * P], w,
                                  start=row is None, stop=True, skip_group_check=True)
                return m

            def transposes_paired(o, x):
                for q in range(T // 2):
                    m = pe.transpose(o[:, q * P:(q + 1) * P], x[:, q * P:(q + 1) * P], ident[:, :])
                return m

            pe.wait_ge(s_setup_done, 1)
            pe.wait_ge(s_bias_in, 48)
            def node0(at):
                st = NS[0]
                for u, g, i in at(3):
                    pe.wait_ge(*done(st["h"], g))
                    pe.wait_ge(*reuse(st["htc"], g))
                    transposes_paired(ps[u], buf[4][:, u, :]).then_inc(st["ht"].sem, 1)
                for u, g, i in at(4):
                    pe.wait_ge(*done(st["htc"], g))
                    pe.wait_ge(*reuse(st["o"], g))
                    products_paired(ps[2 + u], wide_t[:, u, 0:512], w_pair[:, PA, :])
                    products_paired(ps[4 + u], wide_t[:, u, 0:512], w_pair[:, PB, :], B1M)
                    products_paired(ps[6 + u], wide_t[:, u, 0:512], w_pair[:, PQ, :], B1U).then_inc(st["mm"].sem, 1)
            over_groups(pe, 4, node0)

            slow = pe.alloc_register("slow_pe")
            pe.reg_mov(slow, 0)

            def segment(k, msg, width, weights=False):
                e = E[k]

                def body(b, u, n, tile_hook=None):
                    some = beyond_flag(pe, b)
                    for t in range(n):
                        k_ = b * T + t
                        kt = k_
                        pe.wait_ge(*reuse(e["added"], kt, SEG))
                        if t % HALF == 0:
                            pe.wait_ge(*done(e["hot"], b * 2 + t // HALF))
                            pe.wait_ge(*done(e["spread"], b * 2 + t // HALF))
                        ww = WINDOW * width
                        pe.matmul(seg_ps[t % SEG][:, 0:ww], hot_half[t // HALF][:, t % HALF, :],
                                  wide_t[:, t // HALF, t % HALF * ww:(t % HALF + 1) * ww],
                                  start=True, stop=True).then_inc(e["seg"].sem, 1)
                        if tile_hook:
                            tile_hook(k_, t)
                    beyond(pe, b, some, lambda t: slow_step(msg, u, t, width), n)
                return body

            def slow_step(msg, u, t, width):
                def step(tile):
                    pe.reg_add(slow, slow, 1)
                    pe.wait_ge(s_slow_built, slow)
                    pe.matmul(ps[0][:, 0:width], hot_x[:, :], msg[u][:, t, 0:width], start=True, stop=True
                              ).then_inc(s_slow_mul, 1)
                return step

            def over_blocks(body):
                with pe.Fori(0, PAIRS_E) as i:
                    for u in range(2):
                        body(i * 2 + u, i, u, T)
                body(BLOCKS - 1, PAIRS_E, 0, TAIL)

            e = E[0]
            seg0 = segment(0, rows_slot, AW)
            pe.wait_ge(*done(NS[0]["o"], GROUPS - 1))
            pe.matmul(ps[6][:, 0:NODE_TILES], zeros_b[:, 0:P], zeros_b[:, 0:NODE_TILES],
                      start=True, stop=False, skip_group_check=True)

            def hist(k_, t):
                pe.wait_ge(*done(e["hist_hot"], k_))
                pe.matmul(ps[6][:, 0:NODE_TILES], hot_lo[:, t % 2, :], hot_hi[:, t % 2, :],
                          start=False, stop=False, skip_group_check=True).then_inc(e["hist"].sem, 1)

            def edge0(b, i, u, n):
                pe.wait_ge(*landed(e["edge_got"][u], i))
                pe.wait_ge(*done(e["edge_c"], b - 1))
                pe.transpose(ps[5][:, 0:P], edge_in[:, u, :], ident[:, :]).then_inc(e["edge_t"].sem, 1)
                pe.wait_ge(*done(e["edge_c"], b))
                pe.wait_ge(*reuse(e["z"], b))
                pe.matmul(ps[3 + u][:, 0:n * D], edge_t[:, u, :],
                          w1e_diag[:, 0:n, :].rearrange("p t d -> p (t d)"), start=True, stop=True
                          ).then_inc(e["z_mm"].sem, 1)
                pe.wait_ge(*done(e["msg"], b))
                seg0(b, u, n, hist)

            over_blocks(edge0)
            pe.matmul(ps[6][:, 0:NODE_TILES], zeros_b[:, 0:P], zeros_b[:, 0:NODE_TILES],
                      start=False, stop=True, skip_group_check=True).then_inc(e["hist"].sem, 1)

            def node1(at):
                st = NS[1]
                for u, g, i in at(5):
                    pe.wait_ge(*done(st["e"], g))
                    pe.wait_ge(*done(st["etc"], g - 1))
                    transposes_paired(ps[5], buf[5][:, u, :]).then_inc(st["et"].sem, 1)
                for u, g, i in at(1):
                    pe.wait_ge(*done(st["ag"], g))
                    pe.wait_ge(*reuse(st["atc"], g))
                    for t in range(T):
                        m = pe.transpose(ps[(t // 4) * 2 + u][0:AW, (t % 4) * P:(t % 4 + 1) * P],
                                         rows_v[:, u, t, :], ident[:, :])
                    m.then_inc(st["at"].sem, 1)
                for u, g, i in at(6):
                    pe.wait_ge(*done(st["etc"], g))
                    pe.wait_ge(*reuse(st["x"], g))
                    products_paired(ps[6 + u], wide[:, u, 0:512], w_pair[:, PU2, :], B2U).then_inc(st["xmm"].sem, 1)
                for u, g, i in at(2):
                    pe.wait_ge(*done(st["atc"], g))
                    pe.wait_ge(*done(st["z"], g - 1))
                    products(ps[4], wide_t[:, u, :], AW, w_upd_agg[:, :]).then_inc(st["zmm"].sem, 1)
            over_groups(pe, 6, node1)

            def plain_segment(k):
                seg = segment(k, rows_slot, D)

                def body(b, i, q, n):
                    pe.wait_ge(E[k]["got"][q].sem, E[k]["got"][q].base + gathered(i) + 16 * n)
                    seg(b, q, n)

                with pe.Fori(0, QUADS) as i:
                    for q in range(ROW_SLOTS):
                        body(i * ROW_SLOTS + q, i, q, T)
                body(BLOCKS - 1, QUADS, 0, TAIL)

            def graph_conv(st, row, w, used):
                def part(at):
                    for u, g, i in at(1):
                        pe.wait_ge(*done(st["sc"], g))
                        pe.wait_ge(*reuse(st["stc"], g))
                        transposes_paired(ps[u], buf[5][:, u, :]).then_inc(st["st"].sem, 1)
                    for u, g, i in at(2):
                        pe.wait_ge(*done(st["stc"], g))
                        pe.wait_ge(*reuse(used, g))
                        products_paired(ps[4 + u], wide_t[:, u, 0:512], w_pair[:, w, :], row
                                        ).then_inc(st["mm"].sem, 1)
                over_groups(pe, 2, part)

            plain_segment(1)
            graph_conv(NS[2], BG1, PG1, NS[2]["o"])
            plain_segment(2)
            graph_conv(NS[3], BG2, PG2, NS[3]["x"])
            plain_segment(3)

            def conv_cat(st, w, row, used):
                def part(at):
                    for u, g, i in at(1):
                        pe.wait_ge(*done(st["cat"], g))
                        pe.wait_ge(*landed(st["load"][0][u], i))
                        pe.wait_ge(*reuse(st["ctc"], g))
                        for t in range(T):
                            m = pe.transpose(ps[(t // 4) * 2 + u][:, (t % 4) * P:(t % 4 + 1) * P],
                                             wide[:, u, t * P:(t + 1) * P], ident[:, :])
                        m.then_inc(st["ct"].sem, 1)
                    for u, g, i in at(2):
                        pe.wait_ge(*done(st["ctc"], g))
                        pe.wait_ge(*reuse(used, g))
                        products(ps[4 + u], wide_t[:, u, :], P, wt[:, w, :], row).then_inc(st["mm"].sem, 1)
                return part

            over_groups(pe, 2, conv_cat(NS[4], WC1, BR1, NS[4]["o"]))
            plain_segment(4)
            conv5 = conv_cat(NS[5], WC2, BR2, NS[5]["x"])

            def node5(at):
                st = NS[5]
                for u, g, i in at(6):
                    pe.wait_ge(*done(st["h"], g))
                    pe.wait_ge(*done(st["htc"], g - 1))
                    transposes_paired(ps[6], buf[4][:, u, :]).then_inc(st["ht"].sem, 1)
                conv5(at)
                for u, g, i in at(7):
                    pe.wait_ge(*done(st["htc"], g))
                    pe.wait_ge(*done(st["wh"], g - 1))
                    products_paired(ps[7], buf[2][:, u, :], w_pair[:, PL3, :], BL3).then_inc(st["wmm"].sem, 1)
            over_groups(pe, 7, node5)

            e = E[5]

            def firsts(b):
                _, first = nc.values_load_multi_w_load_instructions(
                    first_row[0:1, bass.ds(b * T, T)], engines=[mybir.EngineType.PE], min_val=0,
                    max_val=NODE_TILES - 1, skip_runtime_bounds_check_because="dst names a node")
                return first

            def dst_product(b, u, t, first):
                k_ = b * T + t
                pe.wait_ge(*done(e["dst_hot"], k_))
                if t == 0:
                    pe.wait_ge(*reuse(e["dst_rows"], b))
                for w in range(WINDOW):
                    m = pe.matmul(ps[2 + 2 * u + t // HALF][:, t % HALF * AW:(t % HALF + 1) * AW],
                                  dst_hot[t % 4][:, w * P:(w + 1) * P],
                                  agg[:, bass.ds(first[t] + w, 1), :].rearrange("p o d -> p (o d)"),
                                  start=w == 0, stop=w == WINDOW - 1)
                m.then_inc(e["dst_mm"].sem, 1)

            def edge5(b, i, u, n):
                more = n == T
                first = firsts(b + 1) if more else None
                if more:
                    for t in range(T):
                        dst_product(b + 1, 1 - u, t, first)
                pe.wait_ge(*reuse(e["sum"], b))
                for t in range(n):
                    pe.wait_ge(*done(e["same"], b * T + t))
                    m = pe.matmul(ps[u][:, t * D:(t + 1) * D], same[:, t % 4, :], buf[4][:, u, t * D:(t + 1) * D],
                                  start=True, stop=True)
                    m.then_inc(e["same_used"].sem, 1)
                pe.wait_ge(*done(e["same_used"], b * T + n - 1))
                pe.sem_inc(e["dedup"].sem, 1)

            pe.wait_ge(*done(NS[5]["nrm2"], GROUPS - 1))
            first0 = firsts(0)
            for t in range(T):
                dst_product(0, 0, t, first0)
            over_blocks(edge5)

        @block.vector
        def _(dve):
            count = [0]

            def link(ins, wait=True):
                count[0] += 1
                ins.then_inc(s_dve, 1)
                if wait:
                    dve.wait_ge(s_dve, count[0])
                return count[0]

            def pair(i):
                return [(u, i * 2 + u) for u in range(2)]

            V = nc.vector
            dve.wait_ge(s_credit, 1)
            dve.wait_ge(s_const, 1)
            dve.wait_ge(s_idx_in, 16 * 15)
            link(V.tensor_copy(stage_f[:, :, :], stage_i[0][:, :, :]))
            dve.sem_inc(s_src_staged, 1)
            dve.wait_ge(s_pe_setup, 1)
            link(V.tensor_copy(src_f[:, :, :], ps[0][:, :].rearrange("p (b q) -> p b q", b=4)))
            link(V.tensor_copy(stage_f[:, :, :], stage_i[1][:, :, :]))
            dve.sem_inc(s_dst_staged, 1)
            dve.wait_ge(s_pe_setup, 2)
            link(V.tensor_copy(dst_f[:, :, :], ps[1][:, :].rearrange("p (b q) -> p b q", b=4)))
            dve.wait_ge(s_pe_setup, 4)
            link(V.tensor_copy(ew[:, :], ps[2][:, :]))
            link(V.tensor_copy(buf[5][:, 1, :], ps[3][:, :]))
            link(V.tensor_reduce(first_i[:, :], stage_i[2][:, :, :], AX_X, ALU.min))
            link(V.tensor_reduce(last_i[:, :], stage_i[1][:, :, :], AX_X, ALU.max))
            link(V.tensor_scalar(first_i[:, :], first_i[:, :], float(N - 1), None, ALU.min))
            link(V.tensor_scalar(last_i[:, :], last_i[:, :], 0.0, None, ALU.max))
            for k_, x in enumerate((first_i, last_i)):
                link(V.tensor_scalar(x[:, :], x[:, :], 7, None, ALU.arith_shift_right))
                link(V.tensor_copy(span_f[:, :, k_], x[:, :]))
                w = wide_t[:, k_, 0:512].rearrange("p (b q) -> p b q", b=4)
                for q in range(4):
                    link(V.tensor_scalar(w[:, q, :], ones[:, :], span_f[:, q, k_:k_ + 1], None, ALU.mult))
                dve.sem_inc(s_spans, 1)
            dve.wait_ge(s_pe_setup, 6)
            link(V.tensor_copy(first_f[:, :], ps[4][:, :]))
            link(V.tensor_copy(last_f[:, :], ps[5][:, :]))
            link(V.tensor_copy(first_row[:, :], first_f[0:1, :]))
            ia, ib = stage_i[0][:, :, :].rearrange("p b q -> p (b q)"), stage_i[1][:, :, :].rearrange("p b q -> p (b q)")
            dst_all = dst_f[:, :, :].rearrange("p b q -> p (b q)")
            link(V.tensor_scalar(ia, dst_all, 0.0, None, ALU.max))
            link(V.tensor_scalar(ib, ia, P - 1, None, ALU.bitwise_and))
            link(V.tensor_copy(lane[:, :], ib))
            link(V.scalar_tensor_tensor(out=window_tile[:, :], in0=first_f[:, :], scalar=float(-P), in1=dst_all,
                                        op0=ALU.mult, op1=ALU.add))
            link(V.tensor_tensor(window_tile[:, :], window_tile[:, :], lane[:, :], ALU.subtract))
            link(V.tensor_scalar(window_tile[:, :], window_tile[:, :], 1.0 / P, None, ALU.mult))
            link(V.tensor_scalar(beyond_f[:, :], first_f[0:1, :], float(WINDOW + 1), None, ALU.add))
            link(V.tensor_scalar(last_f[0:1, :], last_f[0:1, :], 1.0, None, ALU.add))
            link(V.tensor_tensor(xhi_row[:, :], beyond_f[:, :], last_f[0:1, :], ALU.max))
            link(V.tensor_tensor(beyond_f[:, :], last_f[0:1, :], beyond_f[:, :], ALU.is_ge))
            link(V.tensor_reduce(beyond_i[:, :], beyond_f[:, :].rearrange("o (b t) -> o b t", t=T), AX_X, ALU.max))
            ic = stage_i[2][:, :, :].rearrange("p b q -> p (b q)")
            for x, row in ((src_f, src_row), (dst_f, dst_row)):
                xf = x[:, :, :].rearrange("p b q -> p (b q)")
                link(V.tensor_scalar(ia, xf, 0.0, None, ALU.max))
                link(V.tensor_scalar(ib, ia, P - 1, 3, ALU.bitwise_and, ALU.logical_shift_left))
                link(V.tensor_scalar(ic, ia, 7, T - 1, ALU.arith_shift_right, ALU.bitwise_and))
                link(V.tensor_tensor(ib, ib, ic, ALU.add))
                link(V.tensor_scalar(ic, ia, 10, None, ALU.arith_shift_right))
                link(V.tensor_scalar(ic, ic, P * T, None, ALU.mult))
                link(V.tensor_tensor(row[:, :], ib, ic, ALU.add))
            link(V.tensor_copy(ia, src_f[:, :, :].rearrange("p b q -> p (b q)")))
            link(V.tensor_scalar(ib, ia, P - 1, None, ALU.bitwise_and))
            link(V.tensor_copy(src_lo[:, :], ib))
            link(V.tensor_scalar(ib, ia, 7, None, ALU.arith_shift_right))
            link(V.tensor_copy(src_hi[:, :], ib))
            sf = src_f[:, :, :].rearrange("p b q -> p (b q)")
            dve.wait_ge(s_in, 16 * N_LOADS)
            link(V.tensor_reduce(par_w[:, 0:1], par[:, 2:5], AX_X, ALU.max))
            link(V.tensor_scalar(par_w[:, 8:11], par[:, 2:5], par_w[:, 0:1], None, ALU.subtract))
            link(V.tensor_scalar(par_w[:, 12:13], par[:, 5:6], -1.0, None, ALU.mult))
            link(V.tensor_tensor(par_w[:, 11:12], par_w[:, 12:13], par[:, 5:6], ALU.min))
            link(V.tensor_scalar(par_w[:, 13:14], par[:, 5:6], 0.0, None, ALU.max))
            link(V.tensor_scalar(buf[6][:, 0, :], buf[5][:, 1, :], par[:, 0:1], par[:, 1:2], ALU.mult, ALU.add))
            link(V.tensor_scalar(buf[6][:, 1, :], buf[6][:, 0, :], -1.0, None, ALU.mult))
            link(V.tensor_tensor(buf[4][:, 0, :], buf[6][:, 0, :], buf[6][:, 1, :], ALU.min))
            dve.sem_inc(s_exp_args, 1)
            dve.wait_ge(s_act_setup, 5)
            link(V.scalar_tensor_tensor(out=base[:, :], in0=buf[6][:, 0, :], scalar=0.0, in1=buf[5][:, 0, :],
                                        op0=ALU.max, op1=ALU.add))
            link(V.tensor_tensor(base[:, :], base[:, :], ew[:, :], ALU.mult))
            link(V.tensor_tensor(buf[6][:, 0, :], sf, dst_f[:, :, :].rearrange("p b q -> p (b q)"), ALU.not_equal))
            link(V.tensor_tensor(base[:, :], base[:, :], buf[6][:, 0, :], ALU.mult))
            link(V.tensor_reduce(par_w[:, 0:1], par_w[:, 2:5], AX_X, ALU.add))
            link(V.reciprocal(par_w[:, 1:2], par_w[:, 0:1]))
            link(V.tensor_tensor(par_w[:, 7:8], par_w[:, 6:7], par_w[:, 13:14], ALU.add))
            link(V.tensor_tensor(par_w[:, 1:2], par_w[:, 1:2], par_w[:, 7:8], ALU.mult))
            link(V.tensor_scalar(par_w[:, 8:11], par_w[:, 2:5], par_w[:, 1:2], None, ALU.mult))
            dve.wait_ge(s_pe_setup, 8)
            link(V.tensor_copy(wt[:, :, :], ps[6][:, 0:7 * D].rearrange("p (w d) -> p w d", d=D)))
            for h in range(2):
                r = slice(h * D, (h + 1) * D)
                link(V.tensor_copy(w_pair[r, PA:PU2 + 1, r], wt[r, WA:WU2 + 1, :]))
            link(V.tensor_copy(w1e_t[:, :], ps[7][:, 0:D]))
            dve.sem_inc(s_wt, 1)
            for t in range(T):
                link(V.tensor_scalar(w1e_diag[:, t, :], w1e_t[:, :], block_mask[:, t:t + 1], None, ALU.mult))
            dve.wait_ge(s_pe_setup, 9)
            link(V.tensor_copy(w_upd_agg[:, :], ps[7][0:AW, D:2 * D]))
            whole_bias, left, back = bias.rearrange("o b d -> o (b d)"), buf[6][0:1, 0, :], buf[6][0:1, 1, :]
            for k in range(3):
                part = bias_parts[:, k * 8 * D:(k + 1) * 8 * D]
                link(V.tensor_copy(part, whole_bias if k == 0 else left))
                if k < 2:
                    link(V.tensor_copy(back, part))
                    link(V.tensor_tensor(left, whole_bias if k == 0 else left, back, ALU.subtract))
            dve.sem_inc(s_bias_split, 1)
            link(V.memset(deg_out, 1.0))
            dve.sem_inc(s_setup_done, 1)

            def ln_centre(st, lag, x, xc, ready=None):
                def part(at):
                    for u, g, i in at(lag):
                        if ready:
                            ready(u, g, i)
                        V.tensor_reduce(small[:, u, 0, :], slot(x, u), AX_X, ALU.add).then_inc(st["s"].sem, 1)
                        dve.wait_ge(*done(st["s"], g))
                        dve.wait_ge(*reuse(st["sq"], g))
                        V.scalar_tensor_tensor(out=slot(xc, u), in0=slot(x, u), scalar=float(D),
                                               in1=over_features(small[:, u, 0, :]), op0=ALU.mult,
                                               op1=ALU.subtract).then_inc(st["xc"].sem, 1)
                return part

            def ln_var(st, lag, sq, norm=False):
                def part(at):
                    for u, g, i in at(lag):
                        dve.wait_ge(*done(st["sq"], g))
                        V.tensor_reduce(small[:, u, 6, :], slot(sq, u), AX_X, ALU.add).then_inc(st["v2"].sem, 1)
                        dve.wait_ge(*done(st["v2"], g))
                        dve.wait_ge(*reuse(st["r"], g))
                        if not norm:
                            V.tensor_scalar(small[:, u, 3, :], small[:, u, 6, :], 1.0 / D, D * D * EPS,
                                            ALU.mult, ALU.add).then_inc(st["v"].sem, 1)
                        else:
                            V.tensor_scalar(small[:, u, 2, :], small[:, u, 6, :], 1.0 / D, D * D * EPS,
                                            ALU.mult, ALU.add).then_inc(s_norm_self, 1)
                            dve.wait_ge(s_norm_self, g + 1)
                            V.tensor_tensor(small[:, u, 3, :], small[:, u, 2, :], cols(deg_out, g, T), ALU.mult
                                            ).then_inc(st["v"].sem, 1)
                return part

            def ln_out(st, lag, xc, to, freed):
                def part(at):
                    for u, g, i in at(lag):
                        dve.wait_ge(*done(st["r"], g))
                        freed(u, g, i)
                        V.scalar_tensor_tensor(out=to(u), in0=slot(xc, u), scalar=0.0,
                                               in1=over_features(small[:, u, 4, :]), op0=ALU.max, op1=ALU.mult
                                               ).then_inc(st["h"].sem, 1)
                return part

            centre0 = ln_centre(NS[0], 0, buf[0], buf[2], lambda u, g, i: dve.wait_ge(*landed(NS[0]["load"][0][u], i)))
            var0 = ln_var(NS[0], 1, buf[3])
            out0 = ln_out(NS[0], 2, buf[2], lambda u: slot(buf[4], u), lambda u, g, i: dve.wait_ge(*reuse(NS[0]["ht"], g)))

            def node0(at):
                out0(at)
                var0(at)
                centre0(at)
            over_groups(dve, 2, node0)

            slow = dve.alloc_register("slow_dve")
            dve.reg_mov(slow, 0)

            def segment(k, msg, width, weighted):
                e = E[k]

                def build(b, half):
                    full = [P, HALF, P]
                    V.tensor_tensor(hot_half[half], iota_node[:, :].unsqueeze(1).to_broadcast(full),
                                    lane[:, bass.ds(b * T + half * HALF, HALF)].unsqueeze(2).to_broadcast(full),
                                    ALU.is_equal).then_inc(e["hot"].sem, 1)

                def masks(b, n):
                    for w in range(WINDOW):
                        m = V.scalar_tensor_tensor(out=in_tile[:, w, 0:n], in0=cols(window_tile, b, n), scalar=float(w),
                                                   in1=cols(ew, b, n) if weighted else ones[:, 0:n],
                                                   op0=ALU.is_equal, op1=ALU.mult)
                    m.then_inc(e["mask"].sem, 1)

                def spread(b, u, half, n):
                    m = n - half * HALF if half else min(n, HALF)
                    full = [P, m, WINDOW, width]
                    V.tensor_tensor(
                        wide_t[:, half, 0:m * WINDOW * width].rearrange("p (t w d) -> p t w d", w=WINDOW, d=width),
                        msg[u][:, half * HALF:half * HALF + m, 0:width].unsqueeze(2).to_broadcast(full),
                        in_tile[:, :, half * HALF:half * HALF + m].rearrange("p w t -> p t w").unsqueeze(3).to_broadcast(full),
                        ALU.mult).then_inc(e["spread"].sem, 1)

                def add(k_, t, first):
                    dve.wait_ge(*done(e["seg"], k_))
                    dve.wait_ge(*done(e["added"], k_ - 1))
                    o = agg[:, bass.ds(first, WINDOW), 0:width]
                    V.tensor_tensor(o, o, seg_ps[t % SEG][:, 0:WINDOW * width].rearrange("p (w d) -> p w d", d=width),
                                    ALU.add).then_inc(e["added"].sem, 1)

                def slow_step(b, t):
                    k_ = b * T + t

                    def step(tile):
                        dve.reg_add(slow, slow, 1)
                        V.tensor_scalar(hot_x[:, :], iota_node[:, 0:P], tile_base[:, bass.ds(tile, 1)],
                                        dst_f[:, :, :].rearrange("p b q -> p (b q)")[:, bass.ds(k_, 1)],
                                        ALU.add, ALU.is_equal).then_inc(s_slow_self, 1)
                        dve.wait_ge(s_slow_self, slow)
                        if weighted:
                            V.tensor_scalar(hot_x[:, :], hot_x[:, :], ew[:, bass.ds(k_, 1)], None, ALU.mult
                                            ).then_inc(s_slow_built, 1)
                        else:
                            V.tensor_copy(hot_x[:, :], hot_x[:, :]).then_inc(s_slow_built, 1)
                        dve.wait_ge(s_slow_mul, slow)
                        o = agg[:, bass.ds(tile, 1), 0:width].rearrange("p o d -> p (o d)")
                        V.tensor_tensor(o, o, ps[0][:, 0:width], ALU.add).then_inc(s_slow_added, 1)
                        dve.wait_ge(s_slow_added, slow)
                    return step

                def body(b, u, n, rows_ready, tile_hook=lambda k_, t: None):
                    masks(b, n)
                    build(b, 0)
                    for t in range(2):
                        tile_hook(b * T + t, t)
                    dve.wait_ge(*done(e["mask"], b))
                    dve.wait_ge(*rows_ready)
                    spread(b, u, 0, n)
                    _, first = nc.values_load_multi_w_load_instructions(
                        first_row[0:1, bass.ds(b * T, n)], engines=[mybir.EngineType.DVE], min_val=0,
                        max_val=NODE_TILES - 1, skip_runtime_bounds_check_because="dst names a node")
                    some = beyond_flag(dve, b)
                    build(b, 1)
                    spread(b, u, 1, n)
                    for t in range(2, n + 2):
                        if t < n:
                            tile_hook(b * T + t, t)
                        add(b * T + t - 2, t - 2, first[t - 2])
                    dve.wait_ge(*done(e["added"], b * T + n - 1))
                    dve.sem_inc(s_dve_hold, 1)
                    beyond(dve, b, some, lambda t: slow_step(b, t), n)
                    dve.sem_inc(e["consumed"].sem, 1)
                return body

            def over_blocks(body):
                with dve.Fori(0, PAIRS_E) as i:
                    for u in range(2):
                        body(i * 2 + u, i, u, T)
                body(BLOCKS - 1, PAIRS_E, 0, TAIL)

            e = E[0]
            seg0 = segment(0, rows_slot, AW, False)

            def hist_hot(k_, t):
                dve.wait_ge(*reuse(e["hist"], k_))
                V.tensor_scalar(hot_lo[:, t % 2, :], iota_node[:, 0:P], src_lo[:, bass.ds(k_, 1)], None, ALU.is_equal)
                V.tensor_scalar(hot_hi[:, t % 2, :], iota_tile[:, :], src_hi[:, bass.ds(k_, 1)], None, ALU.is_equal
                                ).then_inc(e["hist_hot"].sem, 1)

            def edge0(b, i, u, n):
                w = n * D
                dve.wait_ge(e["src_got"][u].sem, e["src_got"][u].base + gathered(i) + 16 * n)
                dve.wait_ge(e["dst_got"][u].sem, e["dst_got"][u].base + gathered(i) + 16 * n)
                dve.wait_ge(*reuse(e["act"], b))
                dve.wait_ge(*reuse(e["z"], b))
                V.tensor_tensor(buf[6][:, u, 0:w], buf[0][:, u, 0:w], buf[1][:, u, 0:w], ALU.add
                                ).then_inc(s_z_self, 1)
                dve.wait_ge(s_z_self, b + 1)
                dve.wait_ge(*done(e["z_mm"], b))
                V.tensor_tensor(buf[2][:, u, 0:w], buf[6][:, u, 0:w], ps[3 + u][:, 0:w], ALU.add).then_inc(e["z"].sem, 1)
                dve.wait_ge(*done(e["act"], b))
                V.tensor_scalar(buf[3][:, u, 0:w], buf[3][:, u, 0:w], 1.0, -1.0, ALU.min, ALU.add
                                ).then_inc(s_elu_self, 1)
                dve.wait_ge(s_elu_self, b + 1)
                dve.wait_ge(*reuse(e["consumed"], b))
                V.tensor_tensor(rows_u[:, u, 0:n, 0:D], buf[3][:, u, 0:w].rearrange("p (t d) -> p t d", d=D),
                                buf[4][:, u, 0:w].rearrange("p (t d) -> p t d", d=D), ALU.add).then_inc(e["msg"].sem, 1)
                seg0(b, u, n, done(e["msg"], b), hist_hot)

            dve.wait_ge(s_agg0, 1)
            over_blocks(edge0)
            dve.wait_ge(*done(e["hist"], ET))
            V.tensor_scalar(deg_out[:, 0:NODE_TILES], ps[6][:, 0:NODE_TILES], 1.0, None, ALU.max).then_inc(s_degrees, 1)
            V.tensor_scalar(deg_in, agg[:, :, D:AW].rearrange("p t o -> p (t o)"), 1.0, None, ALU.max
                            ).then_inc(s_degrees, 1)
            dve.wait_ge(s_degrees, 2)
            dve.sem_inc(e["sums_done"], 1)

            centre1 = ln_centre(NS[1], 7, buf[6], buf[7], lambda u, g, i: dve.wait_ge(*done(NS[1]["x"], g)))
            var1 = ln_var(NS[1], 8, rows_u_flat, True)
            out1 = ln_out(NS[1], 9, buf[7], lambda u: slot(wide, u, D, 512),
                          lambda u, g, i: dve.wait_ge(*landed_before(NS[1]["store"][1][u], i)))

            def node1(at):
                st = NS[1]
                out1(at)
                var1(at)
                for u, g, i in at(3):
                    dve.wait_ge(*done(st["zmm"], g))
                    dve.wait_ge(*landed(st["load"][1][u], i))
                    dve.wait_ge(*reuse(st["act"], g))
                    V.tensor_tensor(buf[2][:, u, :], ps[4][:, :], buf[1][:, u, :], ALU.add).then_inc(st["z"].sem, 1)
                for u, g, i in at(7):
                    dve.wait_ge(*done(st["xmm"], g))
                    dve.wait_ge(*landed(st["load"][0][u], i))
                    dve.wait_ge(*landed_before(st["store"][0][u], i))
                    V.tensor_tensor(buf[6][:, u, :], ps[6 + u][:, :], buf[0][:, u, :], ALU.add
                                    ).then_inc(st["x"].sem, 1)
                for u, g, i in at(4):
                    dve.wait_ge(*done(st["act"], g))
                    V.tensor_scalar(buf[3][:, u, :], buf[3][:, u, :], 1.0, -1.0, ALU.min, ALU.add
                                    ).then_inc(st["e1"].sem, 1)
                centre1(at)
                for u, g, i in at(4):
                    dve.wait_ge(*done(st["e1"], g))
                    dve.wait_ge(*reuse(st["et"], g))
                    V.tensor_tensor(buf[5][:, u, :], buf[3][:, u, :], buf[4][:, u, :], ALU.add
                                    ).then_inc(st["e"].sem, 1)
            over_groups(dve, 9, node1)

            def plain_segment(k, weighted):
                seg = segment(k, rows_slot, D, weighted)

                def body(b, i, q, n):
                    got = E[k]["got"][q]
                    seg(b, q, n, (got.sem, got.base + gathered(i) + 16 * n))

                with dve.Fori(0, QUADS) as i:
                    for q in range(ROW_SLOTS):
                        body(i * ROW_SLOTS + q, i, q, T)
                body(BLOCKS - 1, QUADS, 0, TAIL)

            def sums_cleared(st):
                dve.wait_ge(*done(st["zero"], GROUPS - 1))

            def scaled_sums(st):
                def part(at):
                    for u, g, i in at(0):
                        dve.wait_ge(*reuse(st["st"], g))
                        V.tensor_tensor(slot(buf[5], u), agg[:, bass.ds(g * T, T), 0:D],
                                        over_features(cols(norm_in, g, T)), ALU.mult).then_inc(st["sc"].sem, 1)
                return part

            sums_cleared(NS[1])
            plain_segment(1, False)
            scaled2 = scaled_sums(NS[2])
            dve.wait_ge(s_norms, GROUPS)

            def node2(at):
                st = NS[2]
                for u, g, i in at(3):
                    dve.wait_ge(*done(st["mm"], g))
                    dve.wait_ge(*landed_before(st["store"][0][u], i))
                    V.scalar_tensor_tensor(out=slot(buf[7], u), in0=ps[4 + u][:, :].rearrange("p (t d) -> p t d", d=D),
                                           scalar=0.0, in1=over_features(cols(norm_out, g, T)),
                                           op0=ALU.max, op1=ALU.mult).then_inc(st["o"].sem, 1)
                scaled2(at)
            over_groups(dve, 3, node2)
            sums_cleared(NS[2])
            plain_segment(2, False)
            scaled3 = scaled_sums(NS[3])
            centre3 = ln_centre(NS[3], 3, buf[6], buf[7], lambda u, g, i: dve.wait_ge(*done(NS[3]["x"], g)))
            var3 = ln_var(NS[3], 4, buf[3])
            out3 = ln_out(NS[3], 5, buf[7], lambda u: slot(buf[4], u),
                          lambda u, g, i: dve.wait_ge(*landed_before(NS[3]["store"][1][u], i)))

            def node3(at):
                st = NS[3]
                out3(at)
                for u, g, i in at(3):
                    dve.wait_ge(*done(st["mm"], g))
                    dve.wait_ge(*landed(st["load"][0][u], i))
                    dve.wait_ge(*landed_before(st["store"][0][u], i))
                    V.scalar_tensor_tensor(out=buf[6][:, u, :], in0=ps[4 + u][:, :], scalar=0.0, in1=buf[0][:, u, :],
                                           op0=ALU.max, op1=ALU.add).then_inc(st["x"].sem, 1)
                var3(at)
                centre3(at)
                scaled3(at)
            over_groups(dve, 5, node3)
            sums_cleared(NS[3])
            plain_segment(3, True)

            def cat(st):
                def part(at):
                    for u, g, i in at(0):
                        dve.wait_ge(*reuse(st["ct"], g))
                        V.tensor_copy(wide[:, u, :].rearrange("p (t c) -> p t c", c=P)[:, :, 0:D],
                                      agg[:, bass.ds(g * T, T), 0:D]).then_inc(st["cat"].sem, 1)
                return part

            cat4 = cat(NS[4])

            def node4(at):
                st = NS[4]
                for u, g, i in at(3):
                    dve.wait_ge(*done(st["mm"], g))
                    dve.wait_ge(*landed_before(st["store"][0][u], i))
                    V.tensor_scalar(buf[7][:, u, :], ps[4 + u][:, :], 0.0, None, ALU.max).then_inc(st["o"].sem, 1)
                cat4(at)
            over_groups(dve, 3, node4)
            sums_cleared(NS[4])
            plain_segment(4, True)
            cat5 = cat(NS[5])
            centre5 = ln_centre(NS[5], 3, buf[6], buf[7], lambda u, g, i: dve.wait_ge(*done(NS[5]["x"], g)))
            var5 = ln_var(NS[5], 4, buf[3])
            out5 = ln_out(NS[5], 5, buf[7], lambda u: slot(buf[4], u), lambda u, g, i: dve.wait_ge(*reuse(NS[5]["ht"], g)))

            def node5(at):
                st = NS[5]
                out5(at)
                for u, g, i in at(3):
                    dve.wait_ge(*done(st["mm"], g))
                    dve.wait_ge(*landed(st["load"][1][u], i))
                    dve.wait_ge(*landed_before(st["store"][1][u], i))
                    V.tensor_tensor(buf[6][:, u, :], ps[4 + u][:, :], buf[0][:, u, :], ALU.add
                                    ).then_inc(st["x"].sem, 1)
                var5(at)
                centre5(at)
                for u, g, i in at(9):
                    dve.wait_ge(*done(st["wh"], g))
                    dve.wait_ge(*reuse(st["nrm2"], g))
                    V.tensor_reduce(small[:, u, 5, :], slot(buf[5], u), AX_X, ALU.add).then_inc(st["nrm"].sem, 1)
                cat5(at)
            over_groups(dve, 9, node5)

            e = E[5]
            dst_all = dst_f[:, :, :].rearrange("p b q -> p (b q)")
            link(V.tensor_tensor(lane[:, :], dst_all, lane[:, :], ALU.subtract))
            link(V.scalar_tensor_tensor(out=window_tile[:, :], in0=window_tile[:, :], scalar=float(-P), in1=lane[:, :],
                                        op0=ALU.mult, op1=ALU.add))
            link(V.tensor_scalar(window_tile[:, :], window_tile[:, :], lane_dump[:, 0:1], float(-NP), ALU.add, ALU.add))

            def targets(b, u, i):
                dve.wait_ge(*landed(e["row_dst_got"][u], i))
                if not (isinstance(b, int) and b == 0):
                    dve.wait_ge(*done(e["dst_hot"], b * T - 1))
                for w in range(WINDOW):
                    m = V.tensor_scalar(in_tile[:, w, :], cols(window_tile, b, T), float(w * P), None, ALU.add)
                m.then_inc(e["target"].sem, 1)
                dve.wait_ge(*done(e["target"], b))

            def dst_one_hot(b, u, t):
                dve.wait_ge(*reuse(e["dst_mm"], b * T + t, 4))
                full = [P, WINDOW, P]
                V.tensor_tensor(dst_hot[t % 4].rearrange("p (w q) -> p w q", q=P),
                                wide_t[:, u, t * P:(t + 1) * P].bitcast(I32).unsqueeze(1).to_broadcast(full),
                                in_tile[:, :, t:t + 1].to_broadcast(full), ALU.is_equal).then_inc(e["dst_hot"].sem, 1)

            targets(0, 0, 0)
            for t in range(T):
                dst_one_hot(0, 0, t)

            def edge5(b, i, u, n):
                s = small[:, u, :, 0:n]
                step = [0]

                def mine(ins):
                    step[0] += 1
                    ins.then_inc(s_e5[u], 1)

                def ready():
                    dve.wait_ge(s_e5[u], i * E5_STEPS + step[0])

                def next_hot(t):
                    if n == T:
                        dst_one_hot(b + 1, 1 - u, t)

                wr, wc = rows_u[:, u, 0:n, :], rows_v[:, u, 0:n, :]
                c = lambda x: x[:, u, 0:n * D].rearrange("p (t d) -> p t d", d=D)
                if n == T:
                    targets(b + 1, 1 - u, i + u)
                next_hot(0)
                dve.wait_ge(e["src_got"][u].sem, e["src_got"][u].base + gathered(i) + 16 * n)
                dve.wait_ge(*done(e["dst_rows"], b))
                dve.wait_ge(*done(e["dst_gathered"], b))
                mine(V.tensor_tensor(c(buf[2]), wr[:, :, 0:D], wc[:, :, 0:D], ALU.mult))
                mine(V.tensor_tensor(s[:, 1, :].unsqueeze(2), wr[:, :, D:AW], wc[:, :, D:AW], ALU.mult))
                next_hot(1)
                ready()
                mine(V.tensor_reduce(s[:, 0, :], c(buf[2]), AX_X, ALU.add))
                mine(V.tensor_scalar(s[:, 1, :], s[:, 1, :], SIM_EPS, None, ALU.max))
                next_hot(2)
                ready()
                mine(V.reciprocal(s[:, 2, :], s[:, 1, :]))
                next_hot(3)
                ready()
                mine(V.tensor_tensor(s[:, 3, :], s[:, 0, :], s[:, 2, :], ALU.mult))
                ready()
                mine(V.tensor_scalar(s[:, 4, :], s[:, 3, :], 0.0, par_w[:, 8:9], ALU.max, ALU.mult))
                mine(V.tensor_scalar(s[:, 5, :], s[:, 3, :], 0.0, par_w[:, 9:10], ALU.min, ALU.mult))
                next_hot(4)
                ready()
                mine(V.tensor_tensor(s[:, 4, :], s[:, 4, :], s[:, 5, :], ALU.add))
                ready()
                mine(V.tensor_tensor(s[:, 6, :], s[:, 4, :], cols(base, b, n), ALU.mult))
                next_hot(5)
                ready()
                dve.wait_ge(*reuse(e["dedup"], b))
                V.tensor_tensor(c(buf[4]), wc[:, :, 0:D], s[:, 6, :].unsqueeze(2).to_broadcast([P, n, D]),
                                ALU.mult).then_inc(e["contrib"].sem, 1)
                next_hot(6)
                dve.wait_ge(*landed(e["row_got"][u], i))

                def is_same(t):
                    dve.wait_ge(*reuse(e["same_used"], b * T + t, 4))
                    V.tensor_scalar(same[:, t % 4, :], wide[:, u, t * P:(t + 1) * P].bitcast(I32),
                                    sf[:, bass.ds(b * T + t, 1)], None, ALU.is_equal).then_inc(e["same"].sem, 1)

                dve.wait_ge(*done(e["contrib"], b))
                is_same(0)
                next_hot(7)
                for t in range(n):
                    if t + 1 < n:
                        is_same(t + 1)
                    dve.wait_ge(*done(e["same"], b * T + t))
                    mine(V.tensor_tensor_reduce(earlier[t], same[:, t % 4, :], below[:, :], 1.0, 0.0,
                                                ALU.mult, ALU.add, s[:, 7, t:t + 1]))
                ready()
                dve.sem_inc(e["rows_used"].sem, 1)
                mine(V.tensor_scalar(s[:, 8, :], s[:, 7, :], 0.5, None, ALU.is_lt))
                mine(V.tensor_scalar(s[:, 9, :], cols(sf, b, n), 0.0, None, ALU.is_ge))
                mine(V.tensor_scalar(s[:, 0, :], cols(sf, b, n), lane_dump[:, 0:1], None, ALU.subtract))
                ready()
                mine(V.tensor_tensor(s[:, 8, :], s[:, 8, :], s[:, 9, :], ALU.mult))
                ready()
                mine(V.tensor_tensor(s[:, 8, :], s[:, 8, :], s[:, 0, :], ALU.mult))
                ready()
                dve.wait_ge(*done(e["sum"], b))
                V.tensor_scalar(idx_o[:, u, 0:n], s[:, 8, :], lane_dump[:, 0:1], None, ALU.add).then_inc(e["oidx"].sem, 1)
                assert n != T or step[0] == E5_STEPS, step

            over_blocks(edge5)

            def node6(at):
                st = NS[6]
                for u, g, i in at(1):
                    dve.wait_ge(*done(st["sum1"], g))
                    dve.wait_ge(*landed_before(st["store"][0][u], i))
                    V.tensor_tensor(buf[7][:, u, :], buf[4][:, u, :], buf[5][:, u, :], ALU.add
                                    ).then_inc(st["sum"].sem, 1)
                for u, g, i in at(0):
                    c = st["load"][0][u]
                    dve.wait_ge(c.sem, c.base + 16 * (TABLES * (i + 1) + 1))
                    V.tensor_tensor(buf[4][:, u, :], buf[0][:, u, :], buf[1][:, u, :], ALU.add)
                    V.tensor_tensor(buf[5][:, u, :], buf[2][:, u, :], buf[3][:, u, :], ALU.add
                                    ).then_inc(st["sum1"].sem, 1)
            over_groups(dve, 1, node6, FULL_GROUPS + 1)

_INS = ['x', 'src', 'dst', 'edge_attr_16', 'edge_weight', 'edge_weight_n2', 'L0_gnn_W1m', 'L0_gnn_b1m', 'L0_gnn_W2m',
        'L0_gnn_b2m', 'L0_gnn_W1u', 'L0_gnn_b1u', 'L0_gnn_W2u', 'L0_gnn_b2u', 'L1_gnn_W1', 'L1_gnn_b1', 'L1_gnn_W2',
        'L1_gnn_b2', 'L2_gnn_W_rel1', 'L2_gnn_b_rel1', 'L2_gnn_W_root1', 'L2_gnn_W_rel2', 'L2_gnn_b_rel2',
        'L2_gnn_W_root2', 'L3_gnn_W', 'L3_gnn_b', 'L3_gnn_deg_coeff', 'L3_gnn_coeff_param', 'L3_gnn_scale_param']


def kernel(**inputs):
    import numpy as _np
    import concourse.bacc as _bacc
    from concourse import mybir as _mybir
    from concourse.bass_utils import run_bass_kernel_spmd as _run

    nc = _bacc.Bacc("TRN2", target_bir_lowering=False, num_devices=1)
    arrays, args = {}, {}
    for name in _INS:
        v = _np.ascontiguousarray(inputs[name])
        arrays[f"in_{name}_dram"] = v
        args[name] = nc.dram_tensor(f"in_{name}_dram", v.shape, _mybir.dt.from_np(v.dtype), kind="ExternalInput").ap()
    result = nc.dram_tensor("out_0_dram", (N, D), _mybir.dt.float32, kind="ExternalOutput").ap()
    program(nc, args, result)
    r = _run(nc, [arrays], core_ids=[0])
    return r.results[0]["out_0_dram"]
```
